# Optimizing a Trainium2 kernel written in Bass

```python
import numpy as np
import jax
import jax.numpy as jnp

def _softmax(x, axis=-1):
    return jax.nn.softmax(x, axis=axis)

def _gelu(x):
    return jax.nn.gelu(x, approximate=True)

def _silu(x):
    return jax.nn.silu(x)

def _sigmoid(x):
    return jax.nn.sigmoid(x)

def _layernorm(x, axis=-1, eps=1e-05):
    m = jnp.mean(x, axis=axis, keepdims=True)
    v = jnp.var(x, axis=axis, keepdims=True)
    return (x - m) / jnp.sqrt(v + eps)

def _scatter_add(tgt, idx, src, axis=0):
    return tgt.at[idx].add(src)

def _segment_sum(src, seg, n):
    return jax.ops.segment_sum(src, seg, n)
kernel_name = 'mk_cond_seq_d4_seqx_r2_b2d2cf'

def setup_inputs(seed: int=0):
    np.random.seed(seed)
    _w = jnp.asarray

    def _rec_inputs():
        import jax
        import jax.numpy as jnp
        _rk = jax.random.key(seed)
        x = 0.4999 + 0.2886 * jax.random.normal(jax.random.fold_in(_rk, 1), (16, 512, 512), jnp.float32)
        _lenS = 512 - jax.random.randint(jax.random.fold_in(_rk, 7), (16,), 0, max(1, 512 // 4) + 1, jnp.int32)
        _lenS2 = 512 - jax.random.randint(jax.random.fold_in(_rk, 8), (16,), 0, max(1, 512 // 4) + 1, jnp.int32)
        condB_dt = jax.random.uniform(jax.random.fold_in(_rk, 11), (16,), jnp.float32, 0.0, 0.981965)
        itok_B_34_63 = jax.random.randint(jax.random.fold_in(_rk, 13), (16,), 34, 64, jnp.int32)
        fside_Bx16xSxS_0 = -1.47943e-05 + 1.00017 * jax.random.normal(jax.random.fold_in(_rk, 14), (16, 16, 512, 512), jnp.float32)
        itok_B_0_15 = jax.random.randint(jax.random.fold_in(_rk, 15), (16,), 0, 16, jnp.int32)
        condB_theta = jax.random.uniform(jax.random.fold_in(_rk, 16), (16,), jnp.float32, 0.0, 0.983423)
        condB_phi = jax.random.uniform(jax.random.fold_in(_rk, 17), (16,), jnp.float32, 0.0, 0.961312)
        _validS = jnp.arange(512)[None, :] < _lenS[:, None]
        _validS2 = jnp.arange(512)[None, :] < _lenS2[:, None]
        _causal = jnp.tril(jnp.ones((512, 512), dtype=bool))
        mask_Bx1xSxS_bk0 = jnp.logical_not(jnp.broadcast_to(_validS[:, None, None, :], (16, 1, 512, 512)))
        return (x, condB_dt, itok_B_34_63, fside_Bx16xSxS_0, itok_B_0_15, condB_theta, condB_phi, mask_Bx1xSxS_bk0)
    x, condB_dt, itok_B_34_63, fside_Bx16xSxS_0, itok_B_0_15, condB_theta, condB_phi, mask_Bx1xSxS_bk0 = _rec_inputs()

    def _L0_cond_setup():
        import jax, jax.numpy as jnp
        import numpy as np
        B, NX, NY = (16, 512, 512)

        def _grad(f, axis):
            fm = jnp.moveaxis(f, axis, -1)
            g = (jnp.roll(fm, -1, -1) - jnp.roll(fm, 1, -1)) * 0.5
            g0 = (-3.0 * fm[..., 0] + 4.0 * fm[..., 1] - fm[..., 2]) * 0.5
            gN = (3.0 * fm[..., -1] - 4.0 * fm[..., -2] + fm[..., -3]) * 0.5
            g = g.at[..., 0].set(g0).at[..., -1].set(gN)
            return jnp.moveaxis(g, -1, axis)

        def _grad2(f, axis):
            fm = jnp.moveaxis(f, axis, -1)
            g = jnp.roll(fm, -1, -1) - 2.0 * fm + jnp.roll(fm, 1, -1)
            g0 = 2.0 * fm[..., 0] - 5.0 * fm[..., 1] + 4.0 * fm[..., 2] - fm[..., 3]
            gN = 2.0 * fm[..., -1] - 5.0 * fm[..., -2] + 4.0 * fm[..., -3] - fm[..., -4]
            g = g.at[..., 0].set(g0).at[..., -1].set(gN)
            return jnp.moveaxis(g, -1, axis)
        key = jax.random.key(seed)
        k1, k2, k3, k4 = jax.random.split(key, 4)
        f = jax.random.uniform(k1, (B, NX, NY), dtype=jnp.float32)
        A_grid = jax.random.normal(k2, (2, NX, NY), dtype=jnp.float32)
        B_grid = jax.random.uniform(k3, (3, NX, NY), dtype=jnp.float32)
        dt = jax.random.uniform(k4, (B,), dtype=jnp.float32)
        return {'f': f, 'A_grid': A_grid, 'B_grid': B_grid, 'dt': dt}
    _L0_cond_all = _L0_cond_setup()
    _L0_cond_in = {k: v for k, v in _L0_cond_all.items() if k in ('A_grid', 'B_grid')}
    del _L0_cond_all

    def _L1_cond_setup():
        import jax, jax.numpy as jnp
        import numpy as np
        import math
        D_MODEL = 512
        N_HEAD = 16
        HEAD_DIM = D_MODEL // N_HEAD
        D_FF = 2048
        NUM_STEPS = 100.0
        RESCALE = 4000.0
        EPS = 1e-05

        def _sin_emb(t):
            half = D_MODEL // 2
            x = t.astype(jnp.float32) / NUM_STEPS * RESCALE
            freqs = jnp.exp(jnp.arange(half, dtype=jnp.float32) * (-math.log(10000.0) / (half - 1)))
            e = x[:, None] * freqs[None, :]
            return jnp.concatenate([jnp.sin(e), jnp.cos(e)], axis=-1)

        def _ln(x):
            m = jnp.mean(x, axis=-1, keepdims=True)
            v = jnp.var(x, axis=-1, keepdims=True)
            return (x - m) / jnp.sqrt(v + EPS)

        def _gelu2(x):
            return x * jax.nn.sigmoid(1.702 * x)
        key = jax.random.key(seed)
        ks = jax.random.split(key, 24)
        B, S, D, F = (4, 256, D_MODEL, D_FF)
        std = 0.02
        inp = {'src': jax.random.normal(ks[0], (B, S, D), dtype=jnp.float32), 'src_mask': jax.random.randint(ks[1], (B, 1, S, S), 0, 2).astype(bool), 'timestep': jax.random.randint(ks[2], (B,), 0, 100, dtype=jnp.int32), 'attention_bias': jax.random.normal(ks[3], (B, N_HEAD, S, S), dtype=jnp.float32), 'W_ada': jax.random.normal(ks[4], (D, 2 * D), dtype=jnp.float32) * std, 'b_ada': jnp.zeros((2 * D,), dtype=jnp.float32), 'Wq': jax.random.normal(ks[5], (D, D), dtype=jnp.float32) * std, 'bq': jnp.zeros((D,), dtype=jnp.float32), 'Wk': jax.random.normal(ks[6], (D, D), dtype=jnp.float32) * std, 'bk': jnp.zeros((D,), dtype=jnp.float32), 'Wv': jax.random.normal(ks[7], (D, D), dtype=jnp.float32) * std, 'bv': jnp.zeros((D,), dtype=jnp.float32), 'Wo': jax.random.normal(ks[8], (D, D), dtype=jnp.float32) * std, 'bo': jnp.zeros((D,), dtype=jnp.float32), 'W1': jax.random.normal(ks[9], (D, F), dtype=jnp.float32) * std, 'b1': jnp.zeros((F,), dtype=jnp.float32), 'W2': jax.random.normal(ks[10], (F, D), dtype=jnp.float32) * std, 'b2': jnp.zeros((D,), dtype=jnp.float32), 'g2': jnp.ones((D,), dtype=jnp.float32), 'beta2': jnp.zeros((D,), dtype=jnp.float32)}
        return inp
    _L1_cond_all = _L1_cond_setup()
    _L1_cond_in = {k: v for k, v in _L1_cond_all.items() if k in ('W_ada', 'b_ada', 'Wq', 'bq', 'Wk', 'bk', 'Wv', 'bv', 'Wo', 'bo', 'W1', 'b1', 'W2', 'b2', 'g2', 'beta2')}
    del _L1_cond_all

    def _L2_cond_setup():
        import jax, jax.numpy as jnp
        import numpy as np
        B, S, D = (32, 512, 512)
        A = 128
        E = 16
        LN_EPS = 1e-05
        key = jax.random.key(seed)
        ks = jax.random.split(key, 10)
        s = lambda fan_in: 1.0 / np.sqrt(fan_in)
        return {'hidden_states': jax.random.normal(ks[0], (B, S, D), dtype=jnp.float32), 'domain_id': jax.random.randint(ks[1], (B,), 0, E, dtype=jnp.int64), 'down_W': jax.random.uniform(ks[2], (A, D), jnp.float32, -s(D), s(D)), 'down_b': jax.random.uniform(ks[3], (A,), jnp.float32, -s(D), s(D)), 'up_W': jax.random.uniform(ks[4], (D, A), jnp.float32, -s(A), s(A)), 'up_b': jax.random.uniform(ks[5], (D,), jnp.float32, -s(A), s(A)), 'expert_W': jax.random.uniform(ks[6], (E, A, A), jnp.float32, -s(A), s(A)), 'expert_b': jax.random.uniform(ks[7], (E, A), jnp.float32, -s(A), s(A)), 'domain_emb': jax.random.normal(ks[8], (E, A), dtype=jnp.float32), 'ln_gamma': jnp.ones((D,), jnp.float32), 'ln_beta': jnp.zeros((D,), jnp.float32)}
    _L2_cond_all = _L2_cond_setup()
    _L2_cond_in = {k: v for k, v in _L2_cond_all.items() if k in ('down_W', 'down_b', 'up_W', 'up_b', 'expert_W', 'expert_b', 'domain_emb', 'ln_gamma', 'ln_beta')}
    del _L2_cond_all

    def _L3_cond_setup():
        import jax, jax.numpy as jnp
        import numpy as np
        key = jax.random.key(seed)
        k1, k2, k3 = jax.random.split(key, 3)
        B, N, D = (16, 2048, 512)
        embeddings = jax.random.normal(k1, (B, N, D), dtype=jnp.float32)
        theta = jax.random.uniform(k2, (B,), dtype=jnp.float32)
        phi = jax.random.uniform(k3, (B,), dtype=jnp.float32)
        return {'embeddings': embeddings, 'theta': theta, 'phi': phi}
    _L3_cond_all = _L3_cond_setup()
    _L3_cond_in = {k: v for k, v in _L3_cond_all.items() if k in ()}
    del _L3_cond_all
    return {'x': x, 'condB_dt': condB_dt, 'itok_B_34_63': itok_B_34_63, 'fside_Bx16xSxS_0': fside_Bx16xSxS_0, 'itok_B_0_15': itok_B_0_15, 'condB_theta': condB_theta, 'condB_phi': condB_phi, 'mask_Bx1xSxS_bk0': mask_Bx1xSxS_bk0, 'L0_cond_A_grid': _L0_cond_in['A_grid'], 'L0_cond_B_grid': _L0_cond_in['B_grid'], 'L1_cond_W_ada': _L1_cond_in['W_ada'], 'L1_cond_b_ada': _L1_cond_in['b_ada'], 'L1_cond_Wq': _L1_cond_in['Wq'], 'L1_cond_bq': _L1_cond_in['bq'], 'L1_cond_Wk': _L1_cond_in['Wk'], 'L1_cond_bk': _L1_cond_in['bk'], 'L1_cond_Wv': _L1_cond_in['Wv'], 'L1_cond_bv': _L1_cond_in['bv'], 'L1_cond_Wo': _L1_cond_in['Wo'], 'L1_cond_bo': _L1_cond_in['bo'], 'L1_cond_W1': _L1_cond_in['W1'], 'L1_cond_b1': _L1_cond_in['b1'], 'L1_cond_W2': _L1_cond_in['W2'], 'L1_cond_b2': _L1_cond_in['b2'], 'L1_cond_g2': _L1_cond_in['g2'], 'L1_cond_beta2': _L1_cond_in['beta2'], 'L2_cond_down_W': _L2_cond_in['down_W'], 'L2_cond_down_b': _L2_cond_in['down_b'], 'L2_cond_up_W': _L2_cond_in['up_W'], 'L2_cond_up_b': _L2_cond_in['up_b'], 'L2_cond_expert_W': _L2_cond_in['expert_W'], 'L2_cond_expert_b': _L2_cond_in['expert_b'], 'L2_cond_domain_emb': _L2_cond_in['domain_emb'], 'L2_cond_ln_gamma': _L2_cond_in['ln_gamma'], 'L2_cond_ln_beta': _L2_cond_in['ln_beta']}

def reference(x, condB_dt, itok_B_34_63, fside_Bx16xSxS_0, itok_B_0_15, condB_theta, condB_phi, mask_Bx1xSxS_bk0, L0_cond_A_grid, L0_cond_B_grid, L1_cond_W_ada, L1_cond_b_ada, L1_cond_Wq, L1_cond_bq, L1_cond_Wk, L1_cond_bk, L1_cond_Wv, L1_cond_bv, L1_cond_Wo, L1_cond_bo, L1_cond_W1, L1_cond_b1, L1_cond_W2, L1_cond_b2, L1_cond_g2, L1_cond_beta2, L2_cond_down_W, L2_cond_down_b, L2_cond_up_W, L2_cond_up_b, L2_cond_expert_W, L2_cond_expert_b, L2_cond_domain_emb, L2_cond_ln_gamma, L2_cond_ln_beta):
    import jax
    import jax.numpy as jnp

    def _L0_cond_ref(f, A_grid, B_grid, dt):
        import jax, jax.numpy as jnp
        import numpy as np
        B, NX, NY = (16, 512, 512)

        def _grad(f, axis):
            fm = jnp.moveaxis(f, axis, -1)
            g = (jnp.roll(fm, -1, -1) - jnp.roll(fm, 1, -1)) * 0.5
            g0 = (-3.0 * fm[..., 0] + 4.0 * fm[..., 1] - fm[..., 2]) * 0.5
            gN = (3.0 * fm[..., -1] - 4.0 * fm[..., -2] + fm[..., -3]) * 0.5
            g = g.at[..., 0].set(g0).at[..., -1].set(gN)
            return jnp.moveaxis(g, -1, axis)

        def _grad2(f, axis):
            fm = jnp.moveaxis(f, axis, -1)
            g = jnp.roll(fm, -1, -1) - 2.0 * fm + jnp.roll(fm, 1, -1)
            g0 = 2.0 * fm[..., 0] - 5.0 * fm[..., 1] + 4.0 * fm[..., 2] - fm[..., 3]
            gN = 2.0 * fm[..., -1] - 5.0 * fm[..., -2] + 4.0 * fm[..., -3] - fm[..., -4]
            g = g.at[..., 0].set(g0).at[..., -1].set(gN)
            return jnp.moveaxis(g, -1, axis)
        Af = A_grid[None] * f[:, None]
        Bf = B_grid[None] * f[:, None]
        gradv_Af = _grad(Af[:, 0], 1) + _grad(Af[:, 1], 2)
        gradvv_Bf = _grad2(Bf[:, 0], 1) + _grad2(Bf[:, 1], 2) + _grad(_grad(Bf[:, 2], 2), 1) + _grad(_grad(Bf[:, 2], 1), 2)
        df = -gradv_Af + gradvv_Bf * 0.5
        f_new = f + df * dt[:, None, None]
        return jnp.maximum(f_new, 0.0)

    def _L1_cond_ref(src, src_mask, timestep, attention_bias, W_ada, b_ada, Wq, bq, Wk, bk, Wv, bv, Wo, bo, W1, b1, W2, b2, g2, beta2):
        import jax, jax.numpy as jnp
        import numpy as np
        import math
        D_MODEL = 512
        N_HEAD = 16
        HEAD_DIM = D_MODEL // N_HEAD
        D_FF = 2048
        NUM_STEPS = 100.0
        RESCALE = 4000.0
        EPS = 1e-05

        def _sin_emb(t):
            half = D_MODEL // 2
            x = t.astype(jnp.float32) / NUM_STEPS * RESCALE
            freqs = jnp.exp(jnp.arange(half, dtype=jnp.float32) * (-math.log(10000.0) / (half - 1)))
            e = x[:, None] * freqs[None, :]
            return jnp.concatenate([jnp.sin(e), jnp.cos(e)], axis=-1)

        def _ln(x):
            m = jnp.mean(x, axis=-1, keepdims=True)
            v = jnp.var(x, axis=-1, keepdims=True)
            return (x - m) / jnp.sqrt(v + EPS)

        def _gelu2(x):
            return x * jax.nn.sigmoid(1.702 * x)
        B, S, D = src.shape
        emb = jax.nn.silu(_sin_emb(timestep)) @ W_ada + b_ada
        scale, shift = jnp.split(emb[:, None, :], 2, axis=-1)
        x = _ln(src) * (1.0 + scale) + shift
        q = (x @ Wq + bq).reshape(B, S, N_HEAD, HEAD_DIM).transpose(0, 2, 1, 3)
        k = (x @ Wk + bk).reshape(B, S, N_HEAD, HEAD_DIM).transpose(0, 2, 1, 3)
        v = (x @ Wv + bv).reshape(B, S, N_HEAD, HEAD_DIM).transpose(0, 2, 1, 3)
        scores = jnp.einsum('bhqd,bhkd->bhqk', q / math.sqrt(HEAD_DIM), k)
        scores = scores + attention_bias
        scores = jnp.where(src_mask, -jnp.inf, scores.astype(jnp.float32))
        probs = jax.nn.softmax(scores, axis=-1).astype(v.dtype)
        ctx = jnp.einsum('bhqk,bhkd->bhqd', probs, v)
        ctx = ctx.transpose(0, 2, 1, 3).reshape(B, S, D)
        x = x + (ctx @ Wo + bo)
        h = _ln(x) * g2 + beta2
        ff = _gelu2(h @ W1 + b1) @ W2 + b2
        return x + ff

    def _L2_cond_ref(hidden_states, domain_id, down_W, down_b, up_W, up_b, expert_W, expert_b, domain_emb, ln_gamma, ln_beta):
        import jax, jax.numpy as jnp
        import numpy as np
        B, S, D = (32, 512, 512)
        A = 128
        E = 16
        LN_EPS = 1e-05
        residual = hidden_states
        hidden = jnp.einsum('bsd,ad->bsa', hidden_states, down_W) + down_b
        hidden = jax.nn.gelu(hidden, approximate=False)
        valid = (domain_id >= 0) & (domain_id < E)
        idx = jnp.clip(domain_id, 0, E - 1)
        Wsel = expert_W[idx]
        bsel = expert_b[idx]
        expert_out = jnp.einsum('bsa,boa->bso', hidden, Wsel) + bsel[:, None, :]
        domain_output = jnp.where(valid[:, None, None], expert_out, hidden)
        hidden = domain_output + domain_emb[idx][:, None, :]
        hidden = jnp.einsum('bsa,da->bsd', hidden, up_W) + up_b
        x = hidden + residual
        mu = jnp.mean(x, axis=-1, keepdims=True)
        var = jnp.mean(jnp.square(x - mu), axis=-1, keepdims=True)
        return (x - mu) * jax.lax.rsqrt(var + LN_EPS) * ln_gamma + ln_beta

    def _L3_cond_ref(embeddings, theta, phi):
        import jax, jax.numpy as jnp
        import numpy as np
        B, N, D = embeddings.shape
        e = embeddings.reshape(B, N, D // 4, 4)
        ct = jnp.cos(theta)[:, None, None]
        st = jnp.sin(theta)[:, None, None]
        cp = jnp.cos(phi)[:, None, None]
        sp = jnp.sin(phi)[:, None, None]
        x0, x1, x2, x3 = (e[..., 0], e[..., 1], e[..., 2], e[..., 3])
        out = jnp.stack([x0 * ct + x1 * st, -x0 * st + x1 * ct, x2 * cp + x3 * sp, -x2 * sp + x3 * cp], axis=-1)
        return out.reshape(B, N, D)
    x = _L0_cond_ref(x, L0_cond_A_grid, L0_cond_B_grid, condB_dt)
    x = _L1_cond_ref(x, mask_Bx1xSxS_bk0, itok_B_34_63, fside_Bx16xSxS_0, L1_cond_W_ada, L1_cond_b_ada, L1_cond_Wq, L1_cond_bq, L1_cond_Wk, L1_cond_bk, L1_cond_Wv, L1_cond_bv, L1_cond_Wo, L1_cond_bo, L1_cond_W1, L1_cond_b1, L1_cond_W2, L1_cond_b2, L1_cond_g2, L1_cond_beta2)
    x = _L2_cond_ref(x, itok_B_0_15, L2_cond_down_W, L2_cond_down_b, L2_cond_up_W, L2_cond_up_b, L2_cond_expert_W, L2_cond_expert_b, L2_cond_domain_emb, L2_cond_ln_gamma, L2_cond_ln_beta)
    x = _L3_cond_ref(x, condB_theta, condB_phi)
    return x

_drawn_inputs = setup_inputs


def setup_inputs(seed=0):
    import zlib

    import numpy as np

    out = dict(_drawn_inputs(seed))
    spreads = {'L1_cond_b_ada': (0.0, 0.1),
     'L1_cond_bq': (0.0, 0.8),
     'L1_cond_bk': (0.0, 0.8),
     'L1_cond_bv': (0.0, 0.1),
     'L1_cond_bo': (0.0, 0.1),
     'L1_cond_b1': (0.0, 0.1),
     'L1_cond_b2': (0.0, 0.1),
     'L1_cond_g2': (1.0, 0.2),
     'L1_cond_beta2': (0.0, 0.378),
     'L2_cond_ln_gamma': (1.0, 0.2),
     'L2_cond_ln_beta': (0.0, 0.1)}
    factors = {'fside_Bx16xSxS_0': 5.065, 'L1_cond_Wq': 8.0, 'L1_cond_Wk': 8.0, 'L2_cond_down_b': 8.0}
    for name, (base, spread) in spreads.items():
        noise = np.random.default_rng([zlib.crc32(name.encode()), seed]).standard_normal(out[name].shape)
        drawn = base * np.exp(spread * noise) if base else spread * noise
        out[name] = jnp.asarray(drawn.astype(out[name].dtype))
    for name, factor in factors.items():
        out[name] = (out[name] * factor).astype(out[name].dtype)
    return out
```

```python
from contextlib import ExitStack

import numpy as np

import concourse.bass as bass
from concourse import mybir

F32 = mybir.dt.float32
F32R = mybir.dt.float32r
BF16 = mybir.dt.bfloat16
U8 = mybir.dt.uint8
I32 = mybir.dt.int32
ALU = mybir.AluOpType
ACT = mybir.ActivationFunctionType

P = 128
B, S, D = 16, 512, 512
NH, DH = 16, 32
FF = 2048
A, E = 128, 16
TB = S // P
KB = D // P
G = NH * DH // P
HG = P // DH
NF = FF // P
EPS = 1e-5
QSCALE = float(DH) ** -0.5
MASKED = -3.0e38
MIN_START = 1.0e30
MAGIC = 12582912.0
PI = float(np.pi)
TWO_PI = (6.28125, 0.0019340515136718750, 1.2556659146713e-06)

FILLS = 19
FILL_V, FILL_QK, FILL_O, FILL_F, FILL_L2, FILL_UP = 0, 2, 6, 8, 16, 17
W0, W1_ = 14, 10
W0_V, W0_QK, W0_O, W0_F = 0, 1, 5, 6
W1_V, W1_O, W1_F = 0, 1, 2
TURNS = 12


class Link:

    def __init__(self, eng, sem, base=0):
        self.eng, self.sem, self.base, self.n = eng, sem, base, 0

    def mark(self, ins):
        ins.then_inc(self.sem, 1)
        self.n += 1

    def sync(self):
        self.eng.wait_ge(self.sem, self.base + self.n)

    def __call__(self, ins):
        self.mark(ins)
        self.sync()


def pair(ap, c):
    n = ap.shape[2]
    return ap[:, :, c:n - c:n - 1 - 2 * c]


def end_slope(link, v, tmp, w):
    link(v.tensor_scalar(tmp, pair(w, 0), -3.0, None, ALU.mult))
    link(v.scalar_tensor_tensor(tmp, pair(w, 1), 4.0, tmp, ALU.mult, ALU.add))
    link(v.tensor_tensor(tmp, tmp, pair(w, 2), ALU.subtract))


def slope_y(link, v, out, w, tmp):
    v.tensor_tensor(out[:, :, 1:D - 1], w[:, :, 2:D], w[:, :, 0:D - 2], ALU.subtract)
    end_slope(link, v, tmp, w)
    v.tensor_copy(out[:, :, 0:1], tmp[:, :, 0:1])
    link(v.tensor_scalar(out[:, :, D - 1:D], tmp[:, :, 1:2], -1.0, None, ALU.mult))


def sub_slope_y(link, v, s, w, tmp):
    link(v.tensor_tensor(s[:, :, 1:D - 1], s[:, :, 1:D - 1], w[:, :, 2:D], ALU.subtract))
    link(v.tensor_tensor(s[:, :, 1:D - 1], s[:, :, 1:D - 1], w[:, :, 0:D - 2], ALU.add))
    end_slope(link, v, tmp, w)
    link(v.tensor_tensor(s[:, :, 0:1], s[:, :, 0:1], tmp[:, :, 0:1], ALU.subtract))
    link(v.tensor_tensor(s[:, :, D - 1:D], s[:, :, D - 1:D], tmp[:, :, 1:2], ALU.add))


def add_curve_y(link, v, s, w):
    inner = s[:, :, 1:D - 1]
    link(v.tensor_tensor(inner, inner, w[:, :, 2:D], ALU.add))
    link(v.tensor_tensor(inner, inner, w[:, :, 0:D - 2], ALU.add))
    link(v.scalar_tensor_tensor(inner, w[:, :, 1:D - 1], -2.0, inner, ALU.mult, ALU.add))
    for c, k in enumerate((2.0, -5.0, 4.0, -1.0)):
        link(v.scalar_tensor_tensor(pair(s, 0), pair(w, c), k, pair(s, 0), ALU.mult, ALU.add))


def field_step(nc, x, A_grid, B_grid, dt, x1):
    R = S // P
    with ExitStack() as ctx:
        sb = lambda name, shape, t=F32: ctx.enter_context(nc.sbuf_tensor(name, shape, t))
        sem = lambda name: ctx.enter_context(nc.semaphore(name))
        grid_a0, grid_b0, grid_b2 = (sb(n, [P, R + 2, D]) for n in ("grid_a0", "grid_b0", "grid_b2"))
        grid_a1, grid_b1 = (sb(n, [P, R, D]) for n in ("grid_a1", "grid_b1"))
        field = [sb(f"field{u}", [P, R + 2, D]) for u in range(2)]
        a0f = [sb(f"a0f{u}", [P, R + 2, D]) for u in range(2)]
        b0f = [sb(f"b0f{u}", [P, R + 2, D]) for u in range(2)]
        b1f = [sb(f"b1f{u}", [P, R, D]) for u in range(2)]
        total = [sb(f"total{u}", [P, R, D]) for u in range(2)]
        b2f = sb("b2f", [P, R + 2, D])
        flow = sb("flow", [P, R + 2, D])
        a1f = sb("a1f", [P, R, D])
        half_dt = sb("half_dt", [P, B])
        tmp = sb("tmp", [P, R + 2, 2])
        grids_in, zeroed, dt_in = sem("grids_in"), sem("zeroed"), sem("dt_in")
        field_in = [sem(f"field_in{u}") for u in range(2)]
        products = sem("products")
        dve_step = sem("dve_step")
        stepped = [sem(f"stepped{u}") for u in range(2)]
        clipped = [sem(f"clipped{u}") for u in range(2)]
        stored = [sem(f"stored{u}") for u in range(2)]
        STEPS = 24

        def halo_loads(eng, tile, src, s):
            eng.dma_start(tile[:, 1:R + 1, :], src.rearrange("(p r) c -> p r c", r=R)).then_inc(s, 16)
            eng.dma_start(tile[64:128, 0, :], src[255:508:4, :]).then_inc(s, 16)
            eng.dma_start(tile[1:64, 0, :], src[3:252:4, :]).then_inc(s, 16)
            eng.dma_start(tile[0:64, R + 1, :], src[4:257:4, :]).then_inc(s, 16)
            eng.dma_start(tile[64:127, R + 1, :], src[260:509:4, :]).then_inc(s, 16)

        with nc.Block() as block:

            @block.sync
            def _(sp):
                sp.dma_start(half_dt[:], dt.partition_broadcast(P)).then_inc(dt_in, 16)
                sp.wait_ge(zeroed, 1)
                for tile, src in ((grid_b2, B_grid[2]), (grid_a0, A_grid[0]), (grid_b0, B_grid[0])):
                    halo_loads(sp, tile, src, grids_in)
                for tile, src in ((grid_b1, B_grid[1]), (grid_a1, A_grid[1])):
                    sp.dma_start(tile[:], src.rearrange("(p r) c -> p r c", r=R)).then_inc(grids_in, 16)
                with sp.Fori(0, B // 2) as i:
                    for u in range(2):
                        sp.wait_ge(stepped[u], i)
                        halo_loads(sp, field[u], x[bass.ds(2 * i + u, 1)].rearrange("o s c -> (o s) c"), field_in[u])

            @block.gpsimd
            def _(pool):
                pool.wait_ge(grids_in, 16 * 17)
                with pool.Fori(0, B // 2) as i:
                    for u in range(2):
                        n = 2 * i + u
                        pool.wait_ge(stepped[u], i)
                        pool.wait_ge(stored[u], 16 * i)
                        pool.wait_ge(field_in[u], 80 * (i + 1))
                        pool.tensor_tensor(a0f[u][:], grid_a0[:], field[u][:], ALU.mult).then_inc(products, 1)
                        pool.tensor_tensor(b0f[u][:], grid_b0[:], field[u][:], ALU.mult).then_inc(products, 1)
                        pool.wait_ge(products, 4 * n + 2)
                        pool.tensor_tensor(total[u][:], b0f[u][:, 0:R, :], b0f[u][:, 2:R + 2, :], ALU.add).then_inc(products, 1)
                        pool.tensor_tensor(b1f[u][:], grid_b1[:], field[u][:, 1:R + 1, :], ALU.mult).then_inc(products, 1)

            @block.vector
            def _(v):
                zero = Link(v, dve_step)
                for t in (grid_a0, grid_b0, grid_b2, field[0], field[1]):
                    zero.mark(v.memset(t[:], 0.0))
                zero.sync()
                v.wait_ge(dt_in, 16)
                zero.mark(v.tensor_scalar(half_dt[:], half_dt[:], 0.5, None, ALU.mult))
                zero.sync()
                v.sem_inc(zeroed, 1)
                v.wait_ge(grids_in, 16 * 17)
                with v.Fori(0, B // 2) as i:
                    for u in range(2):
                        n = 2 * i + u
                        link = Link(v, dve_step, STEPS * n + 6)
                        f, s = field[u][:], total[u][:]
                        v.wait_ge(field_in[u], 80 * (i + 1))
                        link(v.tensor_tensor(b2f[:], grid_b2[:], f, ALU.mult))
                        slope_y(link, v, flow[:], b2f[:], tmp[:])
                        v.wait_ge(products, 4 * n + 1)
                        link(v.scalar_tensor_tensor(flow[:], flow[:], 0.5, a0f[u][:], ALU.mult, ALU.subtract))
                        v.wait_ge(products, 4 * n + 3)
                        link(v.scalar_tensor_tensor(s, b0f[u][:, 1:R + 1, :], -2.0, s, ALU.mult, ALU.add))
                        link(v.tensor_tensor(s, s, flow[:, 2:R + 2, :], ALU.add))
                        link(v.tensor_tensor(s, s, flow[:, 0:R, :], ALU.subtract))
                        v.wait_ge(products, 4 * n + 4)
                        add_curve_y(link, v, s, b1f[u][:])
                        link(v.tensor_tensor(a1f[:], grid_a1[:], f[:, 1:R + 1, :], ALU.mult))
                        sub_slope_y(link, v, s, a1f[:], tmp[:, 0:R, :])
                        v.scalar_tensor_tensor(s, s, half_dt[:, bass.ds(n, 1)], f[:, 1:R + 1, :], ALU.mult, ALU.add).then_inc(stepped[u], 1)
                        assert link.n == STEPS

            @block.scalar
            def _(act):
                with act.Fori(0, B // 2) as i:
                    for u in range(2):
                        act.wait_ge(stepped[u], i + 1)
                        act.activation(total[u][:], total[u][:], ACT.Relu).then_inc(clipped[u], 1)
                        act.wait_ge(clipped[u], i + 1)
                        act.dma_start(x1[bass.ds(2 * i + u, 1)].rearrange("o (p r) c -> p (o r) c", r=R),
                                      total[u][:]).then_inc(stored[u], 16)
                act.wait_ge(stored[0], 16 * (B // 2))
                act.wait_ge(stored[1], 16 * (B // 2))


def field_edges(nc, x, A_grid, B_grid, dt, x1):
    NE = 4
    with ExitStack() as ctx:
        sb = lambda name, shape, t=F32: ctx.enter_context(nc.sbuf_tensor(name, shape, t))
        sem = lambda name: ctx.enter_context(nc.semaphore(name))
        Q = 2 * B
        f, ga0, gb0, gb2 = (sb(n, [Q, NE, D]) for n in ("edge_f", "edge_a0", "edge_b0", "edge_b2"))
        ga1, gb1 = (sb(n, [Q, 1, D]) for n in ("edge_a1", "edge_b1"))
        flow, s = sb("edge_flow", [Q, NE, D]), sb("edge_s", [Q, 1, D])
        tmp, scal = sb("edge_tmp", [Q, NE, 2]), sb("edge_scal", [Q, 4])
        loads, steps, stores = sem("edge_loads"), sem("edge_steps"), sem("edge_stores")
        with nc.Block() as block:

            @block.sync
            def _(sp):
                count = 0
                for side in range(2):
                    rows = [r if side == 0 else S - 1 - r for r in range(NE)]
                    half = slice(side * B, side * B + B)
                    for r, row in enumerate(rows):
                        sp.dma_start(f[half, r, :], x[:, row, :]).then_inc(loads, 16)
                        for tile, src in ((ga0, A_grid[0]), (gb0, B_grid[0]), (gb2, B_grid[2])):
                            sp.dma_start(tile[half, r, :], src[row, :].partition_broadcast(B)).then_inc(loads, 16)
                        count += 4
                    for tile, src in ((ga1, A_grid[1]), (gb1, B_grid[1])):
                        sp.dma_start(tile[half, 0, :], src[rows[0], :].partition_broadcast(B)).then_inc(loads, 16)
                    sp.dma_start(scal[half, 0:1], dt.rearrange("(b o) -> b o", o=1)).then_inc(loads, 16)
                    count += 3
                sp.wait_ge(steps, 1000)
                for side, row in ((0, 0), (1, S - 1)):
                    sp.dma_start(x1[0:B, row, :], s[side * B:side * B + B, 0, :]).then_inc(stores, 16)
                sp.wait_ge(stores, 32)

            @block.vector
            def _(v):
                link = Link(v, steps)
                link(v.memset(scal[:, 1:2], -1.0))
                link(v.memset(scal[0:B, 1:2], 1.0))
                v.wait_ge(loads, 16 * 2 * (4 * NE + 3))
                link(v.tensor_scalar(scal[:, 0:1], scal[:, 0:1], 0.5, None, ALU.mult))
                link(v.tensor_tensor(gb2[:], gb2[:], f[:], ALU.mult))
                slope_y(link, v, flow[:], gb2[:], tmp[:])
                link(v.tensor_tensor(ga0[:], ga0[:], f[:], ALU.mult))
                link(v.scalar_tensor_tensor(flow[:], flow[:], 0.5, ga0[:], ALU.mult, ALU.subtract))
                link(v.tensor_scalar(s[:], flow[:, 0:1, :], -3.0, None, ALU.mult))
                link(v.scalar_tensor_tensor(s[:], flow[:, 1:2, :], 4.0, s[:], ALU.mult, ALU.add))
                link(v.tensor_tensor(s[:], s[:], flow[:, 2:3, :], ALU.subtract))
                link(v.tensor_scalar(s[:], s[:], scal[:, 1:2], None, ALU.mult))
                link(v.tensor_tensor(gb0[:], gb0[:], f[:], ALU.mult))
                for r, k in enumerate((2.0, -5.0, 4.0, -1.0)):
                    link(v.scalar_tensor_tensor(s[:], gb0[:, r:r + 1, :], k, s[:], ALU.mult, ALU.add))
                link(v.tensor_tensor(gb1[:], gb1[:], f[:, 0:1, :], ALU.mult))
                add_curve_y(link, v, s[:], gb1[:])
                link(v.tensor_tensor(ga1[:], ga1[:], f[:, 0:1, :], ALU.mult))
                sub_slope_y(link, v, s[:], ga1[:], tmp[:, 0:1, :])
                link(v.scalar_tensor_tensor(s[:], s[:], scal[:, 0:1], f[:, 0:1, :], ALU.mult, ALU.add))
                v.tensor_scalar(s[:], s[:], 0.0, None, ALU.max).then_inc(steps, 1000 - link.n)


def reduce_angle(link, v, r, k):
    link(v.tensor_scalar(k, r, 1.0 / (2.0 * PI), None, ALU.mult))
    link(v.tensor_scalar(k, k, MAGIC, None, ALU.add))
    link(v.tensor_scalar(k, k, -MAGIC, None, ALU.add))
    for c in TWO_PI:
        link(v.scalar_tensor_tensor(r, k, -c, r, ALU.mult, ALU.add))


def quarter_turn(link, v, out, r, k):
    link(v.tensor_scalar(k, r, PI / 2, -2.0 * PI, ALU.is_gt, ALU.mult))
    link(v.tensor_tensor(out, r, k, ALU.add))
    link(v.tensor_scalar(out, out, PI / 2, None, ALU.add))
    for t in (out, r):
        link(v.tensor_scalar(t, t, 3.1415925, -3.1415925, ALU.min, ALU.max))


def prepare(nc, keep, step_id, domain, theta, phi, W_ada, b_ada, down_W, up_W, expert_W, expert_b, emb,
            freqs, lane, ada_rows, sel_rows, sel_turned):
    ident = keep["ident"]
    with ExitStack() as ctx:
        sb = lambda name, shape, t=F32: ctx.enter_context(nc.sbuf_tensor(name, shape, t))
        sem = lambda name: ctx.enter_context(nc.semaphore(name))
        bank = [ctx.enter_context(nc.psum_tensor(f"prep_bank{i}", [P, 512], F32)) for i in range(4)]
        tt = sb("time", [B, 4])
        ti = sb("time_i", [B, 1], I32)
        fr = sb("freqs_sb", [B, D // 2])
        ang, kk, emb_rows = sb("ang", [B, D]), sb("kk", [B, D]), sb("emb_rows", [B, D])
        embT = sb("embT", [P, KB, B])
        w_ada = sb("w_ada", [P, KB, 2 * D])
        bada = sb("bada", [B, 2 * D])
        ada = sb("ada", [B, 2 * D])
        idi, idf = sb("idi", [P, B], I32), sb("idf", [P, B])
        hot, ge, lt = sb("hot", [P, B]), sb("ge", [P, B]), sb("lt", [P, B])
        ln = sb("lane_sb", [P, 1])
        ew = sb("ew", [E, 4096])
        ewo = sb("ewo", [B, 4096])
        vecs = sb("vecs", [E, 2, A])
        bs = sb("bs", [A, 2, B])
        turn = sb("turn", [P, 2, B])
        turn2, tk = sb("turn2", [P, 2, B]), sb("tk", [P, 2, B])
        dw = sb("dw", [A, D])
        uw = sb("uw", [P, KB, A])
        selb = sb("selb", [P, B, A])
        selt = sb("selt", [P, B, A])
        loads, ew_in, steps, pe, at, st, sel_in = (sem(f"prep_{n}") for n in ("loads", "ew_in", "steps", "pe", "at", "st", "sel_in"))
        scal = keep["scal"]

        with nc.Block() as block:

            @block.sync
            def _(sp):
                for dst, src in (
                    (ti[:], step_id.rearrange("(b o) -> b o", o=1)),
                    (fr[:], freqs.partition_broadcast(B)),
                    (w_ada[:], W_ada.rearrange("(k p) n -> p k n", p=P)),
                    (bada[:], b_ada.partition_broadcast(B)),
                    (idi[:], domain.partition_broadcast(P)),
                    (ln[:], lane),
                    (vecs[:, 0, :], expert_b), (vecs[:, 1, :], emb),
                    (turn[:, 0, :], theta.partition_broadcast(P)), (turn[:, 1, :], phi.partition_broadcast(P)),
                    (dw[:], down_W), (uw[:], up_W.rearrange("(k p) a -> p k a", p=P)),
                ):
                    sp.dma_start(dst, src).then_inc(loads, 16)
                ew_flat = expert_W.rearrange("e o a -> e (o a)")
                for r in range(4):
                    if r:
                        sp.wait_ge(pe, 100 + 8 * r)
                    sp.dma_start(ew[:], ew_flat[:, r * 4096:(r + 1) * 4096]).then_inc(ew_in, 16)
                    sp.wait_ge(at, 8 * (r + 1))
                    sp.dma_start(sel_rows[:, r * 4096:(r + 1) * 4096], ewo[:]).then_inc(st, 16)
                    sp.wait_ge(st, 16 * (r + 1))
                sp.dma_start(selb[:], sel_rows.rearrange("b (o a) -> o b a", a=A)).then_inc(sel_in, 16)
                sp.wait_ge(at, 32 + 4)
                sp.dma_start(sel_turned.rearrange("b a o -> a b o"), selt[:]).then_inc(st, 16)
                sp.wait_ge(steps, 1000)
                sp.dma_start(ada_rows, ada[:]).then_inc(st, 16)
                sp.wait_ge(st, 16 * 6)

            @block.vector
            def _(v):
                link = Link(v, steps)
                v.wait_ge(loads, 16 * 12)
                link(v.tensor_scalar(tt[:, 0:1], ti[:], 1.0, None, ALU.mult))
                link(v.tensor_scalar(tt[:, 1:2], tt[:, 0:1], 0.01, None, ALU.mult))
                link(v.tensor_scalar(tt[:, 1:2], tt[:, 1:2], 4000.0, None, ALU.mult))
                link(v.tensor_scalar(ang[:, 0:D // 2], fr[:], tt[:, 1:2], None, ALU.mult))
                reduce_angle(link, v, ang[:, 0:D // 2], kk[:, 0:D // 2])
                quarter_turn(link, v, ang[:, D // 2:D], ang[:, 0:D // 2], kk[:, 0:D // 2])
                reduce_angle(link, v, turn[:], tk[:])
                quarter_turn(link, v, turn2[:], turn[:], tk[:])
                link(v.tensor_scalar(idf[:], idi[:], 1.0, None, ALU.mult))
                link(v.tensor_scalar(ge[:], idf[:], 0.0, None, ALU.is_ge))
                link(v.tensor_scalar(lt[:], idf[:], float(E), None, ALU.is_lt))
                link(v.tensor_tensor(ge[:], ge[:], lt[:], ALU.mult))
                link(v.tensor_scalar(idf[:], idf[:], 0.0, float(E - 1), ALU.max, ALU.min))
                link(v.tensor_scalar(hot[:], idf[:], ln[:, 0:1], None, ALU.is_equal))
                v.sem_inc(pe, 100)
                link(v.tensor_copy(scal[:, :, 0], ge[:]))
                link(v.tensor_scalar(scal[:, :, 1], ge[:], -1.0, 1.0, ALU.mult, ALU.add))
                v.wait_ge(keep["prep_sin"], 1)
                link(v.scalar_tensor_tensor(emb_rows[:], kk[:], 1.0, ang[:], ALU.add, ALU.mult))
                v.sem_inc(keep["prep_emb"], 1)
                v.wait_ge(keep["prep_ada"], 1)
                link(v.tensor_copy(embT[:], bank[3][:, 0:KB * B].rearrange("p (k b) -> p k b", b=B)))
                v.sem_inc(keep["prep_emb"], 1)
                v.wait_ge(keep["prep_ada"], 3)
                for h in range(2):
                    link(v.scalar_tensor_tensor(ada[:, h * D:h * D + D], bank[2 + h][0:B, :], 0.5, bada[:, h * D:h * D + D], ALU.mult, ALU.add))
                link(v.tensor_scalar(ada[:, 0:D], ada[:, 0:D], 1.0, None, ALU.add))
                v.sem_inc(keep["prep_emb"], 1)
                v.wait_ge(keep["prep_ada"], 4)
                link(v.tensor_copy(bs[:], bank[2][:, 0:2 * B].rearrange("p (v b) -> p v b", v=2)))
                link(v.tensor_tensor(bs[:, 0, :], bs[:, 0, :], scal[:, :, 0], ALU.mult))
                link(v.tensor_tensor(scal[:, :, 2], bs[:, 0, :], bs[:, 1, :], ALU.add))
                v.sem_inc(keep["prep_emb"], 1)
                v.wait_ge(keep["prep_ada"], 5)
                link(v.tensor_copy(keep["down_hi"][:], bank[3][:].rearrange("p (k a) -> p k a", a=A)))
                link(v.tensor_tensor(keep["down_lo"][:], bank[3][:].rearrange("p (k a) -> p k a", a=A), keep["down_hi"][:], ALU.subtract))
                v.sem_inc(keep["prep_emb"], 1)
                v.wait_ge(keep["prep_ada"], 6)
                v.tensor_copy(keep["up_T"][:], bank[2][:]).then_inc(steps, 1000 - link.n)

            @block.scalar
            def _(act):
                act.wait_ge(steps, 3 + 1 + 6 + 5 + 6 + 5)
                act.activation(ang[:], ang[:], ACT.Sin)
                act.activation(scal[:, :, 4], turn[:, 0, :], ACT.Sin)
                act.activation(scal[:, :, 6], turn[:, 1, :], ACT.Sin)
                act.activation(scal[:, :, 3], turn2[:, 0, :], ACT.Sin)
                act.activation(scal[:, :, 5], turn2[:, 1, :], ACT.Sin).then_inc(keep["prep_turn"], 1)
                act.wait_ge(keep["prep_turn"], 1)
                act.activation(kk[:], ang[:], ACT.Tanh, scale=0.5).then_inc(keep["prep_sin"], 1)
                for r in range(4):
                    for c in range(8):
                        m = 8 * r + c
                        act.wait_ge(pe, 100 + m + 1)
                        if c == 0 and r:
                            act.wait_ge(st, 16 * r)
                        act.activation(ewo[:, c * 512:(c + 1) * 512], bank[m % 2][0:B, :], ACT.Copy).then_inc(at, 1)
                for q in range(4):
                    act.wait_ge(pe, 100 + 32 + q + 1)
                    act.activation(selt[:, 4 * q:4 * q + 4, :], bank[q % 2][:].rearrange("p (b a) -> p b a", a=A), ACT.Copy).then_inc(at, 1)

            @block.tensor
            def _(t):
                t.wait_ge(loads, 16 * 12)
                t.wait_ge(keep["ident_in"], 16)
                t.wait_ge(pe, 100)
                t.wait_ge(keep["prep_emb"], 1)
                for k in range(KB):
                    mm = t.transpose(bank[3][:, k * B:k * B + B], emb_rows[:, k * P:k * P + P], ident[0:B, 0:B])
                mm.then_inc(keep["prep_ada"], 1)
                t.wait_ge(keep["prep_emb"], 2)
                for h in range(2):
                    for k in range(KB):
                        mm = t.matmul(bank[2 + h][0:B, :], embT[:, k, :], w_ada[:, k, h * D:h * D + D], start=k == 0, stop=k == KB - 1)
                    mm.then_inc(keep["prep_ada"], 1)
                t.wait_ge(keep["prep_emb"], 3)
                for w in range(2):
                    mm = t.matmul(bank[2][:, w * B:w * B + B], vecs[:, w, :], hot[0:E, :], start=True, stop=True)
                mm.then_inc(keep["prep_ada"], 1)
                t.wait_ge(keep["prep_emb"], 4)
                for k in range(KB):
                    mm = t.transpose(bank[3][:, k * A:k * A + A], dw[:, k * P:k * P + P], ident[:])
                mm.then_inc(keep["prep_ada"], 1)
                t.wait_ge(keep["prep_emb"], 5)
                for k in range(KB):
                    mm = t.transpose(bank[2][:, k * P:k * P + P], uw[:, k, :], ident[:])
                mm.then_inc(keep["prep_ada"], 1)
                for r in range(4):
                    t.wait_ge(ew_in, 16 * (r + 1))
                    for c in range(8):
                        m = 8 * r + c
                        if m >= 2:
                            t.wait_ge(at, m - 1)
                        t.matmul(bank[m % 2][0:B, :], hot[0:E, :], ew[:, c * 512:(c + 1) * 512], start=True, stop=True).then_inc(pe, 1)
                t.wait_ge(sel_in, 16)
                for q in range(4):
                    t.wait_ge(at, 32 + q - 1)
                    for j in range(4):
                        mm = t.transpose(bank[q % 2][:, j * A:j * A + A], selb[:, 4 * q + j, :], ident[:])
                    mm.then_inc(pe, 1)


def layers(nc, keep, x1, mask, bias, ada_rows, sel_turned, Wq, bq, Wk, bk, Wv, bv, Wo, bo, W1, b1, W2, b2, g2, beta2,
           down_b, up_b, gamma, beta, out):
    ident, scal, down, up_T = keep["ident"], keep["scal"], (keep["down_hi"], keep["down_lo"]), keep["up_T"]
    with ExitStack() as ctx:
        sb = lambda name, shape, t=F32: ctx.enter_context(nc.sbuf_tensor(name, shape, t))
        sem = lambda name: ctx.enter_context(nc.semaphore(name))

        bank = [ctx.enter_context(nc.psum_tensor(f"bank{i}", [P, 512], F32)) for i in range(8)]
        proj, score, turned, context, turns = bank[0:2], bank[2:4], bank[4:6], bank[6], bank[6:8]
        ff_sum = bank[2:6]

        col = {n: sb(f"{n}_col", [P, w]) for n, w in (("bq", G), ("bk", G), ("bv", G), ("b1", NF), ("g2", KB), ("beta2", KB), ("down_b", 1))}
        row = {n: sb(f"{n}_row", [P, D]) for n in ("bo", "b2", "up_b", "gamma", "beta")}
        minus_half = sb("minus_half", [P, TB])
        scale_row, shift_row = sb("scale_row", [P, D]), sb("shift_row", [P, D])
        mask8, mask_add = sb("mask8", [P, TB, S], U8), sb("mask_add", [P, TB, S], BF16)
        sel_T = sb("sel_T", [A, A])
        cur = sb("cur", [P, 8])
        tok_in = sb("tok_in", [P, TB, D])
        tok = sb("tok", [P, TB, D])
        res = sb("res", [P, TB, D])
        xT = [sb(f"xT{h}", [P, KB, S], F32R) for h in range(2)]
        stats, agg, fence = sb("stats", [P, TB, 6]), sb("agg", [P, TB, 2]), sb("fence", [P, 8])
        var, rstd = sb("var", [P, TB]), sb("rstd", [P, TB])
        w_raw = [sb(f"w_raw{s}", [P, 1024]) for s in range(2)]
        w = [sb(f"w{s}", [P, 2, 1024], F32R) for s in range(2)]
        V = sb("V", [P, TB, D])
        Vg = sb("Vg", [P, HG, TB, DH])
        wide = sb("wide", [P, 2, 512])
        parts = sb("parts", [P, 4, 512], F32R)
        stack = sb("stack", [P, HG, 2, 512], F32R)
        prob = [sb(f"prob{j}", [P, TB, S]) for j in range(HG)]
        low, total, inv = (sb(n, [P, 16]) for n in ("low", "total", "inv"))
        probT = sb("probT", [P, TB, S])
        ctxT = sb("ctxT", [P, G, S])
        gel = sb("gel", [P, 2, 512])

        consts_in, half_set = sem("consts_in"), sem("half_set")
        x_in, ada_in, mask_in, sel_in = sem("x_in"), sem("ada_in"), sem("mask_in"), sem("sel_in")
        raw_in = [sem(f"raw_in{s}") for s in range(2)]
        bias_in = [[sem(f"bias_in{j}_{h}") for h in range(2)] for j in range(HG)]
        stack_in = [sem(f"stack_in{j}") for j in range(HG)]
        out_done = sem("out_done")
        dve_step = sem("dve_step")
        var_ready, rstd_ready = sem("var_ready"), sem("rstd_ready")
        x_used, tok_ready, mask_ready = sem("x_used"), sem("tok_ready"), sem("mask_ready")
        tok_biased = sem("tok_biased")
        w_hi, w_lo = [sem(f"w_hi{s}") for s in range(2)], [sem(f"w_lo{s}") for s in range(2)]
        turn_full, turn_hi, turn_lo, turn_wide = sem("turn_full"), sem("turn_hi"), sem("turn_lo"), sem("turn_wide")
        proj_full, proj_read = [sem(f"proj_full{s}") for s in range(2)], [sem(f"proj_read{s}") for s in range(2)]
        v_copied, vg_copied = sem("v_copied"), sem("vg_copied")
        qk_hi, qk_lo = sem("qk_hi"), sem("qk_lo")
        bias_masked, score_full, scored, exped, inverted, normed = (sem(n) for n in ("bias_masked", "score_full", "scored", "exped", "inverted", "normed"))
        probT_full, probT_copied, pv_done, ctx_copied = (sem(n) for n in ("probT_full", "probT_copied", "pv_done", "ctx_copied"))
        ctx_hi, ctx_lo = sem("ctx_hi"), sem("ctx_lo")
        z2_ready, res_biased, geled, g_hi, g_lo, ff2_done = (sem(n) for n in ("z2_ready", "res_biased", "geled", "g_hi", "g_lo", "ff2_done"))
        y_ready, y_biased, hid_wide, hid_ready, mixed, out_ready = (sem(n) for n in ("y_ready", "y_biased", "hid_wide", "hid_ready", "mixed", "out_ready"))

        rows_of = lambda t, b: t[bass.ds(b, 1)].rearrange("o (t p) c -> p (o t) c", p=P)
        bcast = lambda t: t[:].unsqueeze(1).to_broadcast([P, TB, D])
        weight = lambda s, h: w[s][:, h, :].rearrange("p (k n) -> p k n", k=8)

        with nc.Block() as block:

            @block.sync
            def _(sp):
                for n, src, wd in (("bq", bq, G), ("bk", bk, G), ("bv", bv, G), ("b1", b1, NF), ("g2", g2, KB), ("beta2", beta2, KB), ("down_b", down_b, 1)):
                    sp.dma_start(col[n][:], src.rearrange("(k p) -> p k", p=P), allow_slow_non_contiguous=True).then_inc(consts_in, 16)
                for n, src in (("bo", bo), ("b2", b2), ("up_b", up_b), ("gamma", gamma), ("beta", beta)):
                    sp.dma_start(row[n][:], src.partition_broadcast(P)).then_inc(consts_in, 16)

                def load_weight(s, count, first, second):
                    sp.wait_ge(w_hi[s], count)
                    sp.wait_ge(w_lo[s], count)
                    for dst, src in (first, second):
                        sp.dma_start(dst, src).then_inc(raw_in[s], 16)

                raw = lambda s, h: w_raw[s][:, 512 * h:512 * h + 512]
                blocks = lambda s, h: raw(s, h).rearrange("p (k n) -> p k n", k=4)

                def load_qk(b, g):
                    load_weight(0, W0 * b + W0_QK + g, *(
                        (blocks(0, h), t[:, bass.ds(P * g, P)].rearrange("(k p) n -> p k n", p=P)) for h, t in ((0, Wq), (1, Wk))))

                def load_rows(s, count, t, k):
                    load_weight(s, count, *((raw(s, h), t[P * (k + h):P * (k + h + 1), :]) for h in range(2)))

                def load_bias(b, g, j):
                    src = bias[bass.ds(b, 1), bass.ds(HG * g + j, 1)].rearrange("o h (t p) k -> p (o h t) k", p=P)
                    for h in range(2):
                        sp.dma_start(prob[j][:, 2 * h:2 * h + 2, :], src[:, 2 * h:2 * h + 2, :]).then_inc(bias_in[j][h], 16)

                def load_stack(b, g, j):
                    for quad, (q, step) in enumerate(((0, 2), (1, 1), (0, 3), (1, 2))):
                        sp.dma_start(stack[DH * quad:DH * (quad + 1), j, :, :].bitcast(F32),
                                     parts[DH * j:DH * (j + 1), q:q + step + 1:step, :].bitcast(F32)).then_inc(stack_in[j], 16)

                def group(b, g, first, last):
                    n = 4 * b + g
                    if not last:
                        sp.wait_ge(probT_full, 16 * n + 4)
                        load_bias(b, g + 1, 0)
                        sp.wait_ge(qk_hi, 2 * n + 4)
                        sp.wait_ge(qk_lo, 2 * n + 4)
                        for j in range(HG):
                            if j == 2:
                                sp.wait_ge(probT_full, 16 * n + 8)
                                load_bias(b, g + 1, 1)
                            sp.wait_ge(score_full, 16 * n + 4 * j + 4)
                            load_stack(b, g + 1, j)
                        sp.wait_ge(probT_full, 16 * n + 12)
                        load_bias(b, g + 1, 2)
                        if g is not None and not isinstance(g, int) or (isinstance(g, int) and g < G - 2):
                            pass
                        sp.wait_ge(probT_full, 16 * n + 16)
                        load_bias(b, g + 1, 3)

                with sp.Fori(0, B) as b:
                    sp.wait_ge(probT_full, 64 * b)
                    for j in range(2):
                        load_bias(b, 0, j)
                    sp.wait_ge(x_used, b)
                    sp.dma_start(tok_in[:], rows_of(x1, b)).then_inc(x_in, 16)
                    sp.wait_ge(tok_ready, b)
                    sp.dma_start(scale_row[:], ada_rows[bass.ds(b, 1), 0:D].rearrange("o c -> (o c)").partition_broadcast(P)).then_inc(ada_in, 16)
                    sp.dma_start(shift_row[:], ada_rows[bass.ds(b, 1), D:2 * D].rearrange("o c -> (o c)").partition_broadcast(P)).then_inc(ada_in, 16)
                    sp.wait_ge(mask_ready, b)
                    sp.dma_start(mask8[:], mask[bass.ds(b, 1), 0].rearrange("o (t p) k -> p (o t) k", p=P)).then_inc(mask_in, 16)
                    load_rows(0, W0 * b + W0_V, Wv, 0)
                    load_rows(1, W1_ * b + W1_V, Wv, 2)
                    for j in range(2, HG):
                        load_bias(b, 0, j)
                    load_qk(b, 0)
                    sp.wait_ge(mixed, b)
                    sp.dma_start(sel_T[:], sel_turned[bass.ds(b, 1)].rearrange("o a c -> a (o c)")).then_inc(sel_in, 16)
                    load_qk(b, 1)
                    sp.wait_ge(qk_hi, 8 * b + 2)
                    sp.wait_ge(qk_lo, 8 * b + 2)
                    for j in range(HG):
                        load_stack(b, 0, j)
                    group(b, 0, True, False)
                    load_qk(b, 2)
                    group(b, 1, False, False)
                    load_qk(b, 3)
                    group(b, 2, False, False)
                    load_rows(0, W0 * b + W0_O, Wo, 0)
                    load_rows(1, W1_ * b + W1_O, Wo, 2)
                    with sp.Fori(0, NF // 2) as i:
                        for s in range(2):
                            f = 2 * i + s
                            load_weight(s, (W0 * b + W0_F if s == 0 else W1_ * b + W1_F) + i,
                                        (blocks(s, 0), W1[:, bass.ds(P * f, P)].rearrange("(k p) n -> p k n", p=P)),
                                        (raw(s, 1), W2[bass.ds(P * f, P), :]))

            @block.gpsimd
            def _(pool):
                pool.memset(minus_half[:], -0.5).then_inc(half_set, 1)
                pool.wait_ge(half_set, 1)
                pool.wait_ge(consts_in, 16 * 12)

                def split_lo(s, count):
                    pool.wait_ge(w_hi[s], count + 1)
                    pool.tensor_tensor(w[s][:, 1, :], w_raw[s][:], w[s][:, 0, :].bitcast(F32), ALU.subtract).then_inc(w_lo[s], 1)

                def root(count):
                    pool.wait_ge(var_ready, count)
                    pool.tensor_tensor(rstd[:], var[:], minus_half[:], ALU.pow).then_inc(rstd_ready, 1)

                def add_mask(b, g, j):
                    for h in range(2):
                        pool.wait_ge(bias_in[j][h], 16 * (4 * b + g + 1))
                        half = prob[j][:, 2 * h:2 * h + 2, :]
                        pool.tensor_tensor(half, half, mask_add[:, 2 * h:2 * h + 2, :], ALU.add).then_inc(bias_masked, 1)

                def group(b, g, last):
                    if not last:
                        split_lo(0, W0 * b + W0_QK + g + 1)
                    for j in (2, 3):
                        add_mask(b, g, j)
                    if not last:
                        for j in (0, 1):
                            add_mask(b, g + 1, j)

                with pool.Fori(0, B) as b:
                    split_lo(0, W0 * b + W0_V)
                    root(3 * b + 1)
                    split_lo(1, W1_ * b + W1_V)
                    pool.wait_ge(mask_ready, b + 1)
                    add_mask(b, 0, 0)
                    split_lo(0, W0 * b + W0_QK)
                    add_mask(b, 0, 1)
                    pool.wait_ge(turn_full, TURNS * b + KB)
                    pool.tensor_tensor(tok[:], tok[:], bcast(row["bo"]), ALU.add).then_inc(tok_biased, 1)
                    for g in range(G):
                        group(b, g, g == G - 1)
                    split_lo(0, W0 * b + W0_O)
                    split_lo(1, W1_ * b + W1_O)
                    split_lo(0, W0 * b + W0_F)
                    root(3 * b + 2)
                    pool.wait_ge(z2_ready, b + 1)
                    pool.tensor_tensor(res[:], res[:], bcast(row["b2"]), ALU.add).then_inc(res_biased, 1)
                    split_lo(1, W1_ * b + W1_F)
                    with pool.Fori(1, NF // 2) as i:
                        split_lo(0, W0 * b + W0_F + i)
                        split_lo(1, W1_ * b + W1_F + i)
                    pool.wait_ge(y_ready, b + 1)
                    pool.tensor_tensor(res[:], tok[:], bcast(row["up_b"]), ALU.add).then_inc(y_biased, 1)
                    root(3 * b + 3)

            @block.scalar
            def _(act):
                def split_hi(s, count, used_sem, used):
                    act.wait_ge(used_sem, used)
                    act.wait_ge(raw_in[s], 32 * (count + 1))
                    act.activation(w[s][:, 0, :], w_raw[s][:], ACT.Copy).then_inc(w_hi[s], 1)

                def turn_hi_from(b, n, src, k):
                    act.activation(xT[0][:, k, :], src, ACT.Copy).then_inc(turn_hi, 1)

                def exp(b, m, mm):
                    act.wait_ge(scored, m + 1)
                    j, qb = (mm % 16) // 4, mm % 4
                    act.activation(prob[j][:, qb, :], prob[j][:, qb, :], ACT.Exp, bias=low[:, mm % 16:mm % 16 + 1], scale=-1.0,
                                   accum_out=total[:, mm % 16:mm % 16 + 1]).then_inc(exped, 1)

                def group(b, g, first, last):
                    n = 4 * b + g
                    for i in range(16):
                        m = 16 * n + i
                        if i == 0 and not last:
                            split_hi(0, W0 * b + W0_QK + g + 1, proj_full[1], FILLS * b + FILL_QK + g + 1)
                        act.wait_ge(probT_full, m + 1)
                        act.wait_ge(pv_done, 64 * b if first and i < 4 else m - 3)
                        act.activation(probT[:, i % 4, :], turned[i % 2][:], ACT.Copy).then_inc(probT_copied, 1)
                        if not (last and i + 5 >= 16):
                            exp(b, m + 5, i + 5)
                        if i in (6, 7) and not last:
                            q_hi(b, g + 1, i - 6)

                def q_hi(b, g, c):
                    if c == 0:
                        for j in range(HG):
                            act.wait_ge(stack_in[j], 64 * (4 * b + g))
                    act.wait_ge(proj_read[c], FILLS * b + FILL_QK + g + 1)
                    act.activation(parts[:, 2 * c, :], wide[:, c, :], ACT.Copy).then_inc(qk_hi, 1)

                with act.Fori(0, B) as b:
                    split_hi(0, W0 * b + W0_V, ff2_done, NF * b)
                    split_hi(1, W1_ * b + W1_V, ff2_done, NF * b)
                    for k in range(KB):
                        act.wait_ge(turn_full, TURNS * b + k + 1)
                        if k == 0:
                            act.wait_ge(proj_full[0], FILLS * b)
                        turn_hi_from(b, k, turns[k % 2][:], k)
                    act.wait_ge(vg_copied, NH * b)
                    for t in range(TB):
                        act.wait_ge(proj_full[t % 2], FILLS * b + FILL_V + t // 2 + 1)
                        act.activation(V[:, t, :], proj[t % 2][:], ACT.Copy).then_inc(proj_read[t % 2], 1)
                        if t == TB - 1:
                            split_hi(0, W0 * b + W0_QK, proj_full[1], FILLS * b + FILL_QK)
                    for c in range(2):
                        q_hi(b, 0, c)
                    for m in range(5):
                        exp(b, 64 * b + m, m)
                    group(b, 0, True, False)
                    with act.Fori(1, G - 1) as g:
                        group(b, g, False, False)
                    group(b, G - 1, False, True)
                    split_hi(0, W0 * b + W0_O, proj_full[1], FILLS * b + FILL_QK + G)
                    split_hi(1, W1_ * b + W1_O, proj_full[1], FILLS * b + FILL_QK + G)
                    for g in range(G):
                        if g == 0:
                            act.wait_ge(ctx_copied, NH * b + NH)
                        act.activation(xT[0][:, g, :], ctxT[:, g, :], ACT.Copy).then_inc(ctx_hi, 1)
                    split_hi(0, W0 * b + W0_F, proj_full[1], FILLS * b + FILL_O + 2)
                    split_hi(1, W1_ * b + W1_F, proj_full[1], FILLS * b + FILL_O + 2)
                    for k in range(KB):
                        act.wait_ge(turn_wide, KB * b + k + 1)
                        turn_hi_from(b, KB + k, wide[:, k % 2, :], k)

                    def chunk(i, s, first, last):
                        n = NF * b + 2 * i + s
                        act.wait_ge(proj_read[s], FILLS * b + FILL_F + i + 1)
                        act.wait_ge(g_lo, NF * b if first else n - 1)
                        act.activation(gel[:, s, :], wide[:, s, :], ACT.Gelu_apprx_sigmoid).then_inc(geled, 1)
                        act.wait_ge(geled, n + 1)
                        act.wait_ge(ff2_done, NF * b if first else n - 1)
                        act.activation(parts[:, 2 * s, :], gel[:, s, :], ACT.Copy).then_inc(g_hi, 1)
                        if not last:
                            split_hi(s, (W0 * b + W0_F if s == 0 else W1_ * b + W1_F) + i + 1, ff2_done, n + 1)

                    for s in range(2):
                        chunk(0, s, True, False)
                    with act.Fori(1, NF // 2 - 1) as i:
                        for s in range(2):
                            chunk(i, s, False, False)
                    for s in range(2):
                        chunk(NF // 2 - 1, s, False, True)
                    for k in range(KB):
                        act.wait_ge(turn_full, TURNS * b + 2 * KB + k + 1)
                        turn_hi_from(b, 2 * KB + k, turns[k % 2][:], k)
                    act.wait_ge(hid_wide, b + 1)
                    act.activation(gel[:, 0, :], wide[:, 0, :], ACT.Gelu).then_inc(hid_ready, 1)
                    act.wait_ge(out_ready, b + 1)
                    act.dma_start(rows_of(out, b), res[:]).then_inc(out_done, 16)
                act.wait_ge(out_done, 16 * B)

            @block.tensor
            def _(t):
                def split_product(dst, stat, mov, ks, start, stop):
                    n, count = 0, 3 * len(ks)
                    for k in ks:
                        for hs, hm in ((0, 0), (0, 1), (1, 0)):
                            mm = t.matmul(dst, stat(hs, k), mov(hm, k), start=start and n == 0, stop=stop and n == count - 1)
                            n += 1
                    return mm

                def turn(b, n, src, k):
                    t.wait_ge(turn_lo, TURNS * b + n - 1 if n else TURNS * b)
                    for q in range(TB):
                        mm = t.transpose(turns[k % 2][:, q * P:(q + 1) * P], src[:, q, k * P:(k + 1) * P], ident[:])
                    mm.then_inc(turn_full, 1)

                def v_weight(h, k):
                    return w[k // 2][:, h, 512 * (k % 2):512 * (k % 2) + 512]

                def rows_product(b, fill, x_sem, weights_ready):
                    for q in range(TB):
                        t.wait_ge(proj_read[q % 2], FILLS * b + fill + q // 2)
                        split_product(proj[q % 2][:], lambda h, k: xT[h][:, k, q * P:(q + 1) * P], v_weight, range(KB), True, True) \
                            .then_inc(proj_full[q % 2], 1)

                def qk(b, g, c):
                    t.wait_ge(proj_read[c], FILLS * b + FILL_QK + g)
                    if c == 0:
                        t.wait_ge(w_hi[0], W0 * b + W0_QK + g + 1)
                        t.wait_ge(w_lo[0], W0 * b + W0_QK + g + 1)
                    split_product(proj[c][:], lambda h, k: weight(0, h)[:, KB * c + k, :], lambda h, k: xT[h][:, k, :], range(KB), True, True) \
                        .then_inc(proj_full[c], 1)

                def score_block(b, m, mm, g):
                    j, qb = (mm % 16) // 4, mm % 4
                    t.wait_ge(scored, m - 1 if not isinstance(g, int) or g or mm >= 2 else 64 * b)
                    if qb == 0:
                        t.wait_ge(stack_in[j], 64 * (4 * b + g + 1))
                    t.matmul(score[mm % 2][:], stack[:, j, 0, qb * P:(qb + 1) * P], stack[:, j, 1, :], start=True, stop=True) \
                        .then_inc(score_full, 1)

                def pv(b, m, mm, vals):
                    j, kb = (mm % 16) // 4, mm % 4
                    t.wait_ge(probT_copied, m + 1)
                    if kb == 0:
                        t.wait_ge(vg_copied, vals[0])
                        t.wait_ge(ctx_copied, vals[1])
                    t.matmul(context[DH * j:DH * (j + 1), :], Vg[:, j, kb, :], probT[:, kb, :], start=kb == 0, stop=kb == TB - 1,
                             tile_position=(0, DH * j)).then_inc(pv_done, 1)

                def group(b, g, first, last):
                    n = 4 * b + g
                    for i in range(16):
                        m = 16 * n + i
                        j, kb = i // 4, i % 4
                        if kb == 0:
                            t.wait_ge(normed, m + 4)
                        t.wait_ge(probT_copied, 64 * b if first and i < 2 else m - 1)
                        for q in range(TB):
                            mm = t.transpose(turned[i % 2][:, q * P:(q + 1) * P], prob[j][:, q, kb * P:(kb + 1) * P], ident[:])
                        mm.then_inc(probT_full, 1)
                        if not (last and i + 6 >= 16):
                            score_block(b, m + 6, i + 6, g + (i + 6) // 16 if not first or i + 6 >= 16 else 0)
                        if not last and i in (2, 3):
                            qk(b, g + 1, i - 2)
                        if not (first and i < 2):
                            head = 4 * n + (i - 2) // 4
                            pv(b, m - 2, (i - 2) % 16, (head + 1, NH * b if first else head - 3))

                with t.Fori(0, B) as b:
                    t.wait_ge(tok_ready, b + 1)
                    for k in range(KB):
                        turn(b, k, tok, k)
                    t.wait_ge(w_lo[0], W0 * b + W0_V + 1)
                    t.wait_ge(w_lo[1], W1_ * b + W1_V + 1)
                    t.wait_ge(turn_lo, TURNS * b + KB)
                    rows_product(b, FILL_V, None, None)
                    qk(b, 0, 0)
                    qk(b, 0, 1)
                    for m in range(6):
                        score_block(b, 64 * b + m, m, 0)
                    group(b, 0, True, False)
                    with t.Fori(1, G - 1) as g:
                        group(b, g, False, False)
                    group(b, G - 1, False, True)
                    for mm in (14, 15):
                        pv(b, 64 * b + 48 + mm, mm, None)
                    t.wait_ge(ctx_hi, G * b + G)
                    t.wait_ge(ctx_lo, G * b + G)
                    t.wait_ge(w_lo[0], W0 * b + W0_O + 1)
                    t.wait_ge(w_lo[1], W1_ * b + W1_O + 1)
                    rows_product(b, FILL_O, None, None)
                    t.wait_ge(z2_ready, b + 1)
                    for k in range(KB):
                        turn(b, KB + k, tok, k)
                    t.wait_ge(turn_lo, TURNS * b + 2 * KB)

                    def ff1(i, s):
                        t.wait_ge(w_lo[s], (W0 * b + W0_F if s == 0 else W1_ * b + W1_F) + i + 1)
                        t.wait_ge(proj_read[s], FILLS * b + FILL_F + i)
                        split_product(proj[s][:], lambda h, k: weight(s, h)[:, k, :], lambda h, k: xT[h][:, k, :], range(KB), True, True) \
                            .then_inc(proj_full[s], 1)

                    def ff2(f, s, start, stop):
                        t.wait_ge(g_lo, NF * b + f + 1)
                        for q in range(TB):
                            mm = split_product(ff_sum[q][:], lambda h, _: parts[:, 2 * s + h, q * P:(q + 1) * P],
                                               lambda h, _: w[s][:, h, 512:1024], range(1), start, stop)
                        mm.then_inc(ff2_done, 1)

                    ff1(0, 0)
                    ff1(0, 1)
                    ff2(0, 0, True, False)
                    with t.Fori(1, NF // 2) as i:
                        ff1(i, 0)
                        ff2(2 * i - 1, 1, False, False)
                        ff1(i, 1)
                        ff2(2 * i, 0, False, False)
                    ff2(NF - 1, 1, False, True)
                    t.wait_ge(y_ready, b + 1)
                    for k in range(KB):
                        turn(b, 2 * KB + k, tok, k)
                    t.wait_ge(turn_lo, TURNS * b + 3 * KB)
                    split_product(proj[0][:], lambda h, k: down[h][:, k, :], lambda h, k: xT[h][:, k, :], range(KB), True, True) \
                        .then_inc(proj_full[0], 1)
                    t.wait_ge(hid_ready, b + 1)
                    t.wait_ge(sel_in, 16 * (b + 1))
                    t.matmul(proj[1][:], sel_T[:], gel[:, 0, :], start=True, stop=True).then_inc(proj_full[1], 1)
                    t.wait_ge(mixed, b + 1)
                    for q in range(TB):
                        t.wait_ge(proj_read[q % 2], FILLS * b + FILL_UP + q // 2)
                        t.matmul(proj[q % 2][:], wide[:, 1, q * P:(q + 1) * P], up_T[:], start=True, stop=True).then_inc(proj_full[q % 2], 1)

            @block.vector
            def _(v):
                STEPS = 46
                v.wait_ge(consts_in, 16 * 12)

                def normalise(link, b, n, src, dst, done):
                    for q in range(TB):
                        link.mark(v.bn_stats(stats[:, q, :], src[:, q, :]))
                    link.sync()
                    link.mark(v.tensor_copy(fence[:, 7:8], stats[:, TB - 1, 0:1]))
                    for q in range(TB):
                        link.mark(v.bn_aggr(agg[:, q, :], stats[:, q, :]))
                    link.sync()
                    v.tensor_scalar(var[:], agg[:, :, 1], EPS, None, ALU.add).then_inc(var_ready, 1)
                    v.wait_ge(rstd_ready, 3 * b + n)
                    for q in range(TB):
                        ins = v.tensor_scalar(dst[:, q, :], src[:, q, :], agg[:, q, 0:1], rstd[:, q:q + 1], ALU.subtract, ALU.mult)
                        if q == TB - 1 and done is not None:
                            ins.then_inc(done, 1)
                        else:
                            link.mark(ins)
                    link.sync()

                def turn_lo_part(b, n, k, src):
                    v.wait_ge(turn_hi, TURNS * b + n + 1)
                    v.tensor_tensor(xT[1][:, k, :], src, xT[0][:, k, :].bitcast(F32), ALU.subtract).then_inc(turn_lo, 1)

                def qk_wide(b, g, c):
                    v.wait_ge(proj_full[c], FILLS * b + FILL_QK + g + 1)
                    bias_col = col["bk" if c else "bq"][:, bass.ds(g, 1)]
                    if c:
                        ins = v.tensor_scalar(wide[:, 1, :], proj[1][:], bias_col, None, ALU.add)
                    else:
                        ins = v.tensor_scalar(wide[:, 0, :], proj[0][:], bias_col, QSCALE, ALU.add, ALU.mult)
                    ins.then_inc(proj_read[c], 1)

                def qk_lo_part(b, g, c):
                    v.wait_ge(qk_hi, 8 * b + 2 * g + c + 1)
                    v.tensor_tensor(parts[:, 2 * c + 1, :], wide[:, c, :], parts[:, 2 * c, :].bitcast(F32), ALU.subtract).then_inc(qk_lo, 1)

                def invert(m, mm):
                    v.wait_ge(exped, m + 1)
                    v.reciprocal(inv[:, mm % 16:mm % 16 + 1], total[:, mm % 16:mm % 16 + 1]).then_inc(inverted, 1)

                def scale_rows(m, mm):
                    j, qb = (mm % 16) // 4, mm % 4
                    v.wait_ge(inverted, m + 1)
                    v.tensor_scalar(prob[j][:, qb, :], prob[j][:, qb, :], inv[:, mm % 16:mm % 16 + 1], None, ALU.mult).then_inc(normed, 1)

                def await_scores(n, i):
                    v.wait_ge(score_full, 16 * n + i + 1)
                    if i % 2 == 0:
                        v.wait_ge(bias_masked, 8 * n + i // 2 + 1)

                def scores_at(i):
                    j, qb = (i % 16) // 4, i % 4
                    v.tensor_tensor_reduce(prob[j][:, qb, :], score[i % 2][:], prob[j][:, qb, :], -1.0, MIN_START, ALU.add, ALU.min,
                                           low[:, i % 16:i % 16 + 1]).then_inc(scored, 1)

                def copy_v(b, g, j, pv_count):
                    v.wait_ge(pv_done, pv_count)
                    v.tensor_copy(Vg[:, j, :, :], V[:, :, bass.ds(P * g + DH * j, DH)]).then_inc(vg_copied, 1)

                def take_context(b, g, j):
                    v.wait_ge(pv_done, 64 * b + 16 * g + 4 * j + 4)
                    quad = slice(DH * j, DH * (j + 1))
                    v.tensor_scalar(ctxT[quad, bass.ds(g, 1), :].rearrange("p o s -> p (o s)"), context[quad, :], col["bv"][quad, bass.ds(g, 1)], None, ALU.add) \
                        .then_inc(ctx_copied, 1)

                def group(b, g, first, last):
                    n = 4 * b + g
                    for i in range(16):
                        m = 16 * n + i
                        if not (last and i + 6 >= 16):
                            await_scores(n, i + 6)
                        if not (last and i + 4 >= 16):
                            invert(m + 4, i + 4)
                        if not (last and i + 6 >= 16):
                            scores_at(i + 6)
                        if not (last and i + 4 >= 16):
                            scale_rows(m + 4, i + 4)
                        if i % 4 == 2 and not (first and i == 2):
                            take_context(b, g if i > 2 else g - 1, (i - 6) // 4 % 4)
                        if i == 3:
                            copy_v(b, g, 3, 16 * n)
                        elif i % 4 == 3 and not last:
                            copy_v(b, g + 1, i // 4 - 1, 16 * n + i - 3)
                        if not last and i in (5, 6):
                            qk_wide(b, g + 1, i - 5)
                        if not last and i in (7, 8):
                            qk_lo_part(b, g + 1, i - 7)

                with v.Fori(0, B) as b:
                    link = Link(v, dve_step, STEPS * b)
                    v.wait_ge(mask_in, 16 * (b + 1))
                    v.wait_ge(bias_masked, 32 * b)
                    v.tensor_scalar(mask_add[:], mask8[:], MASKED, None, ALU.mult).then_inc(mask_ready, 1)
                    v.wait_ge(out_ready, b)
                    link(v.tensor_copy(cur[:], scal[:, bass.ds(b, 1), :].rearrange("p o c -> p (o c)")))
                    v.wait_ge(x_in, 16 * (b + 1))
                    normalise(link, b, 1, tok_in, tok_in, None)
                    v.wait_ge(ada_in, 32 * (b + 1))
                    v.tensor_tensor(tok[:], tok_in[:], bcast(scale_row), ALU.mult).then_inc(x_used, 1)
                    v.wait_ge(x_used, b + 1)
                    v.tensor_tensor(tok[:], tok[:], bcast(shift_row), ALU.add).then_inc(tok_ready, 1)
                    for k in range(KB):
                        turn_lo_part(b, k, k, turns[k % 2][:])
                    for c in range(2):
                        qk_wide(b, 0, c)
                    for c in range(2):
                        qk_lo_part(b, 0, c)
                    v.wait_ge(proj_read[0], FILLS * b + FILL_V + 2)
                    v.wait_ge(proj_read[1], FILLS * b + FILL_V + 2)
                    for j in range(3):
                        copy_v(b, 0, j, 64 * b)
                    for i in range(6):
                        await_scores(4 * b, i)
                        v.tensor_copy(fence[:, i:i + 1], cur[:, 0:1])
                        scores_at(i)
                    for i in range(4):
                        invert(64 * b + i, i)
                    for i in range(4):
                        scale_rows(64 * b + i, i)
                    group(b, 0, True, False)
                    with v.Fori(1, G - 1) as g:
                        group(b, g, False, False)
                    group(b, G - 1, False, True)
                    take_context(b, G - 1, 3)
                    for g in range(G):
                        v.wait_ge(ctx_hi, G * b + g + 1)
                        v.tensor_tensor(xT[1][:, g, :], ctxT[:, g, :], xT[0][:, g, :].bitcast(F32), ALU.subtract).then_inc(ctx_lo, 1)
                    v.wait_ge(out_done, 16 * b)
                    v.wait_ge(tok_biased, b + 1)
                    for q in range(TB):
                        v.wait_ge(proj_full[q % 2], FILLS * b + FILL_O + q // 2 + 1)
                        v.tensor_tensor(res[:, q, :], proj[q % 2][:], tok[:, q, :], ALU.add).then_inc(proj_read[q % 2], 1)
                    for s in range(2):
                        v.wait_ge(proj_read[s], FILLS * b + FILL_O + 2)
                    normalise(link, b, 2, res, tok, z2_ready)
                    for k in range(KB):
                        v.wait_ge(turn_full, TURNS * b + KB + k + 1)
                        v.tensor_scalar(wide[:, k % 2, :], turns[k % 2][:], col["g2"][:, k:k + 1], col["beta2"][:, k:k + 1], ALU.mult, ALU.add) \
                            .then_inc(turn_wide, 1)
                        v.wait_ge(turn_wide, KB * b + k + 1)
                        turn_lo_part(b, KB + k, k, wide[:, k % 2, :])

                    def widen(i, s):
                        v.wait_ge(proj_full[s], FILLS * b + FILL_F + i + 1)
                        v.tensor_scalar(wide[:, s, :], proj[s][:], col["b1"][:, bass.ds(2 * i + s, 1)], None, ALU.add).then_inc(proj_read[s], 1)

                    def gelu_lo(i, s):
                        v.wait_ge(g_hi, NF * b + 2 * i + s + 1)
                        v.tensor_tensor(parts[:, 2 * s + 1, :], gel[:, s, :], parts[:, 2 * s, :].bitcast(F32), ALU.subtract).then_inc(g_lo, 1)

                    widen(0, 0)
                    gelu_lo(0, 0)
                    widen(0, 1)
                    gelu_lo(0, 1)
                    with v.Fori(1, NF // 2) as i:
                        for s in range(2):
                            widen(i, s)
                            gelu_lo(i, s)
                    v.wait_ge(ff2_done, NF * b + NF)
                    v.wait_ge(res_biased, b + 1)
                    for q in range(TB):
                        ins = v.tensor_tensor(tok[:, q, :], ff_sum[q][:], res[:, q, :], ALU.add)
                    ins.then_inc(y_ready, 1)
                    for k in range(KB):
                        turn_lo_part(b, 2 * KB + k, k, turns[k % 2][:])
                    v.wait_ge(proj_full[0], FILLS * b + FILL_L2 + 1)
                    v.tensor_scalar(wide[:, 0, :], proj[0][:], col["down_b"][:, 0:1], None, ALU.add).then_inc(proj_read[0], 1)
                    v.wait_ge(proj_read[0], FILLS * b + FILL_L2 + 1)
                    v.sem_inc(hid_wide, 1)
                    v.wait_ge(hid_ready, b + 1)
                    v.wait_ge(proj_full[1], FILLS * b + FILL_L2 + 1)
                    v.tensor_scalar(wide[:, 1, :], proj[1][:], cur[:, 0:1], cur[:, 2:3], ALU.mult, ALU.add).then_inc(proj_read[1], 1)
                    v.wait_ge(proj_read[1], FILLS * b + FILL_L2 + 1)
                    v.scalar_tensor_tensor(wide[:, 1, :], gel[:, 0, :], cur[:, 1:2], wide[:, 1, :], ALU.mult, ALU.add).then_inc(mixed, 1)
                    v.wait_ge(y_biased, b + 1)
                    for q in range(TB):
                        v.wait_ge(proj_full[q % 2], FILLS * b + FILL_UP + q // 2 + 1)
                        v.tensor_tensor(res[:, q, :], proj[q % 2][:], res[:, q, :], ALU.add).then_inc(proj_read[q % 2], 1)
                    for s in range(2):
                        v.wait_ge(proj_read[s], FILLS * b + FILL_UP + 2)
                    normalise(link, b, 3, res, res, None)
                    link(v.tensor_tensor(res[:], res[:], bcast(row["gamma"]), ALU.mult))
                    link(v.tensor_tensor(res[:], res[:], bcast(row["beta"]), ALU.add))
                    quads = res[:].rearrange("p t (q c) -> p (t q) c", c=4)
                    sines = tok[:].rearrange("p t (q c) -> p (t q) c", c=4)
                    for h in range(2):
                        link.mark(v.tensor_scalar(sines[:, :, 2 * h:2 * h + 2], quads[:, :, 2 * h:2 * h + 2], cur[:, 4 + 2 * h:5 + 2 * h], None, ALU.mult))
                    link.sync()
                    for h in range(2):
                        for c in range(2):
                            a, o = 2 * h + c, 2 * h + 1 - c
                            ins = v.scalar_tensor_tensor(quads[:, :, a], quads[:, :, a], cur[:, 3 + 2 * h:4 + 2 * h], sines[:, :, o],
                                                         ALU.mult, ALU.add if c == 0 else ALU.subtract)
                            if a < 3:
                                link.mark(ins)
                    ins.then_inc(out_ready, 1)
                    link.sync()
                    assert link.n == STEPS, link.n


def program(nc, x, dt, step_id, bias, domain, theta, phi, mask, A_grid, B_grid, W_ada, b_ada, Wq, bq, Wk, bk, Wv, bv,
            Wo, bo, W1, b1, W2, b2, g2, beta2, down_W, down_b, up_W, up_b, expert_W, expert_b, emb, gamma, beta,
            freqs, lane, identity, out):
    x1 = nc.dram_tensor("x1", [B, S, D], F32).ap()
    ada_rows = nc.dram_tensor("ada_rows", [B, 2 * D], F32).ap()
    sel_rows = nc.dram_tensor("sel_rows", [B, A * A], F32).ap()
    sel_turned = nc.dram_tensor("sel_turned", [B, A, A], F32).ap()
    field_step(nc, x, A_grid, B_grid, dt, x1)
    field_edges(nc, x, A_grid, B_grid, dt, x1)
    with ExitStack() as ctx:
        sb = lambda name, shape, t=F32: ctx.enter_context(nc.sbuf_tensor(name, shape, t))
        keep = {"ident": sb("ident", [P, P]), "scal": sb("scal", [P, B, 8]), "up_T": sb("up_T", [A, D]),
                "down_hi": sb("down_hi", [P, KB, A], F32R), "down_lo": sb("down_lo", [P, KB, A], F32R)}
        for name in ("ident_in", "prep_sin", "prep_emb", "prep_ada", "prep_turn"):
            keep[name] = ctx.enter_context(nc.semaphore(name))
        with nc.Block() as block:

            @block.sync
            def _(sp):
                sp.dma_start(keep["ident"][:], identity).then_inc(keep["ident_in"], 16)
                sp.wait_ge(keep["ident_in"], 16)

            @block.gpsimd
            def _(pool):
                pool.memset(keep["scal"][:], 0.0)

        prepare(nc, keep, step_id, domain, theta, phi, W_ada, b_ada, down_W, up_W, expert_W, expert_b, emb,
                freqs, lane, ada_rows, sel_rows, sel_turned)
        layers(nc, keep, x1, mask, bias, ada_rows, sel_turned, Wq, bq, Wk, bk, Wv, bv, Wo, bo, W1, b1, W2, b2, g2, beta2,
               down_b, up_b, gamma, beta, out)


_INS = ["x", "condB_dt", "itok_B_34_63", "fside_Bx16xSxS_0", "itok_B_0_15", "condB_theta", "condB_phi", "mask_Bx1xSxS_bk0",
        "L0_cond_A_grid", "L0_cond_B_grid", "L1_cond_W_ada", "L1_cond_b_ada", "L1_cond_Wq", "L1_cond_bq", "L1_cond_Wk",
        "L1_cond_bk", "L1_cond_Wv", "L1_cond_bv", "L1_cond_Wo", "L1_cond_bo", "L1_cond_W1", "L1_cond_b1", "L1_cond_W2",
        "L1_cond_b2", "L1_cond_g2", "L1_cond_beta2", "L2_cond_down_W", "L2_cond_down_b", "L2_cond_up_W", "L2_cond_up_b",
        "L2_cond_expert_W", "L2_cond_expert_b", "L2_cond_domain_emb", "L2_cond_ln_gamma", "L2_cond_ln_beta"]


def constants():
    half = D // 2
    step = np.float32(-np.log(10000.0) / (half - 1))
    return {"freqs": np.exp(np.arange(half, dtype=np.float32) * step).astype(np.float32),
            "lane": np.arange(P, dtype=np.float32).reshape(P, 1), "identity": np.eye(P, dtype=np.float32)}


def kernel(**inputs):
    import concourse.bacc as bacc
    from concourse.bass_utils import run_bass_kernel_spmd

    nc = bacc.Bacc("TRN2", target_bir_lowering=False, num_devices=1)
    arrays, args = {}, []
    for name in _INS:
        a = np.ascontiguousarray(inputs[name])
        arrays[f"in_{name}"] = a
    for name, a in constants().items():
        arrays[f"in_{name}"] = a
    for name, a in arrays.items():
        args.append(nc.dram_tensor(name, a.shape, mybir.dt.from_np(a.dtype), kind="ExternalInput").ap())
    args.append(nc.dram_tensor("out", (B, S, D), F32, kind="ExternalOutput").ap())
    program(nc, *args)
    r = run_bass_kernel_spmd(nc, [arrays], core_ids=[0])
    return r.results[0]["out"]
```

```python
from contextlib import ExitStack

import numpy as np

import concourse.bass as bass
from concourse import mybir

F32 = mybir.dt.float32
F32R = mybir.dt.float32r
BF16 = mybir.dt.bfloat16
U8 = mybir.dt.uint8
I32 = mybir.dt.int32
ALU = mybir.AluOpType
ACT = mybir.ActivationFunctionType

P = 128
B, S, D = 16, 512, 512
NH, DH = 16, 32
FF = 2048
A, E = 128, 16
TB = S // P
KB = D // P
G = NH * DH // P
HG = P // DH
NF = FF // P
EPS = 1e-5
QSCALE = float(DH) ** -0.5
MASKED = -3.0e38
MIN_START = 1.0e30
MAGIC = 12582912.0
PI = float(np.pi)
TWO_PI = (6.28125, 0.0019340515136718750, 1.2556659146713e-06)

FILLS = 19
FILL_V, FILL_QK, FILL_O, FILL_F, FILL_L2, FILL_UP = 0, 2, 6, 8, 16, 17
ITEMS = (10, 6, 4, 4)
W0_V, W0_QK, W0_O = 0, 1, 5
W1_V, W1_O = 0, 1
F_ITEM = (6, 2, 0, 0)
START = 2
TURNS = 12


class Link:

    def __init__(self, eng, sem, base=0):
        self.eng, self.sem, self.base, self.n = eng, sem, base, 0

    def mark(self, ins):
        ins.then_inc(self.sem, 1)
        self.n += 1

    def sync(self):
        self.eng.wait_ge(self.sem, self.base + self.n)

    def __call__(self, ins):
        self.mark(ins)
        self.sync()


def pair(ap, c):
    n = ap.shape[2]
    return ap[:, :, c:n - c:n - 1 - 2 * c]


def end_slope(link, v, tmp, w):
    link(v.tensor_scalar(tmp, pair(w, 0), -3.0, None, ALU.mult))
    link(v.scalar_tensor_tensor(tmp, pair(w, 1), 4.0, tmp, ALU.mult, ALU.add))
    link(v.tensor_tensor(tmp, tmp, pair(w, 2), ALU.subtract))


def slope_y(link, v, out, w, tmp):
    v.tensor_tensor(out[:, :, 1:D - 1], w[:, :, 2:D], w[:, :, 0:D - 2], ALU.subtract)
    end_slope(link, v, tmp, w)
    v.tensor_copy(out[:, :, 0:1], tmp[:, :, 0:1])
    link(v.tensor_scalar(out[:, :, D - 1:D], tmp[:, :, 1:2], -1.0, None, ALU.mult))


def sub_slope_y(link, v, s, w, tmp):
    link(v.tensor_tensor(s[:, :, 1:D - 1], s[:, :, 1:D - 1], w[:, :, 2:D], ALU.subtract))
    link(v.tensor_tensor(s[:, :, 1:D - 1], s[:, :, 1:D - 1], w[:, :, 0:D - 2], ALU.add))
    end_slope(link, v, tmp, w)
    link(v.tensor_tensor(s[:, :, 0:1], s[:, :, 0:1], tmp[:, :, 0:1], ALU.subtract))
    link(v.tensor_tensor(s[:, :, D - 1:D], s[:, :, D - 1:D], tmp[:, :, 1:2], ALU.add))


def add_curve_y(link, v, s, w):
    inner = s[:, :, 1:D - 1]
    link(v.tensor_tensor(inner, inner, w[:, :, 2:D], ALU.add))
    link(v.tensor_tensor(inner, inner, w[:, :, 0:D - 2], ALU.add))
    link(v.scalar_tensor_tensor(inner, w[:, :, 1:D - 1], -2.0, inner, ALU.mult, ALU.add))
    for c, k in enumerate((2.0, -5.0, 4.0, -1.0)):
        link(v.scalar_tensor_tensor(pair(s, 0), pair(w, c), k, pair(s, 0), ALU.mult, ALU.add))


def field_step(nc, x, A_grid, B_grid, dt, x1):
    R = S // P
    with ExitStack() as ctx:
        sb = lambda name, shape, t=F32: ctx.enter_context(nc.sbuf_tensor(name, shape, t))
        sem = lambda name: ctx.enter_context(nc.semaphore(name))
        grid_a0, grid_b0, grid_b2 = (sb(n, [P, R + 2, D]) for n in ("grid_a0", "grid_b0", "grid_b2"))
        grid_a1, grid_b1 = (sb(n, [P, R, D]) for n in ("grid_a1", "grid_b1"))
        field = [sb(f"field{u}", [P, R + 2, D]) for u in range(2)]
        a0f = [sb(f"a0f{u}", [P, R + 2, D]) for u in range(2)]
        b0f = [sb(f"b0f{u}", [P, R + 2, D]) for u in range(2)]
        b1f = [sb(f"b1f{u}", [P, R, D]) for u in range(2)]
        total = [sb(f"total{u}", [P, R, D]) for u in range(2)]
        b2f = sb("b2f", [P, R + 2, D])
        flow = sb("flow", [P, R + 2, D])
        a1f = sb("a1f", [P, R, D])
        half_dt = sb("half_dt", [P, B])
        tmp = sb("tmp", [P, R + 2, 2])
        grids_in, zeroed, dt_in = sem("grids_in"), sem("zeroed"), sem("dt_in")
        field_in = [sem(f"field_in{u}") for u in range(2)]
        products = sem("products")
        dve_step = sem("dve_step")
        stepped = [sem(f"stepped{u}") for u in range(2)]
        clipped = [sem(f"clipped{u}") for u in range(2)]
        stored = [sem(f"stored{u}") for u in range(2)]
        STEPS = 24

        def halo_loads(eng, tile, src, s):
            eng.dma_start(tile[:, 1:R + 1, :], src.rearrange("(p r) c -> p r c", r=R)).then_inc(s, 16)
            eng.dma_start(tile[64:128, 0, :], src[255:508:4, :]).then_inc(s, 16)
            eng.dma_start(tile[1:64, 0, :], src[3:252:4, :]).then_inc(s, 16)
            eng.dma_start(tile[0:64, R + 1, :], src[4:257:4, :]).then_inc(s, 16)
            eng.dma_start(tile[64:127, R + 1, :], src[260:509:4, :]).then_inc(s, 16)

        with nc.Block() as block:

            @block.sync
            def _(sp):
                sp.dma_start(half_dt[:], dt.partition_broadcast(P)).then_inc(dt_in, 16)
                sp.wait_ge(zeroed, 1)
                for tile, src in ((grid_b2, B_grid[2]), (grid_a0, A_grid[0]), (grid_b0, B_grid[0])):
                    halo_loads(sp, tile, src, grids_in)
                for tile, src in ((grid_b1, B_grid[1]), (grid_a1, A_grid[1])):
                    sp.dma_start(tile[:], src.rearrange("(p r) c -> p r c", r=R)).then_inc(grids_in, 16)
                with sp.Fori(0, B // 2) as i:
                    for u in range(2):
                        sp.wait_ge(stepped[u], i)
                        halo_loads(sp, field[u], x[bass.ds(2 * i + u, 1)].rearrange("o s c -> (o s) c"), field_in[u])

            @block.gpsimd
            def _(pool):
                pool.wait_ge(grids_in, 16 * 17)
                with pool.Fori(0, B // 2) as i:
                    for u in range(2):
                        n = 2 * i + u
                        pool.wait_ge(stepped[u], i)
                        pool.wait_ge(stored[u], 16 * i)
                        pool.wait_ge(field_in[u], 80 * (i + 1))
                        pool.tensor_tensor(a0f[u][:], grid_a0[:], field[u][:], ALU.mult).then_inc(products, 1)
                        pool.tensor_tensor(b0f[u][:], grid_b0[:], field[u][:], ALU.mult).then_inc(products, 1)
                        pool.wait_ge(products, 4 * n + 2)
                        pool.tensor_tensor(total[u][:], b0f[u][:, 0:R, :], b0f[u][:, 2:R + 2, :], ALU.add).then_inc(products, 1)
                        pool.tensor_tensor(b1f[u][:], grid_b1[:], field[u][:, 1:R + 1, :], ALU.mult).then_inc(products, 1)

            @block.vector
            def _(v):
                zero = Link(v, dve_step)
                for t in (grid_a0, grid_b0, grid_b2, field[0], field[1]):
                    zero.mark(v.memset(t[:], 0.0))
                zero.sync()
                v.wait_ge(dt_in, 16)
                zero.mark(v.tensor_scalar(half_dt[:], half_dt[:], 0.5, None, ALU.mult))
                zero.sync()
                v.sem_inc(zeroed, 1)
                v.wait_ge(grids_in, 16 * 17)
                with v.Fori(0, B // 2) as i:
                    for u in range(2):
                        n = 2 * i + u
                        link = Link(v, dve_step, STEPS * n + 6)
                        f, s = field[u][:], total[u][:]
                        v.wait_ge(field_in[u], 80 * (i + 1))
                        link(v.tensor_tensor(b2f[:], grid_b2[:], f, ALU.mult))
                        slope_y(link, v, flow[:], b2f[:], tmp[:])
                        v.wait_ge(products, 4 * n + 1)
                        link(v.scalar_tensor_tensor(flow[:], flow[:], 0.5, a0f[u][:], ALU.mult, ALU.subtract))
                        v.wait_ge(products, 4 * n + 3)
                        link(v.scalar_tensor_tensor(s, b0f[u][:, 1:R + 1, :], -2.0, s, ALU.mult, ALU.add))
                        link(v.tensor_tensor(s, s, flow[:, 2:R + 2, :], ALU.add))
                        link(v.tensor_tensor(s, s, flow[:, 0:R, :], ALU.subtract))
                        v.wait_ge(products, 4 * n + 4)
                        add_curve_y(link, v, s, b1f[u][:])
                        link(v.tensor_tensor(a1f[:], grid_a1[:], f[:, 1:R + 1, :], ALU.mult))
                        sub_slope_y(link, v, s, a1f[:], tmp[:, 0:R, :])
                        v.scalar_tensor_tensor(s, s, half_dt[:, bass.ds(n, 1)], f[:, 1:R + 1, :], ALU.mult, ALU.add).then_inc(stepped[u], 1)
                        assert link.n == STEPS

            @block.scalar
            def _(act):
                with act.Fori(0, B // 2) as i:
                    for u in range(2):
                        act.wait_ge(stepped[u], i + 1)
                        act.activation(total[u][:], total[u][:], ACT.Relu).then_inc(clipped[u], 1)
                        act.wait_ge(clipped[u], i + 1)
                        act.dma_start(x1[bass.ds(2 * i + u, 1)].rearrange("o (p r) c -> p (o r) c", r=R),
                                      total[u][:]).then_inc(stored[u], 16)
                act.wait_ge(stored[0], 16 * (B // 2))
                act.wait_ge(stored[1], 16 * (B // 2))


def field_edges(nc, x, A_grid, B_grid, dt, x1):
    NE = 4
    with ExitStack() as ctx:
        sb = lambda name, shape, t=F32: ctx.enter_context(nc.sbuf_tensor(name, shape, t))
        sem = lambda name: ctx.enter_context(nc.semaphore(name))
        Q = 2 * B
        f, ga0, gb0, gb2 = (sb(n, [Q, NE, D]) for n in ("edge_f", "edge_a0", "edge_b0", "edge_b2"))
        ga1, gb1 = (sb(n, [Q, 1, D]) for n in ("edge_a1", "edge_b1"))
        flow, s = sb("edge_flow", [Q, NE, D]), sb("edge_s", [Q, 1, D])
        tmp, scal = sb("edge_tmp", [Q, NE, 2]), sb("edge_scal", [Q, 4])
        loads, steps, stores = sem("edge_loads"), sem("edge_steps"), sem("edge_stores")
        with nc.Block() as block:

            @block.sync
            def _(sp):
                count = 0
                for side in range(2):
                    rows = [r if side == 0 else S - 1 - r for r in range(NE)]
                    half = slice(side * B, side * B + B)
                    for r, row in enumerate(rows):
                        sp.dma_start(f[half, r, :], x[:, row, :]).then_inc(loads, 16)
                        for tile, src in ((ga0, A_grid[0]), (gb0, B_grid[0]), (gb2, B_grid[2])):
                            sp.dma_start(tile[half, r, :], src[row, :].partition_broadcast(B)).then_inc(loads, 16)
                        count += 4
                    for tile, src in ((ga1, A_grid[1]), (gb1, B_grid[1])):
                        sp.dma_start(tile[half, 0, :], src[rows[0], :].partition_broadcast(B)).then_inc(loads, 16)
                    sp.dma_start(scal[half, 0:1], dt.rearrange("(b o) -> b o", o=1)).then_inc(loads, 16)
                    count += 3
                sp.wait_ge(steps, 1000)
                for side, row in ((0, 0), (1, S - 1)):
                    sp.dma_start(x1[0:B, row, :], s[side * B:side * B + B, 0, :]).then_inc(stores, 16)
                sp.wait_ge(stores, 32)

            @block.vector
            def _(v):
                link = Link(v, steps)
                link(v.memset(scal[:, 1:2], -1.0))
                link(v.memset(scal[0:B, 1:2], 1.0))
                v.wait_ge(loads, 16 * 2 * (4 * NE + 3))
                link(v.tensor_scalar(scal[:, 0:1], scal[:, 0:1], 0.5, None, ALU.mult))
                link(v.tensor_tensor(gb2[:], gb2[:], f[:], ALU.mult))
                slope_y(link, v, flow[:], gb2[:], tmp[:])
                link(v.tensor_tensor(ga0[:], ga0[:], f[:], ALU.mult))
                link(v.scalar_tensor_tensor(flow[:], flow[:], 0.5, ga0[:], ALU.mult, ALU.subtract))
                link(v.tensor_scalar(s[:], flow[:, 0:1, :], -3.0, None, ALU.mult))
                link(v.scalar_tensor_tensor(s[:], flow[:, 1:2, :], 4.0, s[:], ALU.mult, ALU.add))
                link(v.tensor_tensor(s[:], s[:], flow[:, 2:3, :], ALU.subtract))
                link(v.tensor_scalar(s[:], s[:], scal[:, 1:2], None, ALU.mult))
                link(v.tensor_tensor(gb0[:], gb0[:], f[:], ALU.mult))
                for r, k in enumerate((2.0, -5.0, 4.0, -1.0)):
                    link(v.scalar_tensor_tensor(s[:], gb0[:, r:r + 1, :], k, s[:], ALU.mult, ALU.add))
                link(v.tensor_tensor(gb1[:], gb1[:], f[:, 0:1, :], ALU.mult))
                add_curve_y(link, v, s[:], gb1[:])
                link(v.tensor_tensor(ga1[:], ga1[:], f[:, 0:1, :], ALU.mult))
                sub_slope_y(link, v, s[:], ga1[:], tmp[:, 0:1, :])
                link(v.scalar_tensor_tensor(s[:], s[:], scal[:, 0:1], f[:, 0:1, :], ALU.mult, ALU.add))
                v.tensor_scalar(s[:], s[:], 0.0, None, ALU.max).then_inc(steps, 1000 - link.n)


def reduce_angle(link, v, r, k):
    link(v.tensor_scalar(k, r, 1.0 / (2.0 * PI), None, ALU.mult))
    link(v.tensor_scalar(k, k, MAGIC, None, ALU.add))
    link(v.tensor_scalar(k, k, -MAGIC, None, ALU.add))
    for c in TWO_PI:
        link(v.scalar_tensor_tensor(r, k, -c, r, ALU.mult, ALU.add))


def quarter_turn(link, v, out, r, k):
    link(v.tensor_scalar(k, r, PI / 2, -2.0 * PI, ALU.is_gt, ALU.mult))
    link(v.tensor_tensor(out, r, k, ALU.add))
    link(v.tensor_scalar(out, out, PI / 2, None, ALU.add))
    for t in (out, r):
        link(v.tensor_scalar(t, t, 3.1415925, -3.1415925, ALU.min, ALU.max))


def prepare(nc, keep, step_id, domain, theta, phi, W_ada, b_ada, down_W, up_W, expert_W, expert_b, emb,
            freqs, lane, ada_rows, sel_rows, sel_turned):
    ident = keep["ident"]
    with ExitStack() as ctx:
        sb = lambda name, shape, t=F32: ctx.enter_context(nc.sbuf_tensor(name, shape, t))
        sem = lambda name: ctx.enter_context(nc.semaphore(name))
        bank = [ctx.enter_context(nc.psum_tensor(f"prep_bank{i}", [P, 512], F32)) for i in range(4)]
        tt = sb("time", [B, 4])
        ti = sb("time_i", [B, 1], I32)
        fr = sb("freqs_sb", [B, D // 2])
        ang, kk, emb_rows = sb("ang", [B, D]), sb("kk", [B, D]), sb("emb_rows", [B, D])
        embT = sb("embT", [P, KB, B])
        w_ada = sb("w_ada", [P, KB, 2 * D])
        bada = sb("bada", [B, 2 * D])
        ada = sb("ada", [B, 2 * D])
        idi, idf = sb("idi", [P, B], I32), sb("idf", [P, B])
        hot, ge, lt = sb("hot", [P, B]), sb("ge", [P, B]), sb("lt", [P, B])
        ln = sb("lane_sb", [P, 1])
        ew = sb("ew", [E, 4096])
        ewo = sb("ewo", [B, 4096])
        vecs = sb("vecs", [E, 2, A])
        bs = sb("bs", [A, 2, B])
        turn = sb("turn", [P, 2, B])
        turn2, tk = sb("turn2", [P, 2, B]), sb("tk", [P, 2, B])
        dw = sb("dw", [A, D])
        uw = sb("uw", [P, KB, A])
        selb = sb("selb", [P, B, A])
        selt = sb("selt", [P, B, A])
        loads, ew_in, steps, pe, at, st, sel_in = (sem(f"prep_{n}") for n in ("loads", "ew_in", "steps", "pe", "at", "st", "sel_in"))
        scal = keep["scal"]

        with nc.Block() as block:

            @block.sync
            def _(sp):
                for dst, src in (
                    (ti[:], step_id.rearrange("(b o) -> b o", o=1)),
                    (fr[:], freqs.partition_broadcast(B)),
                    (w_ada[:], W_ada.rearrange("(k p) n -> p k n", p=P)),
                    (bada[:], b_ada.partition_broadcast(B)),
                    (idi[:], domain.partition_broadcast(P)),
                    (ln[:], lane),
                    (vecs[:, 0, :], expert_b), (vecs[:, 1, :], emb),
                    (turn[:, 0, :], theta.partition_broadcast(P)), (turn[:, 1, :], phi.partition_broadcast(P)),
                    (dw[:], down_W), (uw[:], up_W.rearrange("(k p) a -> p k a", p=P)),
                ):
                    sp.dma_start(dst, src).then_inc(loads, 16)
                ew_flat = expert_W.rearrange("e o a -> e (o a)")
                for r in range(4):
                    if r:
                        sp.wait_ge(pe, 100 + 8 * r)
                    sp.dma_start(ew[:], ew_flat[:, r * 4096:(r + 1) * 4096]).then_inc(ew_in, 16)
                    sp.wait_ge(at, 8 * (r + 1))
                    sp.dma_start(sel_rows[:, r * 4096:(r + 1) * 4096], ewo[:]).then_inc(st, 16)
                    sp.wait_ge(st, 16 * (r + 1))
                sp.dma_start(selb[:], sel_rows.rearrange("b (o a) -> o b a", a=A)).then_inc(sel_in, 16)
                sp.wait_ge(at, 32 + 4)
                sp.dma_start(sel_turned.rearrange("b a o -> a b o"), selt[:]).then_inc(st, 16)
                sp.wait_ge(steps, 1000)
                sp.dma_start(ada_rows, ada[:]).then_inc(st, 16)
                sp.wait_ge(st, 16 * 6)

            @block.vector
            def _(v):
                link = Link(v, steps)
                v.wait_ge(loads, 16 * 12)
                link(v.tensor_scalar(tt[:, 0:1], ti[:], 1.0, None, ALU.mult))
                link(v.tensor_scalar(tt[:, 1:2], tt[:, 0:1], 0.01, None, ALU.mult))
                link(v.tensor_scalar(tt[:, 1:2], tt[:, 1:2], 4000.0, None, ALU.mult))
                link(v.tensor_scalar(ang[:, 0:D // 2], fr[:], tt[:, 1:2], None, ALU.mult))
                reduce_angle(link, v, ang[:, 0:D // 2], kk[:, 0:D // 2])
                quarter_turn(link, v, ang[:, D // 2:D], ang[:, 0:D // 2], kk[:, 0:D // 2])
                reduce_angle(link, v, turn[:], tk[:])
                quarter_turn(link, v, turn2[:], turn[:], tk[:])
                link(v.tensor_scalar(idf[:], idi[:], 1.0, None, ALU.mult))
                link(v.tensor_scalar(ge[:], idf[:], 0.0, None, ALU.is_ge))
                link(v.tensor_scalar(lt[:], idf[:], float(E), None, ALU.is_lt))
                link(v.tensor_tensor(ge[:], ge[:], lt[:], ALU.mult))
                link(v.tensor_scalar(idf[:], idf[:], 0.0, float(E - 1), ALU.max, ALU.min))
                link(v.tensor_scalar(hot[:], idf[:], ln[:, 0:1], None, ALU.is_equal))
                v.sem_inc(pe, 100)
                link(v.tensor_copy(scal[:, :, 0], ge[:]))
                link(v.tensor_scalar(scal[:, :, 1], ge[:], -1.0, 1.0, ALU.mult, ALU.add))
                v.wait_ge(keep["prep_sin"], 1)
                link(v.scalar_tensor_tensor(emb_rows[:], kk[:], 1.0, ang[:], ALU.add, ALU.mult))
                v.sem_inc(keep["prep_emb"], 1)
                v.wait_ge(keep["prep_ada"], 1)
                link(v.tensor_copy(embT[:], bank[3][:, 0:KB * B].rearrange("p (k b) -> p k b", b=B)))
                v.sem_inc(keep["prep_emb"], 1)
                v.wait_ge(keep["prep_ada"], 3)
                for h in range(2):
                    link(v.scalar_tensor_tensor(ada[:, h * D:h * D + D], bank[2 + h][0:B, :], 0.5, bada[:, h * D:h * D + D], ALU.mult, ALU.add))
                link(v.tensor_scalar(ada[:, 0:D], ada[:, 0:D], 1.0, None, ALU.add))
                v.sem_inc(keep["prep_emb"], 1)
                v.wait_ge(keep["prep_ada"], 4)
                link(v.tensor_copy(bs[:], bank[2][:, 0:2 * B].rearrange("p (v b) -> p v b", v=2)))
                link(v.tensor_tensor(bs[:, 0, :], bs[:, 0, :], scal[:, :, 0], ALU.mult))
                link(v.tensor_tensor(scal[:, :, 2], bs[:, 0, :], bs[:, 1, :], ALU.add))
                v.sem_inc(keep["prep_emb"], 1)
                v.wait_ge(keep["prep_ada"], 5)
                link(v.tensor_copy(keep["down_hi"][:], bank[3][:].rearrange("p (k a) -> p k a", a=A)))
                link(v.tensor_tensor(keep["down_lo"][:], bank[3][:].rearrange("p (k a) -> p k a", a=A), keep["down_hi"][:], ALU.subtract))
                v.sem_inc(keep["prep_emb"], 1)
                v.wait_ge(keep["prep_ada"], 6)
                v.tensor_copy(keep["up_T"][:], bank[2][:]).then_inc(steps, 1000 - link.n)

            @block.scalar
            def _(act):
                act.wait_ge(steps, 3 + 1 + 6 + 5 + 6 + 5)
                act.activation(ang[:], ang[:], ACT.Sin)
                act.activation(scal[:, :, 4], turn[:, 0, :], ACT.Sin)
                act.activation(scal[:, :, 6], turn[:, 1, :], ACT.Sin)
                act.activation(scal[:, :, 3], turn2[:, 0, :], ACT.Sin)
                act.activation(scal[:, :, 5], turn2[:, 1, :], ACT.Sin).then_inc(keep["prep_turn"], 1)
                act.wait_ge(keep["prep_turn"], 1)
                act.activation(kk[:], ang[:], ACT.Tanh, scale=0.5).then_inc(keep["prep_sin"], 1)
                for r in range(4):
                    for c in range(8):
                        m = 8 * r + c
                        act.wait_ge(pe, 100 + m + 1)
                        if c == 0 and r:
                            act.wait_ge(st, 16 * r)
                        act.activation(ewo[:, c * 512:(c + 1) * 512], bank[m % 2][0:B, :], ACT.Copy).then_inc(at, 1)
                for q in range(4):
                    act.wait_ge(pe, 100 + 32 + q + 1)
                    act.activation(selt[:, 4 * q:4 * q + 4, :], bank[q % 2][:].rearrange("p (b a) -> p b a", a=A), ACT.Copy).then_inc(at, 1)

            @block.tensor
            def _(t):
                t.wait_ge(loads, 16 * 12)
                t.wait_ge(keep["ident_in"], 16)
                t.wait_ge(pe, 100)
                t.wait_ge(keep["prep_emb"], 1)
                for k in range(KB):
                    mm = t.transpose(bank[3][:, k * B:k * B + B], emb_rows[:, k * P:k * P + P], ident[0:B, 0:B])
                mm.then_inc(keep["prep_ada"], 1)
                t.wait_ge(keep["prep_emb"], 2)
                for h in range(2):
                    for k in range(KB):
                        mm = t.matmul(bank[2 + h][0:B, :], embT[:, k, :], w_ada[:, k, h * D:h * D + D], start=k == 0, stop=k == KB - 1)
                    mm.then_inc(keep["prep_ada"], 1)
                t.wait_ge(keep["prep_emb"], 3)
                for w in range(2):
                    mm = t.matmul(bank[2][:, w * B:w * B + B], vecs[:, w, :], hot[0:E, :], start=True, stop=True)
                mm.then_inc(keep["prep_ada"], 1)
                t.wait_ge(keep["prep_emb"], 4)
                for k in range(KB):
                    mm = t.transpose(bank[3][:, k * A:k * A + A], dw[:, k * P:k * P + P], ident[:])
                mm.then_inc(keep["prep_ada"], 1)
                t.wait_ge(keep["prep_emb"], 5)
                for k in range(KB):
                    mm = t.transpose(bank[2][:, k * P:k * P + P], uw[:, k, :], ident[:])
                mm.then_inc(keep["prep_ada"], 1)
                for r in range(4):
                    t.wait_ge(ew_in, 16 * (r + 1))
                    for c in range(8):
                        m = 8 * r + c
                        if m >= 2:
                            t.wait_ge(at, m - 1)
                        t.matmul(bank[m % 2][0:B, :], hot[0:E, :], ew[:, c * 512:(c + 1) * 512], start=True, stop=True).then_inc(pe, 1)
                t.wait_ge(sel_in, 16)
                for q in range(4):
                    t.wait_ge(at, 32 + q - 1)
                    for j in range(4):
                        mm = t.transpose(bank[q % 2][:, j * A:j * A + A], selb[:, 4 * q + j, :], ident[:])
                    mm.then_inc(pe, 1)


def layers(nc, keep, x1, mask, bias, ada_rows, sel_turned, Wq, bq, Wk, bk, Wv, bv, Wo, bo, W1, b1, W2, b2, g2, beta2,
           down_b, up_b, gamma, beta, out):
    ident, scal, down, up_T = keep["ident"], keep["scal"], (keep["down_hi"], keep["down_lo"]), keep["up_T"]
    with ExitStack() as ctx:
        sb = lambda name, shape, t=F32: ctx.enter_context(nc.sbuf_tensor(name, shape, t))
        sem = lambda name: ctx.enter_context(nc.semaphore(name))

        bank = [ctx.enter_context(nc.psum_tensor(f"bank{i}", [P, 512], F32)) for i in range(8)]
        proj, score, turned, context, turns = bank[0:2], bank[2:4], bank[4:6], bank[6], bank[6:8]
        ff_sum = bank[2:6]

        col = {n: sb(f"{n}_col", [P, w]) for n, w in (("bq", G), ("bk", G), ("bv", G), ("b1", NF), ("g2", KB), ("beta2", KB), ("down_b", 1))}
        row = {n: sb(f"{n}_row", [P, D]) for n in ("bo", "b2", "up_b", "gamma", "beta")}
        minus_half = sb("minus_half", [P, TB])
        scale_row, shift_row = sb("scale_row", [P, D]), sb("shift_row", [P, D])
        mask8, mask_add = sb("mask8", [P, TB, S], U8), sb("mask_add", [P, TB, S], BF16)
        sel_T = sb("sel_T", [A, A])
        cur = sb("cur", [P, 8])
        tok_in = sb("tok_in", [P, TB, D])
        tok = sb("tok", [P, TB, D])
        res = sb("res", [P, TB, D])
        xT = [sb(f"xT{h}", [P, KB, S], F32R) for h in range(2)]
        stats, agg, fence = sb("stats", [P, TB, 6]), sb("agg", [P, TB, 2]), sb("fence", [P, 8])
        var, rstd = sb("var", [P, TB]), sb("rstd", [P, TB])
        V = sb("V", [P, TB, D])
        Vg = sb("Vg", [P, HG, TB, DH])
        wide = sb("wide", [P, 2, 512])
        parts = sb("parts", [P, 4, 512], F32R)
        stack = sb("stack", [P, HG, 2, 512], F32R)
        prob = [sb(f"prob{j}", [P, TB, S]) for j in range(HG)]
        low, total, inv = (sb(n, [P, 16]) for n in ("low", "total", "inv"))
        probT = sb("probT", [P, TB, S])
        ctxT = sb("ctxT", [P, G, S])
        gel = sb("gel", [P, 2, 512])
        w_raw = [sb(f"w_raw{s}", [P, 1024])[:] for s in range(2)]
        w_raw += [V[:, 2 * s:2 * s + 2, :].rearrange("p a b -> p (a b)") for s in range(2)]
        w = [sb(f"w{s}", [P, 2, 1024], F32R)[:] for s in range(2)]
        w += [stack[:, 2 * s:2 * s + 2, :, :].rearrange("p h a b -> p h (a b)") for s in range(2)]

        consts_in, half_set = sem("consts_in"), sem("half_set")
        x_in, ada_in, mask_in, sel_in = sem("x_in"), sem("ada_in"), sem("mask_in"), sem("sel_in")
        raw_in = [sem(f"raw_in{s}") for s in range(4)]
        bias_in = [[sem(f"bias_in{j}_{h}") for h in range(2)] for j in range(HG)]
        stack_in = [sem(f"stack_in{j}") for j in range(HG)]
        out_done = sem("out_done")
        dve_step = sem("dve_step")
        var_ready, rstd_ready = sem("var_ready"), sem("rstd_ready")
        x_used, tok_ready, mask_ready = sem("x_used"), sem("tok_ready"), sem("mask_ready")
        tok_biased = sem("tok_biased")
        w_hi, w_lo = [sem(f"w_hi{s}") for s in range(4)], [sem(f"w_lo{s}") for s in range(4)]
        turn_full, turn_hi, turn_lo, turn_wide = sem("turn_full"), sem("turn_hi"), sem("turn_lo"), sem("turn_wide")
        proj_full, proj_read = [sem(f"proj_full{s}") for s in range(2)], [sem(f"proj_read{s}") for s in range(2)]
        v_copied, vg_copied = sem("v_copied"), sem("vg_copied")
        qk_hi, qk_lo = sem("qk_hi"), sem("qk_lo")
        bias_masked, score_full, scored, exped, inverted, normed = (sem(n) for n in ("bias_masked", "score_full", "scored", "exped", "inverted", "normed"))
        probT_full, probT_copied, pv_done, ctx_copied = (sem(n) for n in ("probT_full", "probT_copied", "pv_done", "ctx_copied"))
        ctx_hi, ctx_lo = sem("ctx_hi"), sem("ctx_lo")
        z2_ready, res_biased, geled, g_hi, g_lo, ff2_done = (sem(n) for n in ("z2_ready", "res_biased", "geled", "g_hi", "g_lo", "ff2_done"))
        y_ready, y_biased, hid_wide, hid_ready, mixed, out_ready = (sem(n) for n in ("y_ready", "y_biased", "hid_wide", "hid_ready", "mixed", "out_ready"))

        rows_of = lambda t, b: t[bass.ds(b, 1)].rearrange("o (t p) c -> p (o t) c", p=P)
        bcast = lambda t: t[:].unsqueeze(1).to_broadcast([P, TB, D])
        weight = lambda s, h: w[s][:, h, :].rearrange("p (k n) -> p k n", k=8)

        def chunk_item(b, i, c):
            i, c = (i + 1, c - 4) if c >= 4 else (i, c)
            s = (c + 2) % 4
            return s, ITEMS[s] * b + F_ITEM[s] + i

        with nc.Block() as block:

            @block.sync
            def _(sp):
                for signal in (*w_hi, *w_lo, *proj_full, *proj_read, probT_full, x_used, tok_ready, mask_ready, mixed, ff2_done,
                               vg_copied, pv_done, g_lo, turn_lo, scored, probT_copied, ctx_copied, bias_masked, out_ready):
                    sp.sem_inc(signal, START)
                sp.sem_inc(out_done, 16)
                for signal in stack_in:
                    sp.sem_inc(signal, 64)
                for n, src, wd in (("bq", bq, G), ("bk", bk, G), ("bv", bv, G), ("b1", b1, NF), ("g2", g2, KB), ("beta2", beta2, KB), ("down_b", down_b, 1)):
                    sp.dma_start(col[n][:], src.rearrange("(k p) -> p k", p=P), allow_slow_non_contiguous=True).then_inc(consts_in, 16)
                for n, src in (("bo", bo), ("b2", b2), ("up_b", up_b), ("gamma", gamma), ("beta", beta)):
                    sp.dma_start(row[n][:], src.partition_broadcast(P)).then_inc(consts_in, 16)

                def load_weight(s, count, first, second):
                    sp.wait_ge(w_hi[s], count + START)
                    sp.wait_ge(w_lo[s], count + START)
                    for dst, src in (first, second):
                        sp.dma_start(dst, src).then_inc(raw_in[s], 16)

                raw = lambda s, h: w_raw[s][:, 512 * h:512 * h + 512]
                blocks = lambda s, h: raw(s, h).rearrange("p (k n) -> p k n", k=4)

                def load_qk(b, g):
                    load_weight(0, ITEMS[0] * b + W0_QK + g, *(
                        (blocks(0, h), t[:, bass.ds(P * g, P)].rearrange("(k p) n -> p k n", p=P)) for h, t in ((0, Wq), (1, Wk))))

                def load_rows(s, count, t, k):
                    load_weight(s, count, *((raw(s, h), t[P * (k + h):P * (k + h + 1), :]) for h in range(2)))

                def load_bias(b, g, j):
                    src = bias[bass.ds(b, 1), bass.ds(HG * g + j, 1)].rearrange("o h (t p) k -> p (o h t) k", p=P)
                    for h in range(2):
                        sp.dma_start(prob[j][:, 2 * h:2 * h + 2, :], src[:, 2 * h:2 * h + 2, :]).then_inc(bias_in[j][h], 16)

                def load_stack(b, g, j):
                    for quad, (q, step) in enumerate(((0, 2), (1, 1), (0, 3), (1, 2))):
                        sp.dma_start(stack[DH * quad:DH * (quad + 1), j, :, :].bitcast(F32),
                                     parts[DH * j:DH * (j + 1), q:q + step + 1:step, :].bitcast(F32)).then_inc(stack_in[j], 16)

                def group(b, g):
                    n = 4 * b + g
                    sp.wait_ge(probT_full, 16 * n + 4 + START)
                    load_bias(b, g + 1, 0)
                    sp.wait_ge(qk_hi, 2 * n + 4)
                    sp.wait_ge(qk_lo, 2 * n + 4)
                    for j in range(HG):
                        if j == 3:
                            sp.wait_ge(probT_full, 16 * n + 8 + START)
                            load_bias(b, g + 1, 1)
                        if j:
                            sp.wait_ge(score_full, 16 * n + 4 * j + 4)
                        load_stack(b, g + 1, j)
                    for j in (2, 3):
                        sp.wait_ge(probT_full, 16 * n + 4 * j + 4 + START)
                        load_bias(b, g + 1, j)

                def load_chunk(s, count, f):
                    load_weight(s, count, (blocks(s, 0), W1[:, bass.ds(P * f, P)].rearrange("(k p) n -> p k n", p=P)),
                                (raw(s, 1), W2[bass.ds(P * f, P), :]))

                with sp.Fori(0, B) as b:
                    sp.wait_ge(probT_full, 64 * b + START)
                    for j in range(2):
                        load_bias(b, 0, j)
                    sp.wait_ge(x_used, b + START)
                    sp.dma_start(tok_in[:], rows_of(x1, b)).then_inc(x_in, 16)
                    sp.wait_ge(tok_ready, b + START)
                    sp.dma_start(scale_row[:], ada_rows[bass.ds(b, 1), 0:D].rearrange("o c -> (o c)").partition_broadcast(P)).then_inc(ada_in, 16)
                    sp.dma_start(shift_row[:], ada_rows[bass.ds(b, 1), D:2 * D].rearrange("o c -> (o c)").partition_broadcast(P)).then_inc(ada_in, 16)
                    sp.wait_ge(mask_ready, b + START)
                    sp.dma_start(mask8[:], mask[bass.ds(b, 1), 0].rearrange("o (t p) k -> p (o t) k", p=P)).then_inc(mask_in, 16)
                    load_rows(0, ITEMS[0] * b + W0_V, Wv, 0)
                    load_rows(1, ITEMS[1] * b + W1_V, Wv, 2)
                    for j in range(2, HG):
                        load_bias(b, 0, j)
                    load_qk(b, 0)
                    sp.wait_ge(mixed, b + START)
                    sp.dma_start(sel_T[:], sel_turned[bass.ds(b, 1)].rearrange("o a c -> a (o c)")).then_inc(sel_in, 16)
                    load_qk(b, 1)
                    load_rows(1, ITEMS[1] * b + W1_O, Wo, 2)
                    sp.wait_ge(ff2_done, NF * b + START)
                    sp.wait_ge(qk_hi, 8 * b + 2)
                    sp.wait_ge(qk_lo, 8 * b + 2)
                    for j in range(HG):
                        load_stack(b, 0, j)
                    load_qk(b, 2)
                    group(b, 0)
                    load_qk(b, 3)
                    group(b, 1)
                    load_rows(0, ITEMS[0] * b + W0_O, Wo, 0)
                    group(b, 2)
                    sp.wait_ge(vg_copied, NH * (b + 1) + START)
                    for c in range(4):
                        load_chunk(*chunk_item(b, 0, c), c)
                    with sp.Fori(1, NF // 4) as i:
                        for c in range(4):
                            load_chunk(*chunk_item(b, i, c), 4 * i + c)

            @block.gpsimd
            def _(pool):
                pool.memset(minus_half[:], -0.5).then_inc(half_set, 1)
                pool.wait_ge(half_set, 1)
                pool.wait_ge(consts_in, 16 * 12)

                def split_lo(s, count):
                    pool.wait_ge(w_hi[s], count + 1 + START)
                    pool.tensor_tensor(w[s][:, 1, :], w_raw[s], w[s][:, 0, :].bitcast(F32), ALU.subtract).then_inc(w_lo[s], 1)

                def root(count):
                    pool.wait_ge(var_ready, count)
                    pool.tensor_tensor(rstd[:], var[:], minus_half[:], ALU.pow).then_inc(rstd_ready, 1)

                def add_mask(b, g, j):
                    for h in range(2):
                        pool.wait_ge(bias_in[j][h], 16 * (4 * b + g + 1))
                        half = prob[j][:, 2 * h:2 * h + 2, :]
                        pool.tensor_tensor(half, half, mask_add[:, 2 * h:2 * h + 2, :], ALU.add).then_inc(bias_masked, 1)

                def group(b, g):
                    for j in (2, 3):
                        add_mask(b, g, j)
                    add_mask(b, g + 1, 0)
                    split_lo(0, ITEMS[0] * b + W0_QK + g + 2)
                    add_mask(b, g + 1, 1)

                with pool.Fori(0, B) as b:
                    split_lo(0, ITEMS[0] * b + W0_V)
                    root(3 * b + 1)
                    split_lo(1, ITEMS[1] * b + W1_V)
                    pool.wait_ge(mask_ready, b + 1 + START)
                    add_mask(b, 0, 0)
                    split_lo(0, ITEMS[0] * b + W0_QK)
                    add_mask(b, 0, 1)
                    pool.wait_ge(turn_full, TURNS * b + KB)
                    pool.tensor_tensor(tok[:], tok[:], bcast(row["bo"]), ALU.add).then_inc(tok_biased, 1)
                    split_lo(0, ITEMS[0] * b + W0_QK + 1)
                    for g in range(G - 1):
                        group(b, g)
                        if g == 0:
                            split_lo(1, ITEMS[1] * b + W1_O)
                    for j in (2, 3):
                        add_mask(b, G - 1, j)
                    for c in range(2):
                        split_lo(*chunk_item(b, 0, c))
                    root(3 * b + 2)
                    split_lo(*chunk_item(b, 0, 2))
                    pool.wait_ge(z2_ready, b + 1)
                    pool.tensor_tensor(res[:], res[:], bcast(row["b2"]), ALU.add).then_inc(res_biased, 1)
                    split_lo(*chunk_item(b, 0, 3))
                    with pool.Fori(1, NF // 4) as i:
                        for c in range(4):
                            split_lo(*chunk_item(b, i, c))
                    pool.wait_ge(y_ready, b + 1)
                    pool.tensor_tensor(res[:], tok[:], bcast(row["up_b"]), ALU.add).then_inc(y_biased, 1)
                    root(3 * b + 3)

            @block.scalar
            def _(act):
                def split_hi(s, count):
                    act.wait_ge(raw_in[s], 32 * (count + 1))
                    act.activation(w[s][:, 0, :], w_raw[s], ACT.Copy).then_inc(w_hi[s], 1)

                def turn_hi_from(b, n, src, k):
                    act.activation(xT[0][:, k, :], src, ACT.Copy).then_inc(turn_hi, 1)

                def exp(b, m, mm):
                    act.wait_ge(scored, m + 1 + START)
                    j, qb = (mm % 16) // 4, mm % 4
                    act.activation(prob[j][:, qb, :], prob[j][:, qb, :], ACT.Exp, bias=low[:, mm % 16:mm % 16 + 1], scale=-1.0,
                                   accum_out=total[:, mm % 16:mm % 16 + 1]).then_inc(exped, 1)

                def group(b, g, first, last):
                    n = 4 * b + g
                    for i in range(16):
                        m = 16 * n + i
                        act.wait_ge(probT_full, m + 1 + START)
                        act.wait_ge(pv_done, (64 * b if first and i < 4 else m - 3) + START)
                        act.activation(probT[:, i % 4, :], turned[i % 2][:], ACT.Copy).then_inc(probT_copied, 1)
                        if not (last and i + 5 >= 16):
                            exp(b, m + 5, i + 5)
                        if i in (2, 3) and not last:
                            q_hi(b, g + 1, i - 2)
                        if i == 8 and not last:
                            act.wait_ge(proj_full[1], FILLS * b + FILL_QK + g + 2 + START)
                            split_hi(0, ITEMS[0] * b + W0_QK + g + 2)

                def q_hi(b, g, c):
                    if c == 0:
                        for j in range(HG):
                            act.wait_ge(stack_in[j], 64 * (4 * b + g) + 64)
                    act.wait_ge(proj_read[c], FILLS * b + FILL_QK + g + 1 + START)
                    act.activation(parts[:, 2 * c, :], wide[:, c, :], ACT.Copy).then_inc(qk_hi, 1)

                with act.Fori(0, B) as b:
                    act.wait_ge(ff2_done, NF * b + START)
                    split_hi(0, ITEMS[0] * b + W0_V)
                    split_hi(1, ITEMS[1] * b + W1_V)
                    for k in range(KB):
                        act.wait_ge(turn_full, TURNS * b + k + 1)
                        if k == 0:
                            act.wait_ge(proj_full[0], FILLS * b + START)
                        turn_hi_from(b, k, turns[k % 2][:], k)
                    act.wait_ge(vg_copied, NH * b + START)
                    for t in range(TB):
                        act.wait_ge(proj_full[t % 2], FILLS * b + FILL_V + t // 2 + 1 + START)
                        act.activation(V[:, t, :], proj[t % 2][:], ACT.Copy).then_inc(proj_read[t % 2], 1)
                    act.wait_ge(proj_full[1], FILLS * b + FILL_QK + START)
                    split_hi(0, ITEMS[0] * b + W0_QK)
                    for c in range(2):
                        q_hi(b, 0, c)
                    act.wait_ge(proj_full[1], FILLS * b + FILL_QK + 1 + START)
                    split_hi(0, ITEMS[0] * b + W0_QK + 1)
                    split_hi(1, ITEMS[1] * b + W1_O)
                    for m in range(5):
                        exp(b, 64 * b + m, m)
                    group(b, 0, True, False)
                    with act.Fori(1, G - 1) as g:
                        group(b, g, False, False)
                    group(b, G - 1, False, True)
                    for g in range(G):
                        if g == 0:
                            act.wait_ge(ctx_copied, NH * b + NH + START)
                        act.activation(xT[0][:, g, :], ctxT[:, g, :], ACT.Copy).then_inc(ctx_hi, 1)
                    act.wait_ge(score_full, 64 * (b + 1))
                    for c in range(2):
                        split_hi(*chunk_item(b, 0, c))
                    act.wait_ge(proj_full[1], FILLS * b + FILL_O + 2 + START)
                    split_hi(*chunk_item(b, 0, 2))
                    for k in range(KB):
                        act.wait_ge(turn_wide, KB * b + k + 1)
                        turn_hi_from(b, KB + k, wide[:, k % 2, :], k)

                    def chunk(i, c, last):
                        f, s = 4 * i + c, c % 2
                        act.wait_ge(proj_read[s], FILLS * b + FILL_F + 2 * i + c // 2 + 1 + START)
                        act.wait_ge(g_lo, NF * b + f - 1 + START)
                        act.activation(gel[:, s, :], wide[:, s, :], ACT.Gelu_apprx_sigmoid).then_inc(geled, 1)
                        act.wait_ge(geled, NF * b + f + 1)
                        act.wait_ge(ff2_done, NF * b + f - 1 + START)
                        act.activation(parts[:, 2 * s, :], gel[:, s, :], ACT.Copy).then_inc(g_hi, 1)
                        if not (last and c):
                            act.wait_ge(ff2_done, NF * b + f + START)
                            split_hi(*chunk_item(b, i, c + 3))

                    with act.Fori(0, NF // 4 - 1) as i:
                        for c in range(4):
                            chunk(i, c, False)
                    for c in range(4):
                        chunk(NF // 4 - 1, c, True)
                    for k in range(KB):
                        act.wait_ge(turn_full, TURNS * b + 2 * KB + k + 1)
                        turn_hi_from(b, 2 * KB + k, turns[k % 2][:], k)
                    act.wait_ge(hid_wide, b + 1)
                    act.activation(gel[:, 0, :], wide[:, 0, :], ACT.Gelu).then_inc(hid_ready, 1)
                    act.wait_ge(out_ready, b + 1 + START)
                    act.dma_start(rows_of(out, b), res[:]).then_inc(out_done, 16)
                act.wait_ge(out_done, 16 * B + 16)

            @block.tensor
            def _(t):
                def split_product(dst, stat, mov, ks, start, stop):
                    n, count = 0, 3 * len(ks)
                    for k in ks:
                        for hs, hm in ((0, 0), (0, 1), (1, 0)):
                            mm = t.matmul(dst, stat(hs, k), mov(hm, k), start=start and n == 0, stop=stop and n == count - 1)
                            n += 1
                    return mm

                def turn(b, n, src, k):
                    t.wait_ge(turn_lo, (TURNS * b + n - 1 if n else TURNS * b) + START)
                    for q in range(TB):
                        mm = t.transpose(turns[k % 2][:, q * P:(q + 1) * P], src[:, q, k * P:(k + 1) * P], ident[:])
                    mm.then_inc(turn_full, 1)

                def v_weight(h, k):
                    return w[k // 2][:, h, 512 * (k % 2):512 * (k % 2) + 512]

                def rows_product(b, fill, x_sem, weights_ready):
                    for q in range(TB):
                        t.wait_ge(proj_read[q % 2], FILLS * b + fill + q // 2 + START)
                        split_product(proj[q % 2][:], lambda h, k: xT[h][:, k, q * P:(q + 1) * P], v_weight, range(KB), True, True) \
                            .then_inc(proj_full[q % 2], 1)

                def qk(b, g, c):
                    t.wait_ge(proj_read[c], FILLS * b + FILL_QK + g + START)
                    if c == 0:
                        t.wait_ge(w_hi[0], ITEMS[0] * b + W0_QK + g + 1 + START)
                        t.wait_ge(w_lo[0], ITEMS[0] * b + W0_QK + g + 1 + START)
                    split_product(proj[c][:], lambda h, k: weight(0, h)[:, KB * c + k, :], lambda h, k: xT[h][:, k, :], range(KB), True, True) \
                        .then_inc(proj_full[c], 1)

                def score_block(b, m, mm, g):
                    j, qb = (mm % 16) // 4, mm % 4
                    t.wait_ge(scored, (m - 1 if not isinstance(g, int) or g or mm >= 2 else 64 * b) + START)
                    if qb == 0:
                        t.wait_ge(stack_in[j], 64 * (4 * b + g + 1) + 64)
                    t.matmul(score[mm % 2][:], stack[:, j, 0, qb * P:(qb + 1) * P], stack[:, j, 1, :], start=True, stop=True) \
                        .then_inc(score_full, 1)

                def pv(b, m, mm, vals):
                    j, kb = (mm % 16) // 4, mm % 4
                    t.wait_ge(probT_copied, m + 1 + START)
                    if kb == 0:
                        t.wait_ge(vg_copied, vals[0] + START)
                        t.wait_ge(ctx_copied, vals[1] + START)
                    t.matmul(context[DH * j:DH * (j + 1), :], Vg[:, j, kb, :], probT[:, kb, :], start=kb == 0, stop=kb == TB - 1,
                             tile_position=(0, DH * j)).then_inc(pv_done, 1)

                def group(b, g, first, last):
                    n = 4 * b + g
                    for i in range(16):
                        m = 16 * n + i
                        j, kb = i // 4, i % 4
                        if kb == 0:
                            t.wait_ge(normed, m + 4)
                        t.wait_ge(probT_copied, (64 * b if first and i < 2 else m - 1) + START)
                        for q in range(TB):
                            mm = t.transpose(turned[i % 2][:, q * P:(q + 1) * P], prob[j][:, q, kb * P:(kb + 1) * P], ident[:])
                        mm.then_inc(probT_full, 1)
                        if not (last and i + 6 >= 16):
                            score_block(b, m + 6, i + 6, g + (i + 6) // 16 if not first or i + 6 >= 16 else 0)
                        if not last and i in (0, 1):
                            qk(b, g + 1, i)
                        if not (first and i < 2):
                            head = 4 * n + (i - 2) // 4
                            pv(b, m - 2, (i - 2) % 16, (head + 1, NH * b if first else head - 3))

                with t.Fori(0, B) as b:
                    t.wait_ge(tok_ready, b + 1 + START)
                    for k in range(KB):
                        turn(b, k, tok, k)
                    t.wait_ge(w_lo[0], ITEMS[0] * b + W0_V + 1 + START)
                    t.wait_ge(w_lo[1], ITEMS[1] * b + W1_V + 1 + START)
                    t.wait_ge(turn_lo, TURNS * b + KB + START)
                    rows_product(b, FILL_V, None, None)
                    qk(b, 0, 0)
                    qk(b, 0, 1)
                    for m in range(6):
                        score_block(b, 64 * b + m, m, 0)
                    group(b, 0, True, False)
                    with t.Fori(1, G - 1) as g:
                        group(b, g, False, False)
                    group(b, G - 1, False, True)
                    for mm in (14, 15):
                        pv(b, 64 * b + 48 + mm, mm, None)
                    t.wait_ge(ctx_hi, G * b + G)
                    t.wait_ge(ctx_lo, G * b + G)
                    t.wait_ge(w_lo[0], ITEMS[0] * b + W0_O + 1 + START)
                    t.wait_ge(w_lo[1], ITEMS[1] * b + W1_O + 1 + START)
                    rows_product(b, FILL_O, None, None)
                    t.wait_ge(z2_ready, b + 1)
                    for k in range(KB):
                        turn(b, KB + k, tok, k)
                    t.wait_ge(turn_lo, TURNS * b + 2 * KB + START)

                    def ff1(i, c):
                        s, count = chunk_item(b, i, c)
                        t.wait_ge(w_lo[s], count + 1 + START)
                        t.wait_ge(proj_read[c % 2], FILLS * b + FILL_F + 2 * i + c // 2 + START)
                        split_product(proj[c % 2][:], lambda h, k: weight(s, h)[:, k, :], lambda h, k: xT[h][:, k, :], range(KB), True, True) \
                            .then_inc(proj_full[c % 2], 1)

                    def ff2(i, c, start, stop):
                        s, _ = chunk_item(b, i, c)
                        t.wait_ge(g_lo, NF * b + 4 * i + c + 1 + START)
                        for q in range(TB):
                            mm = split_product(ff_sum[q][:], lambda h, _: parts[:, 2 * (c % 2) + h, q * P:(q + 1) * P],
                                               lambda h, _: w[s][:, h, 512:1024], range(1), start, stop)
                        mm.then_inc(ff2_done, 1)

                    ff1(0, 0)
                    for c in range(1, 4):
                        ff1(0, c)
                        ff2(0, c - 1, c == 1, False)
                    with t.Fori(1, NF // 4) as i:
                        ff1(i, 0)
                        ff2(i - 1, 3, False, False)
                        for c in range(1, 4):
                            ff1(i, c)
                            ff2(i, c - 1, False, False)
                    ff2(NF // 4 - 1, 3, False, True)
                    t.wait_ge(y_ready, b + 1)
                    for k in range(KB):
                        turn(b, 2 * KB + k, tok, k)
                    t.wait_ge(turn_lo, TURNS * b + 3 * KB + START)
                    split_product(proj[0][:], lambda h, k: down[h][:, k, :], lambda h, k: xT[h][:, k, :], range(KB), True, True) \
                        .then_inc(proj_full[0], 1)
                    t.wait_ge(hid_ready, b + 1)
                    t.wait_ge(sel_in, 16 * (b + 1))
                    t.matmul(proj[1][:], sel_T[:], gel[:, 0, :], start=True, stop=True).then_inc(proj_full[1], 1)
                    t.wait_ge(mixed, b + 1 + START)
                    for q in range(TB):
                        t.wait_ge(proj_read[q % 2], FILLS * b + FILL_UP + q // 2 + START)
                        t.matmul(proj[q % 2][:], wide[:, 1, q * P:(q + 1) * P], up_T[:], start=True, stop=True).then_inc(proj_full[q % 2], 1)

            @block.vector
            def _(v):
                STEPS = 46
                v.wait_ge(consts_in, 16 * 12)

                def normalise(link, b, n, src, dst, done):
                    for q in range(TB):
                        link.mark(v.bn_stats(stats[:, q, :], src[:, q, :]))
                    link.sync()
                    link.mark(v.tensor_copy(fence[:, 7:8], stats[:, TB - 1, 0:1]))
                    for q in range(TB):
                        link.mark(v.bn_aggr(agg[:, q, :], stats[:, q, :]))
                    link.sync()
                    v.tensor_scalar(var[:], agg[:, :, 1], EPS, None, ALU.add).then_inc(var_ready, 1)
                    v.wait_ge(rstd_ready, 3 * b + n)
                    for q in range(TB):
                        ins = v.tensor_scalar(dst[:, q, :], src[:, q, :], agg[:, q, 0:1], rstd[:, q:q + 1], ALU.subtract, ALU.mult)
                        if q == TB - 1 and done is not None:
                            ins.then_inc(done, 1)
                        else:
                            link.mark(ins)
                    link.sync()

                def turn_lo_part(b, n, k, src):
                    v.wait_ge(turn_hi, TURNS * b + n + 1)
                    v.tensor_tensor(xT[1][:, k, :], src, xT[0][:, k, :].bitcast(F32), ALU.subtract).then_inc(turn_lo, 1)

                def qk_wide(b, g, c):
                    v.wait_ge(proj_full[c], FILLS * b + FILL_QK + g + 1 + START)
                    bias_col = col["bk" if c else "bq"][:, bass.ds(g, 1)]
                    if c:
                        ins = v.tensor_scalar(wide[:, 1, :], proj[1][:], bias_col, None, ALU.add)
                    else:
                        ins = v.tensor_scalar(wide[:, 0, :], proj[0][:], bias_col, QSCALE, ALU.add, ALU.mult)
                    ins.then_inc(proj_read[c], 1)

                def qk_lo_part(b, g, c):
                    v.wait_ge(qk_hi, 8 * b + 2 * g + c + 1)
                    v.tensor_tensor(parts[:, 2 * c + 1, :], wide[:, c, :], parts[:, 2 * c, :].bitcast(F32), ALU.subtract).then_inc(qk_lo, 1)

                def invert(m, mm):
                    v.wait_ge(exped, m + 1)
                    v.reciprocal(inv[:, mm % 16:mm % 16 + 1], total[:, mm % 16:mm % 16 + 1]).then_inc(inverted, 1)

                def scale_rows(m, mm):
                    j, qb = (mm % 16) // 4, mm % 4
                    v.wait_ge(inverted, m + 1)
                    v.tensor_scalar(prob[j][:, qb, :], prob[j][:, qb, :], inv[:, mm % 16:mm % 16 + 1], None, ALU.mult).then_inc(normed, 1)

                def await_scores(n, i):
                    v.wait_ge(score_full, 16 * n + i + 1)
                    if i % 2 == 0:
                        v.wait_ge(bias_masked, 8 * n + i // 2 + 1 + START)

                def scores_at(i):
                    j, qb = (i % 16) // 4, i % 4
                    v.tensor_tensor_reduce(prob[j][:, qb, :], score[i % 2][:], prob[j][:, qb, :], -1.0, MIN_START, ALU.add, ALU.min,
                                           low[:, i % 16:i % 16 + 1]).then_inc(scored, 1)

                def copy_v(b, g, j, pv_count):
                    v.wait_ge(pv_done, pv_count + START)
                    v.tensor_copy(Vg[:, j, :, :], V[:, :, bass.ds(P * g + DH * j, DH)]).then_inc(vg_copied, 1)

                def take_context(b, g, j):
                    v.wait_ge(pv_done, 64 * b + 16 * g + 4 * j + 4 + START)
                    quad = slice(DH * j, DH * (j + 1))
                    v.tensor_scalar(ctxT[quad, bass.ds(g, 1), :].rearrange("p o s -> p (o s)"), context[quad, :], col["bv"][quad, bass.ds(g, 1)], None, ALU.add) \
                        .then_inc(ctx_copied, 1)

                def group(b, g, first, last):
                    n = 4 * b + g
                    for i in range(16):
                        m = 16 * n + i
                        if not (last and i + 6 >= 16):
                            await_scores(n, i + 6)
                        if not (last and i + 4 >= 16):
                            invert(m + 4, i + 4)
                        if not (last and i + 6 >= 16):
                            scores_at(i + 6)
                        if not (last and i + 4 >= 16):
                            scale_rows(m + 4, i + 4)
                        if i % 4 == 2 and not (first and i == 2):
                            take_context(b, g if i > 2 else g - 1, (i - 6) // 4 % 4)
                        if i == 3:
                            copy_v(b, g, 3, 16 * n)
                        elif i % 4 == 3 and not last:
                            copy_v(b, g + 1, i // 4 - 1, 16 * n + i - 3)
                        if not last and i in (2, 3):
                            qk_wide(b, g + 1, i - 2)
                        if not last and i in (4, 5):
                            qk_lo_part(b, g + 1, i - 4)

                with v.Fori(0, B) as b:
                    link = Link(v, dve_step, STEPS * b)
                    v.wait_ge(mask_in, 16 * (b + 1))
                    v.wait_ge(bias_masked, 32 * b + START)
                    v.tensor_scalar(mask_add[:], mask8[:], MASKED, None, ALU.mult).then_inc(mask_ready, 1)
                    v.wait_ge(out_ready, b + START)
                    link(v.tensor_copy(cur[:], scal[:, bass.ds(b, 1), :].rearrange("p o c -> p (o c)")))
                    v.wait_ge(x_in, 16 * (b + 1))
                    normalise(link, b, 1, tok_in, tok_in, None)
                    v.wait_ge(ada_in, 32 * (b + 1))
                    v.tensor_tensor(tok[:], tok_in[:], bcast(scale_row), ALU.mult).then_inc(x_used, 1)
                    v.wait_ge(x_used, b + 1 + START)
                    v.tensor_tensor(tok[:], tok[:], bcast(shift_row), ALU.add).then_inc(tok_ready, 1)
                    for k in range(KB):
                        turn_lo_part(b, k, k, turns[k % 2][:])
                    for c in range(2):
                        qk_wide(b, 0, c)
                    for c in range(2):
                        qk_lo_part(b, 0, c)
                    v.wait_ge(proj_read[0], FILLS * b + FILL_V + 2 + START)
                    v.wait_ge(proj_read[1], FILLS * b + FILL_V + 2 + START)
                    for j in range(3):
                        copy_v(b, 0, j, 64 * b)
                    for i in range(6):
                        await_scores(4 * b, i)
                        v.tensor_copy(fence[:, i:i + 1], cur[:, 0:1])
                        scores_at(i)
                    for i in range(4):
                        invert(64 * b + i, i)
                    for i in range(4):
                        scale_rows(64 * b + i, i)
                    group(b, 0, True, False)
                    with v.Fori(1, G - 1) as g:
                        group(b, g, False, False)
                    group(b, G - 1, False, True)
                    take_context(b, G - 1, 3)
                    for g in range(G):
                        v.wait_ge(ctx_hi, G * b + g + 1)
                        v.tensor_tensor(xT[1][:, g, :], ctxT[:, g, :], xT[0][:, g, :].bitcast(F32), ALU.subtract).then_inc(ctx_lo, 1)
                    v.wait_ge(out_done, 16 * b + 16)
                    v.wait_ge(tok_biased, b + 1)
                    for q in range(TB):
                        v.wait_ge(proj_full[q % 2], FILLS * b + FILL_O + q // 2 + 1 + START)
                        v.tensor_tensor(res[:, q, :], proj[q % 2][:], tok[:, q, :], ALU.add).then_inc(proj_read[q % 2], 1)
                    for s in range(2):
                        v.wait_ge(proj_read[s], FILLS * b + FILL_O + 2 + START)
                    normalise(link, b, 2, res, tok, z2_ready)
                    for k in range(KB):
                        v.wait_ge(turn_full, TURNS * b + KB + k + 1)
                        v.tensor_scalar(wide[:, k % 2, :], turns[k % 2][:], col["g2"][:, k:k + 1], col["beta2"][:, k:k + 1], ALU.mult, ALU.add) \
                            .then_inc(turn_wide, 1)
                        v.wait_ge(turn_wide, KB * b + k + 1)
                        turn_lo_part(b, KB + k, k, wide[:, k % 2, :])

                    def widen(i, s):
                        v.wait_ge(proj_full[s], FILLS * b + FILL_F + i + 1 + START)
                        v.tensor_scalar(wide[:, s, :], proj[s][:], col["b1"][:, bass.ds(2 * i + s, 1)], None, ALU.add).then_inc(proj_read[s], 1)

                    def gelu_lo(i, s):
                        v.wait_ge(g_hi, NF * b + 2 * i + s + 1)
                        v.tensor_tensor(parts[:, 2 * s + 1, :], gel[:, s, :], parts[:, 2 * s, :].bitcast(F32), ALU.subtract).then_inc(g_lo, 1)

                    with v.Fori(0, NF // 2) as i:
                        for s in range(2):
                            widen(i, s)
                            gelu_lo(i, s)
                    v.wait_ge(ff2_done, NF * b + NF + START)
                    v.wait_ge(res_biased, b + 1)
                    for q in range(TB):
                        ins = v.tensor_tensor(tok[:, q, :], ff_sum[q][:], res[:, q, :], ALU.add)
                    ins.then_inc(y_ready, 1)
                    for k in range(KB):
                        turn_lo_part(b, 2 * KB + k, k, turns[k % 2][:])
                    v.wait_ge(proj_full[0], FILLS * b + FILL_L2 + 1 + START)
                    v.tensor_scalar(wide[:, 0, :], proj[0][:], col["down_b"][:, 0:1], None, ALU.add).then_inc(proj_read[0], 1)
                    v.wait_ge(proj_read[0], FILLS * b + FILL_L2 + 1 + START)
                    v.sem_inc(hid_wide, 1)
                    v.wait_ge(hid_ready, b + 1)
                    v.wait_ge(proj_full[1], FILLS * b + FILL_L2 + 1 + START)
                    v.tensor_scalar(wide[:, 1, :], proj[1][:], cur[:, 0:1], cur[:, 2:3], ALU.mult, ALU.add).then_inc(proj_read[1], 1)
                    v.wait_ge(proj_read[1], FILLS * b + FILL_L2 + 1 + START)
                    v.scalar_tensor_tensor(wide[:, 1, :], gel[:, 0, :], cur[:, 1:2], wide[:, 1, :], ALU.mult, ALU.add).then_inc(mixed, 1)
                    v.wait_ge(y_biased, b + 1)
                    for q in range(TB):
                        v.wait_ge(proj_full[q % 2], FILLS * b + FILL_UP + q // 2 + 1 + START)
                        v.tensor_tensor(res[:, q, :], proj[q % 2][:], res[:, q, :], ALU.add).then_inc(proj_read[q % 2], 1)
                    for s in range(2):
                        v.wait_ge(proj_read[s], FILLS * b + FILL_UP + 2 + START)
                    normalise(link, b, 3, res, res, None)
                    link(v.tensor_tensor(res[:], res[:], bcast(row["gamma"]), ALU.mult))
                    link(v.tensor_tensor(res[:], res[:], bcast(row["beta"]), ALU.add))
                    quads = res[:].rearrange("p t (q c) -> p (t q) c", c=4)
                    sines = tok[:].rearrange("p t (q c) -> p (t q) c", c=4)
                    for h in range(2):
                        link.mark(v.tensor_scalar(sines[:, :, 2 * h:2 * h + 2], quads[:, :, 2 * h:2 * h + 2], cur[:, 4 + 2 * h:5 + 2 * h], None, ALU.mult))
                    link.sync()
                    for h in range(2):
                        for c in range(2):
                            a, o = 2 * h + c, 2 * h + 1 - c
                            ins = v.scalar_tensor_tensor(quads[:, :, a], quads[:, :, a], cur[:, 3 + 2 * h:4 + 2 * h], sines[:, :, o],
                                                         ALU.mult, ALU.add if c == 0 else ALU.subtract)
                            if a < 3:
                                link.mark(ins)
                    ins.then_inc(out_ready, 1)
                    link.sync()
                    assert link.n == STEPS, link.n


def program(nc, x, dt, step_id, bias, domain, theta, phi, mask, A_grid, B_grid, W_ada, b_ada, Wq, bq, Wk, bk, Wv, bv,
            Wo, bo, W1, b1, W2, b2, g2, beta2, down_W, down_b, up_W, up_b, expert_W, expert_b, emb, gamma, beta,
            freqs, lane, identity, out):
    x1 = nc.dram_tensor("x1", [B, S, D], F32).ap()
    ada_rows = nc.dram_tensor("ada_rows", [B, 2 * D], F32).ap()
    sel_rows = nc.dram_tensor("sel_rows", [B, A * A], F32).ap()
    sel_turned = nc.dram_tensor("sel_turned", [B, A, A], F32).ap()
    field_step(nc, x, A_grid, B_grid, dt, x1)
    field_edges(nc, x, A_grid, B_grid, dt, x1)
    with ExitStack() as ctx:
        sb = lambda name, shape, t=F32: ctx.enter_context(nc.sbuf_tensor(name, shape, t))
        keep = {"ident": sb("ident", [P, P]), "scal": sb("scal", [P, B, 8]), "up_T": sb("up_T", [A, D]),
                "down_hi": sb("down_hi", [P, KB, A], F32R), "down_lo": sb("down_lo", [P, KB, A], F32R)}
        for name in ("ident_in", "prep_sin", "prep_emb", "prep_ada", "prep_turn"):
            keep[name] = ctx.enter_context(nc.semaphore(name))
        with nc.Block() as block:

            @block.sync
            def _(sp):
                sp.dma_start(keep["ident"][:], identity).then_inc(keep["ident_in"], 16)
                sp.wait_ge(keep["ident_in"], 16)

            @block.gpsimd
            def _(pool):
                pool.memset(keep["scal"][:], 0.0)

        prepare(nc, keep, step_id, domain, theta, phi, W_ada, b_ada, down_W, up_W, expert_W, expert_b, emb,
                freqs, lane, ada_rows, sel_rows, sel_turned)
        layers(nc, keep, x1, mask, bias, ada_rows, sel_turned, Wq, bq, Wk, bk, Wv, bv, Wo, bo, W1, b1, W2, b2, g2, beta2,
               down_b, up_b, gamma, beta, out)


_INS = ["x", "condB_dt", "itok_B_34_63", "fside_Bx16xSxS_0", "itok_B_0_15", "condB_theta", "condB_phi", "mask_Bx1xSxS_bk0",
        "L0_cond_A_grid", "L0_cond_B_grid", "L1_cond_W_ada", "L1_cond_b_ada", "L1_cond_Wq", "L1_cond_bq", "L1_cond_Wk",
        "L1_cond_bk", "L1_cond_Wv", "L1_cond_bv", "L1_cond_Wo", "L1_cond_bo", "L1_cond_W1", "L1_cond_b1", "L1_cond_W2",
        "L1_cond_b2", "L1_cond_g2", "L1_cond_beta2", "L2_cond_down_W", "L2_cond_down_b", "L2_cond_up_W", "L2_cond_up_b",
        "L2_cond_expert_W", "L2_cond_expert_b", "L2_cond_domain_emb", "L2_cond_ln_gamma", "L2_cond_ln_beta"]


def constants():
    half = D // 2
    step = np.float32(-np.log(10000.0) / (half - 1))
    return {"freqs": np.exp(np.arange(half, dtype=np.float32) * step).astype(np.float32),
            "lane": np.arange(P, dtype=np.float32).reshape(P, 1), "identity": np.eye(P, dtype=np.float32)}


def kernel(**inputs):
    import concourse.bacc as bacc
    from concourse.bass_utils import run_bass_kernel_spmd

    nc = bacc.Bacc("TRN2", target_bir_lowering=False, num_devices=1)
    arrays, args = {}, []
    for name in _INS:
        a = np.ascontiguousarray(inputs[name])
        arrays[f"in_{name}"] = a
    for name, a in constants().items():
        arrays[f"in_{name}"] = a
    for name, a in arrays.items():
        args.append(nc.dram_tensor(name, a.shape, mybir.dt.from_np(a.dtype), kind="ExternalInput").ap())
    args.append(nc.dram_tensor("out", (B, S, D), F32, kind="ExternalOutput").ap())
    program(nc, *args)
    r = run_bass_kernel_spmd(nc, [arrays], core_ids=[0])
    return r.results[0]["out"]
```

```python
from contextlib import ExitStack

import numpy as np

import concourse.bass as bass
from concourse import mybir

F32 = mybir.dt.float32
F32R = mybir.dt.float32r
BF16 = mybir.dt.bfloat16
U8 = mybir.dt.uint8
I32 = mybir.dt.int32
ALU = mybir.AluOpType
ACT = mybir.ActivationFunctionType

P = 128
B, S, D = 16, 512, 512
NH, DH = 16, 32
FF = 2048
A, E = 128, 16
TB = S // P
KB = D // P
G = NH * DH // P
HG = P // DH
NF = FF // P
EPS = 1e-5
QSCALE = float(DH) ** -0.5
MASKED = -3.0e38
MIN_START = 1.0e30
MAGIC = 12582912.0
PI = float(np.pi)
TWO_PI = (6.28125, 0.0019340515136718750, 1.2556659146713e-06)

FILLS = 19
FILL_QK0, FILL_V, FILL_QK, FILL_O, FILL_F, FILL_L2, FILL_UP = 0, 1, 2, 6, 8, 16, 17
ITEMS = (9, 6, 5, 4)
W0_V, W0_QK, W0_O = 0, 0, 4
W1_V, W1_O = 0, 1
W2_QK0 = 0
F_ITEM = (5, 2, 1, 0)
S_LEAD, EXP_LEAD, NORM_LEAD = 7, 6, 5
START = 4
ROOTS = 12
TURNS = 12


class Link:

    def __init__(self, eng, sem, base=0):
        self.eng, self.sem, self.base, self.n = eng, sem, base, 0

    def mark(self, ins):
        ins.then_inc(self.sem, 1)
        self.n += 1

    def sync(self):
        self.eng.wait_ge(self.sem, self.base + self.n)

    def __call__(self, ins):
        self.mark(ins)
        self.sync()


def pair(ap, c):
    n = ap.shape[2]
    return ap[:, :, c:n - c:n - 1 - 2 * c]


def end_slope(link, v, tmp, w):
    link(v.tensor_scalar(tmp, pair(w, 0), -3.0, None, ALU.mult))
    link(v.scalar_tensor_tensor(tmp, pair(w, 1), 4.0, tmp, ALU.mult, ALU.add))
    link(v.tensor_tensor(tmp, tmp, pair(w, 2), ALU.subtract))


def slope_y(link, v, out, w, tmp):
    v.tensor_tensor(out[:, :, 1:D - 1], w[:, :, 2:D], w[:, :, 0:D - 2], ALU.subtract)
    end_slope(link, v, tmp, w)
    v.tensor_copy(out[:, :, 0:1], tmp[:, :, 0:1])
    link(v.tensor_scalar(out[:, :, D - 1:D], tmp[:, :, 1:2], -1.0, None, ALU.mult))


def sub_slope_y(link, v, s, w, tmp):
    link(v.tensor_tensor(s[:, :, 1:D - 1], s[:, :, 1:D - 1], w[:, :, 2:D], ALU.subtract))
    link(v.tensor_tensor(s[:, :, 1:D - 1], s[:, :, 1:D - 1], w[:, :, 0:D - 2], ALU.add))
    end_slope(link, v, tmp, w)
    link(v.tensor_tensor(s[:, :, 0:1], s[:, :, 0:1], tmp[:, :, 0:1], ALU.subtract))
    link(v.tensor_tensor(s[:, :, D - 1:D], s[:, :, D - 1:D], tmp[:, :, 1:2], ALU.add))


def curve_y(link, v, s, w):
    inner = s[:, :, 1:D - 1]
    link(v.scalar_tensor_tensor(inner, w[:, :, 1:D - 1], -2.0, w[:, :, 0:D - 2], ALU.mult, ALU.add))
    link.mark(v.tensor_tensor(inner, inner, w[:, :, 2:D], ALU.add))
    link(v.tensor_scalar(pair(s, 0), pair(w, 0), 2.0, None, ALU.mult))
    for c, k in enumerate((-5.0, 4.0, -1.0), 1):
        link(v.scalar_tensor_tensor(pair(s, 0), pair(w, c), k, pair(s, 0), ALU.mult, ALU.add))


def field_step(nc, x, A_grid, B_grid, dt, row_slope, row_curve, x1):
    with ExitStack() as ctx:
        sb = lambda name, shape, t=F32: ctx.enter_context(nc.sbuf_tensor(name, shape, t))
        sem = lambda name: ctx.enter_context(nc.semaphore(name))
        grids = {n: sb(f"grid_{n}", [P, TB, D]) for n in ("b2", "a0", "b0", "b1", "a1")}
        product = {n: [sb(f"{n}f{u}", [P, TB, D]) for u in range(2)] for n in grids}
        field, flow, total = ([sb(f"{n}{u}", [P, TB, D]) for u in range(2)] for n in ("field", "flow", "total"))
        slope, curve = sb("row_slope_sb", [P, TB, S]), sb("row_curve_sb", [P, TB, S])
        half_dt, tmp = sb("half_dt", [P, B]), sb("tmp", [P, TB, 2])
        row_sum = [ctx.enter_context(nc.psum_tensor(f"row_sum{u}", [P, TB, D], F32)) for u in range(2)]
        consts_in, bands_in, dve_step = sem("consts_in"), sem("bands_in"), sem("dve_step")
        grid_in = {n: sem(f"grid_{n}_in") for n in grids}
        field_in = [sem(f"field_in{u}") for u in range(2)]
        products = sem("products")
        flowed = sem("flowed")
        row_summed = sem("row_summed")
        row_taken = sem("row_taken")
        stepped = [sem(f"stepped{u}") for u in range(2)]
        clipped = [sem(f"clipped{u}") for u in range(2)]
        stored = [sem(f"stored{u}") for u in range(2)]
        STEPS = 17

        with nc.Block() as block:

            @block.sync
            def _(sp):
                rows = lambda t: t.rearrange("(t p) c -> p t c", p=P)
                load_field = lambda n, u: sp.dma_start(field[u][:], rows(x[bass.ds(n, 1)].rearrange("o s c -> (o s) c"))).then_inc(field_in[u], 16)
                load_field(0, 0)
                for name, src in zip(grids, (B_grid[2], A_grid[0], B_grid[0], B_grid[1], A_grid[1])):
                    sp.dma_start(grids[name][:], rows(src)).then_inc(grid_in[name], 16)
                load_field(1, 1)
                sp.dma_start(half_dt[:], dt.partition_broadcast(P)).then_inc(consts_in, 16)
                sp.dma_start(curve[:], rows(row_curve)).then_inc(bands_in, 16)
                sp.dma_start(slope[:], rows(row_slope)).then_inc(bands_in, 16)
                with sp.Fori(1, B // 2) as i:
                    for u in range(2):
                        sp.wait_ge(stepped[u], i + 1)
                        load_field(2 * i + u, u)

            @block.gpsimd
            def _(pool):
                with pool.Fori(0, B // 2) as i:
                    for u in range(2):
                        pool.wait_ge(stepped[u], i + 1)
                        pool.wait_ge(field_in[u], 16 * (i + 1))
                        for name in grids:
                            pool.wait_ge(grid_in[name], 16)
                            pool.tensor_tensor(product[name][u][:], grids[name][:], field[u][:], ALU.mult).then_inc(products, 1)

            @block.tensor
            def _(t):
                t.wait_ge(bands_in, 32)
                with t.Fori(0, B // 2) as i:
                    for u in range(2):
                        n = 2 * i + u
                        t.wait_ge(row_taken, n + 1)
                        t.wait_ge(products, 5 * n + 3)
                        for q in range(TB):
                            near = [k for k in range(TB) if abs(k - q) <= 1]
                            for k in near:
                                t.matmul(row_sum[u][:, q, :], curve[:, k, q * P:(q + 1) * P], product["b0"][u][:, k, :], start=k == near[0], stop=False)
                        t.wait_ge(flowed, n + 1)
                        for q in range(TB):
                            near = [k for k in range(TB) if abs(k - q) <= 1]
                            for k in near:
                                mm = t.matmul(row_sum[u][:, q, :], slope[:, k, q * P:(q + 1) * P], flow[u][:, k, :], start=False, stop=k == near[-1])
                        mm.then_inc(row_summed, 1)

            @block.vector
            def _(v):
                v.sem_inc(row_taken, 2)
                for u in range(2):
                    v.sem_inc(stepped[u], 1)
                    v.sem_inc(stored[u], 16)
                v.wait_ge(consts_in, 16)
                link = Link(v, dve_step)
                link(v.tensor_scalar(half_dt[:], half_dt[:], 0.5, None, ALU.mult))
                with v.Fori(0, B // 2) as i:
                    for u in range(2):
                        n = 2 * i + u
                        link = Link(v, dve_step, STEPS * n + 1)
                        f, s = field[u][:], total[u][:]
                        b2f, a0f, b1f, a1f = (product[name][u][:] for name in ("b2", "a0", "b1", "a1"))
                        v.wait_ge(products, 5 * n + 1)
                        slope_y(link, v, flow[u][:], b2f, tmp[:])
                        v.wait_ge(products, 5 * n + 2)
                        v.scalar_tensor_tensor(flow[u][:], flow[u][:], 0.5, a0f, ALU.mult, ALU.subtract).then_inc(flowed, 1)
                        v.wait_ge(stored[u], 16 * i + 16)
                        v.wait_ge(products, 5 * n + 4)
                        curve_y(link, v, s, b1f)
                        v.wait_ge(products, 5 * n + 5)
                        sub_slope_y(link, v, s, a1f, tmp[:])
                        v.wait_ge(row_summed, n + 1)
                        v.tensor_tensor(s, s, row_sum[u][:], ALU.add).then_inc(row_taken, 1)
                        v.wait_ge(row_taken, n + 3)
                        v.scalar_tensor_tensor(s, s, half_dt[:, bass.ds(n, 1)], f, ALU.mult, ALU.add).then_inc(stepped[u], 1)
                        assert link.n == STEPS, link.n

            @block.scalar
            def _(act):
                with act.Fori(0, B // 2) as i:
                    for u in range(2):
                        act.wait_ge(stepped[u], i + 2)
                        act.activation(total[u][:], total[u][:], ACT.Relu).then_inc(clipped[u], 1)
                        act.wait_ge(clipped[u], i + 1)
                        act.dma_start(x1[bass.ds(2 * i + u, 1)].rearrange("o (t p) c -> p (o t) c", p=P), total[u][:]).then_inc(stored[u], 16)
                for u in range(2):
                    act.wait_ge(stored[u], 16 * (B // 2) + 16)


def reduce_angle(link, v, r, k):
    link(v.tensor_scalar(k, r, 1.0 / (2.0 * PI), None, ALU.mult))
    link(v.tensor_scalar(k, k, MAGIC, None, ALU.add))
    link(v.tensor_scalar(k, k, -MAGIC, None, ALU.add))
    for c in TWO_PI:
        link(v.scalar_tensor_tensor(r, k, -c, r, ALU.mult, ALU.add))


def quarter_turn(link, v, out, r, k):
    link(v.tensor_scalar(k, r, PI / 2, -2.0 * PI, ALU.is_gt, ALU.mult))
    link(v.tensor_tensor(out, r, k, ALU.add))
    link(v.tensor_scalar(out, out, PI / 2, None, ALU.add))
    for t in (out, r):
        link(v.tensor_scalar(t, t, 3.1415925, -3.1415925, ALU.min, ALU.max))


def prepare(nc, keep, step_id, domain, theta, phi, W_ada, b_ada, down_W, up_W, expert_W, expert_b, emb,
            freqs, lane, identity, ada_rows, sel_rows, sel_turned):
    ident = keep["ident"]
    with ExitStack() as ctx:
        sb = lambda name, shape, t=F32: ctx.enter_context(nc.sbuf_tensor(name, shape, t))
        sem = lambda name: ctx.enter_context(nc.semaphore(name))
        bank = [ctx.enter_context(nc.psum_tensor(f"prep_bank{i}", [P, 512], F32)) for i in range(8)]
        picked = bank[4:8]
        tt = sb("time", [B, 4])
        ti = sb("time_i", [B, 1], I32)
        fr = sb("freqs_sb", [B, D // 2])
        ang, kk, emb_rows = sb("ang", [B, D]), sb("kk", [B, D]), sb("emb_rows", [B, D])
        embT = sb("embT", [P, KB, B])
        w_ada = sb("w_ada", [P, KB, 2 * D])
        bada = sb("bada", [B, 2 * D])
        ada = sb("ada", [B, 2 * D])
        idi, idf = sb("idi", [P, B], I32), sb("idf", [P, B])
        hot, ge, lt = sb("hot", [P, B]), sb("ge", [P, B]), sb("lt", [P, B])
        ln = sb("lane_sb", [P, 1])
        ew = sb("ew", [E, A * A])
        ewo = sb("ewo", [B, A * A])
        vecs = sb("vecs", [E, 2, A])
        bs = sb("bs", [A, 2, B])
        turn = sb("turn", [P, 2, B])
        turn2, tk = sb("turn2", [P, 2, B]), sb("tk", [P, 2, B])
        dw = sb("dw", [A, D])
        uw = sb("uw", [P, KB, A])
        selb = sb("selb", [P, B, A])
        selt = sb("selt", [P, B, A])
        loads, ew_in, steps, pe, at, st, sel_in = (sem(f"prep_{n}") for n in ("loads", "ew_in", "steps", "pe", "at", "st", "sel_in"))
        scal = keep["scal"]
        PICKS = A * A // 512

        with nc.Block() as block:

            @block.sync
            def _(sp):
                sp.dma_start(ident[:], identity).then_inc(keep["ident_in"], 16)
                for dst, src in ((idi[:], domain.partition_broadcast(P)), (ln[:], lane), (ew[:], expert_W.rearrange("e o a -> e (o a)"))):
                    sp.dma_start(dst, src).then_inc(ew_in, 16)
                for dst, src in (
                    (ti[:], step_id.rearrange("(b o) -> b o", o=1)),
                    (fr[:], freqs.partition_broadcast(B)),
                    (w_ada[:], W_ada.rearrange("(k p) n -> p k n", p=P)),
                    (bada[:], b_ada.partition_broadcast(B)),
                    (vecs[:, 0, :], expert_b), (vecs[:, 1, :], emb),
                    (turn[:, 0, :], theta.partition_broadcast(P)), (turn[:, 1, :], phi.partition_broadcast(P)),
                    (dw[:], down_W), (uw[:], up_W.rearrange("(k p) a -> p k a", p=P)),
                ):
                    sp.dma_start(dst, src).then_inc(loads, 16)
                sp.wait_ge(at, PICKS)
                sp.dma_start(sel_rows, ewo[:]).then_inc(st, 16)
                sp.wait_ge(st, 16)
                sp.dma_start(selb[:], sel_rows.rearrange("b (o a) -> o b a", a=A)).then_inc(sel_in, 16)
                sp.wait_ge(at, PICKS + 4)
                sp.dma_start(sel_turned.rearrange("b a o -> a b o"), selt[:]).then_inc(st, 16)
                sp.wait_ge(steps, 1000)
                sp.dma_start(ada_rows, ada[:]).then_inc(st, 16)
                sp.wait_ge(st, 16 * 3)

            @block.vector
            def _(v):
                link = Link(v, steps)
                link(v.memset(scal[:], 0.0))
                v.wait_ge(ew_in, 16 * 3)
                link(v.tensor_scalar(idf[:], idi[:], 1.0, None, ALU.mult))
                link(v.tensor_scalar(ge[:], idf[:], 0.0, None, ALU.is_ge))
                link(v.tensor_scalar(lt[:], idf[:], float(E), None, ALU.is_lt))
                link(v.tensor_tensor(ge[:], ge[:], lt[:], ALU.mult))
                link(v.tensor_scalar(idf[:], idf[:], 0.0, float(E - 1), ALU.max, ALU.min))
                link(v.tensor_scalar(hot[:], idf[:], ln[:, 0:1], None, ALU.is_equal))
                v.sem_inc(pe, 100)
                v.wait_ge(loads, 16 * 10)
                link(v.tensor_scalar(tt[:, 0:1], ti[:], 1.0, None, ALU.mult))
                link(v.tensor_scalar(tt[:, 1:2], tt[:, 0:1], 0.01, None, ALU.mult))
                link(v.tensor_scalar(tt[:, 1:2], tt[:, 1:2], 4000.0, None, ALU.mult))
                link(v.tensor_scalar(ang[:, 0:D // 2], fr[:], tt[:, 1:2], None, ALU.mult))
                reduce_angle(link, v, ang[:, 0:D // 2], kk[:, 0:D // 2])
                quarter_turn(link, v, ang[:, D // 2:D], ang[:, 0:D // 2], kk[:, 0:D // 2])
                reduce_angle(link, v, turn[:], tk[:])
                quarter_turn(link, v, turn2[:], turn[:], tk[:])
                link(v.tensor_copy(scal[:, :, 0], ge[:]))
                link(v.tensor_scalar(scal[:, :, 1], ge[:], -1.0, 1.0, ALU.mult, ALU.add))
                v.wait_ge(keep["prep_sin"], 1)
                link(v.scalar_tensor_tensor(emb_rows[:], kk[:], 1.0, ang[:], ALU.add, ALU.mult))
                v.sem_inc(keep["prep_emb"], 1)
                v.wait_ge(keep["prep_ada"], 1)
                link(v.tensor_copy(embT[:], bank[3][:, 0:KB * B].rearrange("p (k b) -> p k b", b=B)))
                v.sem_inc(keep["prep_emb"], 1)
                v.wait_ge(keep["prep_ada"], 3)
                for h in range(2):
                    link(v.scalar_tensor_tensor(ada[:, h * D:h * D + D], bank[2 + h][0:B, :], 0.5, bada[:, h * D:h * D + D], ALU.mult, ALU.add))
                link(v.tensor_scalar(ada[:, 0:D], ada[:, 0:D], 1.0, None, ALU.add))
                v.sem_inc(keep["prep_emb"], 1)
                v.wait_ge(keep["prep_ada"], 4)
                link(v.tensor_copy(bs[:], bank[2][:, 0:2 * B].rearrange("p (v b) -> p v b", v=2)))
                link(v.tensor_tensor(bs[:, 0, :], bs[:, 0, :], scal[:, :, 0], ALU.mult))
                link(v.tensor_tensor(scal[:, :, 2], bs[:, 0, :], bs[:, 1, :], ALU.add))
                v.sem_inc(keep["prep_emb"], 1)
                v.wait_ge(keep["prep_ada"], 5)
                link(v.tensor_copy(keep["down_hi"][:], bank[3][:].rearrange("p (k a) -> p k a", a=A)))
                link(v.tensor_tensor(keep["down_lo"][:], bank[3][:].rearrange("p (k a) -> p k a", a=A), keep["down_hi"][:], ALU.subtract))
                v.sem_inc(keep["prep_emb"], 1)
                v.wait_ge(keep["prep_ada"], 6)
                v.tensor_copy(keep["up_T"][:], bank[2][:]).then_inc(steps, 1000 - link.n)

            @block.scalar
            def _(act):
                act.wait_ge(steps, 1 + 6 + 3 + 1 + 6 + 5 + 6 + 5)
                act.activation(ang[:], ang[:], ACT.Sin)
                act.activation(scal[:, :, 4], turn[:, 0, :], ACT.Sin)
                act.activation(scal[:, :, 6], turn[:, 1, :], ACT.Sin)
                act.activation(scal[:, :, 3], turn2[:, 0, :], ACT.Sin)
                act.activation(scal[:, :, 5], turn2[:, 1, :], ACT.Sin).then_inc(keep["prep_turn"], 1)
                act.wait_ge(keep["prep_turn"], 1)
                act.activation(kk[:], ang[:], ACT.Tanh, scale=0.5).then_inc(keep["prep_sin"], 1)
                for m in range(PICKS):
                    act.wait_ge(pe, 100 + m + 1)
                    act.activation(ewo[:, m * 512:(m + 1) * 512], picked[m % 4][0:B, :], ACT.Copy).then_inc(at, 1)
                for q in range(4):
                    act.wait_ge(pe, 100 + PICKS + q + 1)
                    act.activation(selt[:, 4 * q:4 * q + 4, :], bank[q % 2][:].rearrange("p (b a) -> p b a", a=A), ACT.Copy).then_inc(at, 1)

            @block.tensor
            def _(t):
                t.wait_ge(ew_in, 16 * 3)
                t.wait_ge(pe, 100)
                for m in range(PICKS):
                    if m >= 4:
                        t.wait_ge(at, m - 3)
                    t.matmul(picked[m % 4][0:B, :], hot[0:E, :], ew[:, m * 512:(m + 1) * 512], start=True, stop=True).then_inc(pe, 1)
                t.wait_ge(loads, 16 * 10)
                t.wait_ge(keep["ident_in"], 16)
                t.wait_ge(keep["prep_emb"], 1)
                for k in range(KB):
                    mm = t.transpose(bank[3][:, k * B:k * B + B], emb_rows[:, k * P:k * P + P], ident[0:B, 0:B])
                mm.then_inc(keep["prep_ada"], 1)
                t.wait_ge(keep["prep_emb"], 2)
                for h in range(2):
                    for k in range(KB):
                        mm = t.matmul(bank[2 + h][0:B, :], embT[:, k, :], w_ada[:, k, h * D:h * D + D], start=k == 0, stop=k == KB - 1)
                    mm.then_inc(keep["prep_ada"], 1)
                t.wait_ge(keep["prep_emb"], 3)
                for w in range(2):
                    mm = t.matmul(bank[2][:, w * B:w * B + B], vecs[:, w, :], hot[0:E, :], start=True, stop=True)
                mm.then_inc(keep["prep_ada"], 1)
                t.wait_ge(keep["prep_emb"], 4)
                for k in range(KB):
                    mm = t.transpose(bank[3][:, k * A:k * A + A], dw[:, k * P:k * P + P], ident[:])
                mm.then_inc(keep["prep_ada"], 1)
                t.wait_ge(keep["prep_emb"], 5)
                for k in range(KB):
                    mm = t.transpose(bank[2][:, k * P:k * P + P], uw[:, k, :], ident[:])
                mm.then_inc(keep["prep_ada"], 1)
                t.wait_ge(sel_in, 16)
                for q in range(4):
                    t.wait_ge(at, PICKS + q - 1)
                    for j in range(4):
                        mm = t.transpose(bank[q % 2][:, j * A:j * A + A], selb[:, 4 * q + j, :], ident[:])
                    mm.then_inc(pe, 1)


def layers(nc, keep, x1, mask, bias, ada_rows, sel_turned, Wq, bq, Wk, bk, Wv, bv, Wo, bo, W1, b1, W2, b2, g2, beta2,
           down_b, up_b, gamma, beta, out):
    ident, scal, down, up_T = keep["ident"], keep["scal"], (keep["down_hi"], keep["down_lo"]), keep["up_T"]
    with ExitStack() as ctx:
        sb = lambda name, shape, t=F32: ctx.enter_context(nc.sbuf_tensor(name, shape, t))
        sem = lambda name: ctx.enter_context(nc.semaphore(name))

        bank = [ctx.enter_context(nc.psum_tensor(f"bank{i}", [P, 512], F32)) for i in range(8)]
        proj, score, turned, context = bank[0:2], bank[2:4], bank[4:6], bank[6]
        turns = bank[6:8] + bank[2:4]
        ff_sum = bank[2:6]

        col = {n: sb(f"{n}_col", [P, w]) for n, w in (("bq", G), ("bk", G), ("bv", G), ("b1", NF), ("g2", KB), ("beta2", KB), ("down_b", 1))}
        row = {n: sb(f"{n}_row", [P, D]) for n in ("bo", "b2", "up_b", "gamma", "beta")}
        minus_half = sb("minus_half", [P, TB])
        scale_row, shift_row = sb("scale_row", [P, D]), sb("shift_row", [P, D])
        mask8, mask_add = sb("mask8", [P, TB, S], U8), sb("mask_add", [P, TB, S], BF16)
        sel_T = sb("sel_T", [A, A])
        cur = sb("cur", [P, 8])
        xin = sb("xin", [P, TB, D])
        tok = sb("tok", [P, TB, D])
        res = sb("res", [P, TB, D])
        xT = [sb(f"xT{h}", [P, KB, S], F32R) for h in range(2)]
        stats, agg, fence = sb("stats", [P, TB, 6]), sb("agg", [P, TB, 2]), sb("fence", [P, 8])
        var, rstd = sb("var", [P, TB]), sb("rstd", [P, TB])
        V = sb("V", [P, TB, D])
        Vg = sb("Vg", [P, HG, TB, DH])
        wide = sb("wide", [P, 2, 512])
        parts = sb("parts", [P, 4, 512], F32R)
        stack = sb("stack", [P, HG, 2, 512], F32R)
        prob = [sb(f"prob{j}", [P, TB, S]) for j in range(HG)]
        low, total, inv = (sb(n, [P, 16]) for n in ("low", "total", "inv"))
        probT = sb("probT", [P, TB, S])
        ctxT = sb("ctxT", [P, G, S])
        gel = sb("gel", [P, 2, 512])
        w_raw = [sb(f"w_raw{s}", [P, 1024])[:] for s in range(2)]
        w_raw += [V[:, 2 * s:2 * s + 2, :].rearrange("p a b -> p (a b)") for s in range(2)]
        w = [sb(f"w{s}", [P, 2, 1024], F32R)[:] for s in range(2)]
        w += [stack[:, 2 * s:2 * s + 2, :, :].rearrange("p h a b -> p h (a b)") for s in range(2)]

        consts_in, half_set = sem("consts_in"), sem("half_set")
        x_in, ada_in, mask_in, sel_in = sem("x_in"), sem("ada_in"), sem("mask_in"), sem("sel_in")
        raw_in = [sem(f"raw_in{s}") for s in range(4)]
        bias_in = [[sem(f"bias_in{j}_{h}") for h in range(2)] for j in range(HG)]
        stack_in = [sem(f"stack_in{j}") for j in range(HG)]
        out_done = sem("out_done")
        dve_step = sem("dve_step")
        var_ready, rstd_ready = sem("var_ready"), sem("rstd_ready")
        tok_ready, mask_ready = sem("tok_ready"), sem("mask_ready")
        xin_biased = sem("xin_biased")
        w_hi, w_lo = [sem(f"w_hi{s}") for s in range(4)], [sem(f"w_lo{s}") for s in range(4)]
        turn_full, turn_hi, turn_lo, turn_wide = sem("turn_full"), sem("turn_hi"), sem("turn_lo"), sem("turn_wide")
        proj_full, proj_read = [sem(f"proj_full{s}") for s in range(2)], [sem(f"proj_read{s}") for s in range(2)]
        v_copied, vg_copied = sem("v_copied"), sem("vg_copied")
        qk_hi, qk_lo = sem("qk_hi"), sem("qk_lo")
        bias_masked, score_full, scored, exped, inverted, normed = (sem(n) for n in ("bias_masked", "score_full", "scored", "exped", "inverted", "normed"))
        probT_full, probT_copied, pv_done, ctx_copied = (sem(n) for n in ("probT_full", "probT_copied", "pv_done", "ctx_copied"))
        ctx_hi, ctx_lo = sem("ctx_hi"), sem("ctx_lo")
        z2_ready, res_biased, geled, g_hi, g_lo, ff2_done = (sem(n) for n in ("z2_ready", "res_biased", "geled", "g_hi", "g_lo", "ff2_done"))
        y_ready, y_biased, hid_wide, hid_ready, mixed, out_ready = (sem(n) for n in ("y_ready", "y_biased", "hid_wide", "hid_ready", "mixed", "out_ready"))

        rows_of = lambda t, b: t[bass.ds(b, 1)].rearrange("o (t p) c -> p (o t) c", p=P)
        bcast = lambda t: t[:].unsqueeze(1).to_broadcast([P, TB, D])
        weight = lambda s, h: w[s][:, h, :].rearrange("p (k n) -> p k n", k=8)

        def chunk_item(b, i, c):
            i, c = (i + 1, c - 4) if c >= 4 else (i, c)
            s = (c + 2) % 4
            return s, ITEMS[s] * b + F_ITEM[s] + i

        with nc.Block() as block:

            @block.sync
            def _(sp):
                for signal in (*w_hi, *w_lo, *proj_full, *proj_read, probT_full, tok_ready, mask_ready, mixed, ff2_done,
                               vg_copied, pv_done, g_lo, turn_lo, scored, probT_copied, ctx_copied, bias_masked, out_ready):
                    sp.sem_inc(signal, START)
                sp.sem_inc(out_done, 16)
                for signal in stack_in:
                    sp.sem_inc(signal, 64)
                def load_weight(s, count, first, second):
                    sp.wait_ge(w_hi[s], count + START)
                    sp.wait_ge(w_lo[s], count + START)
                    for dst, src in (first, second):
                        sp.dma_start(dst, src).then_inc(raw_in[s], 16)

                raw = lambda s, h: w_raw[s][:, 512 * h:512 * h + 512]
                blocks = lambda s, h: raw(s, h).rearrange("p (k n) -> p k n", k=4)

                def load_qk(s, count, g):
                    load_weight(s, count, *(
                        (blocks(s, h), t[:, bass.ds(P * g, P)].rearrange("(k p) n -> p k n", p=P)) for h, t in ((0, Wq), (1, Wk))))

                def load_rows(s, count, t, k):
                    load_weight(s, count, *((raw(s, h), t[P * (k + h):P * (k + h + 1), :]) for h in range(2)))

                def load_bias(b, g, j):
                    src = bias[bass.ds(b, 1), bass.ds(HG * g + j, 1)].rearrange("o h (t p) k -> p (o h t) k", p=P)
                    for h in range(2):
                        sp.dma_start(prob[j][:, 2 * h:2 * h + 2, :], src[:, 2 * h:2 * h + 2, :]).then_inc(bias_in[j][h], 16)

                def load_stack(b, g, j):
                    for quad, (q, step) in enumerate(((0, 2), (1, 1), (0, 3), (1, 2))):
                        sp.dma_start(stack[DH * quad:DH * (quad + 1), j, :, :].bitcast(F32),
                                     parts[DH * j:DH * (j + 1), q:q + step + 1:step, :].bitcast(F32)).then_inc(stack_in[j], 16)

                def group(b, g):
                    n = 4 * b + g
                    sp.wait_ge(probT_full, 16 * n + 4 + START)
                    load_bias(b, g + 1, 0)
                    sp.wait_ge(qk_hi, 2 * n + 4)
                    sp.wait_ge(qk_lo, 2 * n + 4)
                    for j in range(HG):
                        if j == 2:
                            sp.wait_ge(probT_full, 16 * n + 8 + START)
                            load_bias(b, g + 1, 1)
                        if j:
                            sp.wait_ge(score_full, 16 * n + 4 * j + 4)
                        load_stack(b, g + 1, j)
                    for j in (2, 3):
                        sp.wait_ge(probT_full, 16 * n + 4 * j + 4 + START)
                        load_bias(b, g + 1, j)

                def load_chunk(s, count, f):
                    load_weight(s, count, (blocks(s, 0), W1[:, bass.ds(P * f, P)].rearrange("(k p) n -> p k n", p=P)),
                                (raw(s, 1), W2[bass.ds(P * f, P), :]))

                def load_input(b, batch):
                    sp.dma_start(xin[:], rows_of(x1, batch)).then_inc(x_in, 16)
                    for part, dst in enumerate((scale_row, shift_row)):
                        sp.dma_start(dst[:], ada_rows[bass.ds(batch, 1), part * D:(part + 1) * D].rearrange("o c -> (o c)").partition_broadcast(P)) \
                            .then_inc(ada_in, 16)
                    sp.wait_ge(mask_ready, b + START)
                    sp.dma_start(mask8[:], mask[bass.ds(batch, 1), 0].rearrange("o (t p) k -> p (o t) k", p=P)).then_inc(mask_in, 16)

                def load_first_weights(b):
                    load_qk(2, ITEMS[2] * b + W2_QK0, 0)
                    load_rows(0, ITEMS[0] * b + W0_V, Wv, 0)
                    load_rows(1, ITEMS[1] * b + W1_V, Wv, 2)
                    load_qk(0, ITEMS[0] * b + W0_QK + 1, 1)

                load_input(0, 0)
                load_first_weights(0)
                for n, src, wd in (("bq", bq, G), ("bk", bk, G), ("bv", bv, G), ("b1", b1, NF), ("g2", g2, KB), ("beta2", beta2, KB), ("down_b", down_b, 1)):
                    sp.dma_start(col[n][:], src.rearrange("(k p) -> p k", p=P), allow_slow_non_contiguous=True).then_inc(consts_in, 16)
                for n, src in (("bo", bo), ("b2", b2), ("up_b", up_b), ("gamma", gamma), ("beta", beta)):
                    sp.dma_start(row[n][:], src.partition_broadcast(P)).then_inc(consts_in, 16)
                for j in range(HG):
                    load_bias(0, 0, j)
                with sp.Fori(0, B) as b:
                    following = (b + 1) % B
                    sp.wait_ge(mixed, b + START)
                    sp.dma_start(sel_T[:], sel_turned[bass.ds(b, 1)].rearrange("o a c -> a (o c)")).then_inc(sel_in, 16)
                    load_rows(1, ITEMS[1] * b + W1_O, Wo, 2)
                    sp.wait_ge(qk_hi, 8 * b + 2)
                    sp.wait_ge(qk_lo, 8 * b + 2)
                    for j in range(HG):
                        load_stack(b, 0, j)
                    load_qk(0, ITEMS[0] * b + W0_QK + 2, 2)
                    group(b, 0)
                    load_qk(0, ITEMS[0] * b + W0_QK + 3, 3)
                    group(b, 1)
                    load_rows(0, ITEMS[0] * b + W0_O, Wo, 0)
                    group(b, 2)
                    sp.wait_ge(vg_copied, NH * (b + 1) + START)
                    for c in range(4):
                        load_chunk(*chunk_item(b, 0, c), c)
                    for s in range(2):
                        sp.wait_ge(proj_read[s], FILLS * b + FILL_O + 2 + START)
                    load_input(b + 1, following)
                    for i in range(1, NF // 4):
                        for c in range(4):
                            load_chunk(*chunk_item(b, i, c), 4 * i + c)
                        sp.wait_ge(probT_full, 64 * (b + 1) + START)
                        for j in ((0,), (1, 2), (3,))[i - 1]:
                            load_bias(following, 0, j)
                    load_first_weights(b + 1)

            @block.gpsimd
            def _(pool):
                pool.memset(minus_half[:], -0.5).then_inc(half_set, 1)
                pool.wait_ge(half_set, 1)

                def split_lo(s, count):
                    pool.wait_ge(w_hi[s], count + 1 + START)
                    pool.tensor_tensor(w[s][:, 1, :], w_raw[s], w[s][:, 0, :].bitcast(F32), ALU.subtract).then_inc(w_lo[s], 1)

                def root(count, q):
                    pool.wait_ge(var_ready, count)
                    pool.tensor_tensor(rstd[:, q:q + 1], var[:, q:q + 1], minus_half[:, q:q + 1], ALU.pow).then_inc(rstd_ready, 1)

                def add_mask(b, g, j, halves=(0, 1)):
                    for h in halves:
                        pool.wait_ge(bias_in[j][h], 16 * (4 * b + g + 1))
                        half = prob[j][:, 2 * h:2 * h + 2, :]
                        pool.tensor_tensor(half, half, mask_add[:, 2 * h:2 * h + 2, :], ALU.add).then_inc(bias_masked, 1)

                def group(b, g):
                    split_lo(0, ITEMS[0] * b + W0_QK + g + 2)
                    add_mask(b, g + 1, 0)
                    for j in (1, 2, 3):
                        add_mask(b, g + 1, j)

                for q in range(TB):
                    root(q + 1, q)
                split_lo(2, W2_QK0)
                split_lo(0, W0_V)
                split_lo(1, W1_V)
                split_lo(0, W0_QK + 1)
                pool.wait_ge(mask_ready, 1 + START)
                for j in range(HG):
                    add_mask(0, 0, j)
                pool.wait_ge(consts_in, 16 * 12)
                with pool.Fori(0, B) as b:
                    pool.wait_ge(turn_full, TURNS * b + KB)
                    pool.tensor_tensor(xin[:], xin[:], bcast(row["bo"]), ALU.add).then_inc(xin_biased, 1)
                    split_lo(1, ITEMS[1] * b + W1_O)
                    for g in range(G - 1):
                        group(b, g)
                    for c in range(2):
                        split_lo(*chunk_item(b, 0, c))
                    for q in range(TB):
                        root(ROOTS * b + TB + q + 1, q)
                    split_lo(*chunk_item(b, 0, 2))
                    pool.wait_ge(z2_ready, b + 1)
                    pool.tensor_tensor(res[:], res[:], bcast(row["b2"]), ALU.add).then_inc(res_biased, 1)
                    split_lo(*chunk_item(b, 0, 3))
                    for c in range(4):
                        split_lo(*chunk_item(b, 1, c))
                    pool.wait_ge(mask_ready, b + 2 + START)
                    for f in range(8, NF):
                        split_lo(*chunk_item(b, f // 4, f % 4))
                        add_mask(b + 1, 0, (f - 8) // 2, (f % 2,))
                        if f < 8 + TB:
                            root(ROOTS * b + f + 1, f - 8)
                    split_lo(2, ITEMS[2] * (b + 1) + W2_QK0)
                    split_lo(0, ITEMS[0] * (b + 1) + W0_V)
                    pool.wait_ge(y_ready, b + 1)
                    pool.tensor_tensor(res[:], tok[:], bcast(row["up_b"]), ALU.add).then_inc(y_biased, 1)
                    split_lo(1, ITEMS[1] * (b + 1) + W1_V)
                    for q in range(TB):
                        root(ROOTS * (b + 1) + q + 1, q)
                    split_lo(0, ITEMS[0] * (b + 1) + W0_QK + 1)

            @block.scalar
            def _(act):
                def split_hi(s, count):
                    act.wait_ge(raw_in[s], 32 * (count + 1))
                    act.activation(w[s][:, 0, :], w_raw[s], ACT.Copy).then_inc(w_hi[s], 1)

                def turn_hi_from(b, n, src, k):
                    act.activation(xT[0][:, k, :], src, ACT.Copy).then_inc(turn_hi, 1)

                def exp(b, m, mm):
                    act.wait_ge(scored, m + 1 + START)
                    j, qb = (mm % 16) // 4, mm % 4
                    act.activation(prob[j][:, qb, :], prob[j][:, qb, :], ACT.Exp, bias=low[:, mm % 16:mm % 16 + 1], scale=-1.0,
                                   accum_out=total[:, mm % 16:mm % 16 + 1]).then_inc(exped, 1)

                def group(b, g, first, last):
                    n = 4 * b + g
                    for i in range(16):
                        m = 16 * n + i
                        if not (last and i + EXP_LEAD >= 16):
                            exp(b, m + EXP_LEAD, i + EXP_LEAD)
                        act.wait_ge(probT_full, m + 1 + START)
                        act.wait_ge(pv_done, (64 * b if first and i < 4 else m - 3) + START)
                        act.activation(probT[:, i % 4, :], turned[i % 2][:], ACT.Copy).then_inc(probT_copied, 1)
                        if last and 6 <= i < 9:
                            ctx_hi_part(b, i - 6)
                        if i in (2, 3) and not last:
                            q_hi(b, g + 1, i - 2, FILL_QK + g + 1)
                        if i == 4 and not last:
                            act.wait_ge(proj_full[1], FILLS * b + FILL_QK + g + 2 + START)
                            split_hi(0, ITEMS[0] * b + W0_QK + g + 2)

                def q_hi(b, g, c, fill):
                    if c == 0:
                        for j in range(HG):
                            act.wait_ge(stack_in[j], 64 * (4 * b + g) + 64)
                    act.wait_ge(proj_read[c], FILLS * b + fill + 1 + START)
                    act.activation(parts[:, 2 * c, :], wide[:, c, :], ACT.Copy).then_inc(qk_hi, 1)

                def ctx_hi_part(b, g):
                    act.wait_ge(ctx_copied, NH * b + HG * (g + 1) + START)
                    act.activation(xT[0][:, g, :], ctxT[:, g, :], ACT.Copy).then_inc(ctx_hi, 1)

                def split_first(b):
                    split_hi(2, ITEMS[2] * b + W2_QK0)
                    act.wait_ge(ff2_done, NF * b - 1 + START)
                    split_hi(0, ITEMS[0] * b + W0_V)

                def split_last(b):
                    act.wait_ge(ff2_done, NF * b + START)
                    split_hi(1, ITEMS[1] * b + W1_V)

                def input_parts(b):
                    for k in range(KB):
                        act.wait_ge(turn_full, TURNS * b + k + 1)
                        if k == 0:
                            act.wait_ge(proj_full[0], FILLS * b - (FILLS - FILL_L2 - 1) + START)
                        turn_hi_from(b, k, turns[k][:], k)
                    for c in range(2):
                        q_hi(b, 0, c, FILL_QK0)
                    act.wait_ge(vg_copied, NH * b + START)
                    for t in range(TB):
                        act.wait_ge(proj_full[t % 2], FILLS * b + FILL_V + t // 2 + 1 + START)
                        act.activation(V[:, t, :], proj[t % 2][:], ACT.Copy).then_inc(proj_read[t % 2], 1)
                    split_hi(0, ITEMS[0] * b + W0_QK + 1)

                split_first(0)
                split_last(0)
                input_parts(0)
                act.wait_ge(consts_in, 16 * 12)
                with act.Fori(0, B) as b:
                    split_hi(1, ITEMS[1] * b + W1_O)
                    for m in range(EXP_LEAD):
                        exp(b, 64 * b + m, m)
                    group(b, 0, True, False)
                    with act.Fori(1, G - 1) as g:
                        group(b, g, False, False)
                    group(b, G - 1, False, True)
                    ctx_hi_part(b, G - 1)
                    act.wait_ge(score_full, 64 * (b + 1))
                    for c in range(2):
                        split_hi(*chunk_item(b, 0, c))
                    act.wait_ge(proj_full[1], FILLS * b + FILL_O + 2 + START)
                    split_hi(*chunk_item(b, 0, 2))
                    for k in range(KB):
                        act.wait_ge(turn_full, TURNS * b + KB + k + 1)
                        if k >= 2:
                            act.wait_ge(turn_lo, TURNS * b + KB + k - 1 + START)
                        act.activation(wide[:, k % 2, :], turns[k][:], ACT.Identity, bias=col["beta2"][:, k:k + 1], scale=col["g2"][:, k:k + 1]) \
                            .then_inc(turn_wide, 1)
                        act.wait_ge(turn_wide, KB * b + k + 1)
                        turn_hi_from(b, KB + k, wide[:, k % 2, :], k)

                    def chunk(i, c, last):
                        f, s = 4 * i + c, c % 2
                        act.wait_ge(proj_read[s], FILLS * b + FILL_F + 2 * i + c // 2 + 1 + START)
                        act.wait_ge(g_lo, NF * b + f - 1 + START)
                        act.activation(gel[:, s, :], wide[:, s, :], ACT.Gelu_apprx_sigmoid).then_inc(geled, 1)
                        act.wait_ge(geled, NF * b + f + 1)
                        act.wait_ge(ff2_done, NF * b + f - 1 + START)
                        act.activation(parts[:, 2 * s, :], gel[:, s, :], ACT.Copy).then_inc(g_hi, 1)
                        if not (last and c):
                            act.wait_ge(ff2_done, NF * b + f + START)
                            split_hi(*chunk_item(b, i, c + 3))

                    with act.Fori(0, NF // 4 - 1) as i:
                        for c in range(4):
                            chunk(i, c, False)
                    for c in range(4):
                        chunk(NF // 4 - 1, c, True)
                        if c == 3:
                            split_first(b + 1)
                    for k in range(KB):
                        act.wait_ge(turn_full, TURNS * b + 2 * KB + k + 1)
                        turn_hi_from(b, 2 * KB + k, turns[k][:], k)
                    split_last(b + 1)
                    act.wait_ge(hid_wide, b + 1)
                    act.activation(gel[:, 0, :], wide[:, 0, :], ACT.Gelu).then_inc(hid_ready, 1)
                    input_parts(b + 1)
                    act.wait_ge(out_ready, b + 1 + START)
                    act.dma_start(rows_of(out, b), res[:]).then_inc(out_done, 16)
                act.wait_ge(out_done, 16 * B + 16)

            @block.tensor
            def _(t):
                def split_product(dst, stat, mov, ks, start, stop):
                    n, count = 0, 3 * len(ks)
                    for k in ks:
                        for hs, hm in ((0, 0), (0, 1), (1, 0)):
                            mm = t.matmul(dst, stat(hs, k), mov(hm, k), start=start and n == 0, stop=stop and n == count - 1)
                            n += 1
                    return mm

                def turn(b, n, src, k):
                    t.wait_ge(turn_lo, TURNS * b + n - (KB - 1) + START)
                    for q in range(TB):
                        mm = t.transpose(turns[k][:, q * P:(q + 1) * P], src[:, q, k * P:(k + 1) * P], ident[:])
                    mm.then_inc(turn_full, 1)

                def v_weight(h, k):
                    return w[k // 2][:, h, 512 * (k % 2):512 * (k % 2) + 512]

                def rows_product(b, fill, last_lo=None):
                    for q in range(TB):
                        t.wait_ge(proj_read[q % 2], FILLS * b + fill + q // 2 + START)
                        stat = lambda h, k: xT[h][:, k, q * P:(q + 1) * P]
                        split_product(proj[q % 2][:], stat, v_weight, range(KB - 1), True, False)
                        if q == 0 and last_lo is not None:
                            t.wait_ge(ctx_lo, last_lo)
                        split_product(proj[q % 2][:], stat, v_weight, range(KB - 1, KB), False, True).then_inc(proj_full[q % 2], 1)

                def qk(b, c, fill, s, count):
                    t.wait_ge(proj_read[c], FILLS * b + fill + START)
                    if c == 0:
                        t.wait_ge(w_lo[s], count + 1 + START)
                    split_product(proj[c][:], lambda h, k: weight(s, h)[:, KB * c + k, :], lambda h, k: xT[h][:, k, :], range(KB), True, True) \
                        .then_inc(proj_full[c], 1)

                QK_TERMS = [(k, hs, hm) for k in range(KB) for hs, hm in ((0, 0), (0, 1), (1, 0))]
                QK_PIECES = 12

                def qk_piece(b, g, p):
                    c, part = divmod(p, QK_PIECES // 2)
                    if part == 0:
                        t.wait_ge(proj_read[c], FILLS * b + FILL_QK + g + START)
                    if p == 0:
                        t.wait_ge(w_lo[0], ITEMS[0] * b + W0_QK + g + 1 + START)
                    for n in (2 * part, 2 * part + 1):
                        k, hs, hm = QK_TERMS[n]
                        mm = t.matmul(proj[c][:], weight(0, hs)[:, KB * c + k, :], xT[hm][:, k, :], start=n == 0, stop=n == len(QK_TERMS) - 1)
                    if part == QK_PIECES // 2 - 1:
                        mm.then_inc(proj_full[c], 1)

                def input_turn(b, k):
                    if k == 0:
                        t.wait_ge(tok_ready, b + 1 + START)
                    turn(b, k, xin, k)

                def input_products(b):
                    t.wait_ge(turn_lo, TURNS * b + KB + START)
                    for c in range(2):
                        qk(b, c, FILL_QK0, 2, ITEMS[2] * b + W2_QK0)
                    t.wait_ge(w_lo[0], ITEMS[0] * b + W0_V + 1 + START)
                    t.wait_ge(w_lo[1], ITEMS[1] * b + W1_V + 1 + START)
                    rows_product(b, FILL_V)

                def score_block(b, m, mm, g):
                    j, qb = (mm % 16) // 4, mm % 4
                    t.wait_ge(scored, (m - 1 if not isinstance(g, int) or g or mm >= 2 else 64 * b) + START)
                    if qb == 0:
                        t.wait_ge(stack_in[j], 64 * (4 * b + g + 1) + 64)
                    t.matmul(score[mm % 2][:], stack[:, j, 0, qb * P:(qb + 1) * P], stack[:, j, 1, :], start=True, stop=True) \
                        .then_inc(score_full, 1)

                def pv(b, m, mm, vals):
                    j, kb = (mm % 16) // 4, mm % 4
                    t.wait_ge(probT_copied, m + 1 + START)
                    if kb == 0:
                        t.wait_ge(vg_copied, vals[0] + START)
                        t.wait_ge(ctx_copied, vals[1] + START)
                    t.matmul(context[DH * j:DH * (j + 1), :], Vg[:, j, kb, :], probT[:, kb, :], start=kb == 0, stop=kb == TB - 1,
                             tile_position=(0, DH * j)).then_inc(pv_done, 1)

                def group(b, g):
                    n, first, last = 4 * b + g, g == 0, g == G - 1
                    for i in range(16):
                        m = 16 * n + i
                        j, kb = i // 4, i % 4
                        if not (last and i + S_LEAD >= 16):
                            score_block(b, m + S_LEAD, i + S_LEAD, g + (i + S_LEAD) // 16)
                        if kb == 0:
                            t.wait_ge(normed, m + 4)
                        t.wait_ge(probT_copied, (64 * b if first and i < 2 else m - 1) + START)
                        for q in range(TB):
                            mm = t.transpose(turned[i % 2][:, q * P:(q + 1) * P], prob[j][:, q, kb * P:(kb + 1) * P], ident[:])
                        mm.then_inc(probT_full, 1)
                        if not last and i < 2:
                            qk_piece(b, g + 1, 10 + i)
                        if g + 2 < G and i >= 7:
                            for p in range((i - 7) * 10 // 9, (i - 6) * 10 // 9):
                                qk_piece(b, g + 2, p)
                        if not (first and i < 2):
                            head = 4 * n + (i - 2) // 4
                            pv(b, m - 2, (i - 2) % 16, (head + 1, NH * b if first else head - 3))

                for k in range(KB):
                    input_turn(0, k)
                input_products(0)
                with t.Fori(0, B) as b:
                    for m in range(S_LEAD):
                        score_block(b, 64 * b + m, m, 0)
                        if m >= S_LEAD - 5:
                            for p in range(2):
                                qk_piece(b, 1, 2 * (m - S_LEAD + 5) + p)
                    for g in range(G):
                        group(b, g)
                    for mm in (14, 15):
                        pv(b, 64 * b + 48 + mm, mm, None)
                    t.wait_ge(ctx_lo, G * b + G - 1)
                    t.wait_ge(w_lo[0], ITEMS[0] * b + W0_O + 1 + START)
                    t.wait_ge(w_lo[1], ITEMS[1] * b + W1_O + 1 + START)
                    rows_product(b, FILL_O, G * b + G)
                    t.wait_ge(z2_ready, b + 1)
                    for k in range(KB):
                        turn(b, KB + k, tok, k)
                    def ff1(i, c):
                        s, count = chunk_item(b, i, c)
                        t.wait_ge(w_lo[s], count + 1 + START)
                        t.wait_ge(proj_read[c % 2], FILLS * b + FILL_F + 2 * i + c // 2 + START)
                        split_product(proj[c % 2][:], lambda h, k: weight(s, h)[:, k, :], lambda h, k: xT[h][:, k, :], range(KB), True, True) \
                            .then_inc(proj_full[c % 2], 1)

                    def ff2(i, c, start, stop):
                        s, _ = chunk_item(b, i, c)
                        t.wait_ge(g_lo, NF * b + 4 * i + c + 1 + START)
                        for q in range(TB):
                            mm = split_product(ff_sum[q][:], lambda h, _: parts[:, 2 * (c % 2) + h, q * P:(q + 1) * P],
                                               lambda h, _: w[s][:, h, 512:1024], range(1), start, stop)
                        mm.then_inc(ff2_done, 1)

                    s, count = chunk_item(b, 0, 0)
                    t.wait_ge(w_lo[s], count + 1 + START)
                    t.wait_ge(proj_read[0], FILLS * b + FILL_F + START)
                    for k in range(KB):
                        t.wait_ge(turn_lo, TURNS * b + KB + k + 1 + START)
                        mm = split_product(proj[0][:], lambda h, k: weight(s, h)[:, k, :], lambda h, k: xT[h][:, k, :], (k,), k == 0, k == KB - 1)
                    mm.then_inc(proj_full[0], 1)
                    for c in range(1, 4):
                        ff1(0, c)
                        ff2(0, c - 1, c == 1, False)
                    with t.Fori(1, NF // 4) as i:
                        ff1(i, 0)
                        ff2(i - 1, 3, False, False)
                        for c in range(1, 4):
                            ff1(i, c)
                            ff2(i, c - 1, False, False)
                    ff2(NF // 4 - 1, 3, False, True)
                    t.wait_ge(y_ready, b + 1)
                    for k in range(KB):
                        turn(b, 2 * KB + k, tok, k)
                    for k in range(KB):
                        t.wait_ge(turn_lo, TURNS * b + 2 * KB + k + 1 + START)
                        mm = split_product(proj[0][:], lambda h, k: down[h][:, k, :], lambda h, k: xT[h][:, k, :], (k,), k == 0, k == KB - 1)
                    mm.then_inc(proj_full[0], 1)
                    for k in range(2):
                        input_turn(b + 1, k)
                    t.wait_ge(hid_ready, b + 1)
                    t.wait_ge(sel_in, 16 * (b + 1))
                    t.matmul(proj[1][:], sel_T[:], gel[:, 0, :], start=True, stop=True).then_inc(proj_full[1], 1)
                    for k in range(2, KB):
                        input_turn(b + 1, k)
                    t.wait_ge(mixed, b + 1 + START)
                    for q in range(TB):
                        t.wait_ge(proj_read[q % 2], FILLS * b + FILL_UP + q // 2 + START)
                        t.matmul(proj[q % 2][:], wide[:, 1, q * P:(q + 1) * P], up_T[:], start=True, stop=True).then_inc(proj_full[q % 2], 1)
                    input_products(b + 1)

            @block.vector
            def _(v):
                STEPS, FIRST_STEPS = 62, 23

                def variance(link, src, q):
                    link(v.bn_stats(stats[:, q, :], src[:, q, :]))
                    link.mark(v.tensor_copy(fence[:, 7:8], stats[:, q, 0:1]))
                    link(v.bn_aggr(agg[:, q, :], stats[:, q, :]))
                    v.tensor_scalar(var[:, q:q + 1], agg[:, q, 1:2], EPS, None, ALU.add).then_inc(var_ready, 1)

                def normalise(dst, src, q):
                    return v.tensor_scalar(dst[:, q, :], src[:, q, :], agg[:, q, 0:1], rstd[:, q:q + 1], ALU.subtract, ALU.mult)

                def number_mask(b):
                    v.wait_ge(mask_in, 16 * (b + 1))
                    v.wait_ge(bias_masked, 32 * b + START)
                    v.tensor_scalar(mask_add[:], mask8[:], MASKED, None, ALU.mult).then_inc(mask_ready, 1)

                def adapt(link, b, q, root):
                    v.wait_ge(rstd_ready, root + q + 1)
                    if q == 0:
                        v.wait_ge(ada_in, 32 * (b + 1))
                    link(normalise(xin, xin, q))
                    link(v.tensor_tensor(xin[:, q, :], xin[:, q, :], scale_row[:], ALU.mult))
                    ins = v.tensor_tensor(xin[:, q, :], xin[:, q, :], shift_row[:], ALU.add)
                    if q == TB - 1:
                        ins.then_inc(tok_ready, 1)
                    else:
                        link.mark(ins)

                def turn_lo_part(b, n, k, src):
                    v.wait_ge(turn_hi, TURNS * b + n + 1)
                    v.tensor_tensor(xT[1][:, k, :], src, xT[0][:, k, :].bitcast(F32), ALU.subtract).then_inc(turn_lo, 1)

                def qk_wide(b, g, c, fill):
                    v.wait_ge(proj_full[c], FILLS * b + fill + 1 + START)
                    bias_col = col["bk" if c else "bq"][:, bass.ds(g, 1)]
                    if c:
                        ins = v.tensor_scalar(wide[:, 1, :], proj[1][:], bias_col, None, ALU.add)
                    else:
                        ins = v.tensor_scalar(wide[:, 0, :], proj[0][:], bias_col, QSCALE, ALU.add, ALU.mult)
                    ins.then_inc(proj_read[c], 1)

                def qk_lo_part(b, g, c):
                    v.wait_ge(qk_hi, 8 * b + 2 * g + c + 1)
                    v.tensor_tensor(parts[:, 2 * c + 1, :], wide[:, c, :], parts[:, 2 * c, :].bitcast(F32), ALU.subtract).then_inc(qk_lo, 1)

                def invert(m, mm):
                    v.wait_ge(exped, m + 1)
                    v.reciprocal(inv[:, mm % 16:mm % 16 + 1], total[:, mm % 16:mm % 16 + 1]).then_inc(inverted, 1)

                def scale_rows(m, mm):
                    j, qb = (mm % 16) // 4, mm % 4
                    v.wait_ge(inverted, m + 1)
                    v.tensor_scalar(prob[j][:, qb, :], prob[j][:, qb, :], inv[:, mm % 16:mm % 16 + 1], None, ALU.mult).then_inc(normed, 1)

                def await_scores(n, i):
                    v.wait_ge(score_full, 16 * n + i + 1)
                    if i % 2 == 0:
                        v.wait_ge(bias_masked, 8 * n + i // 2 + 1 + START)

                def scores_at(i):
                    j, qb = (i % 16) // 4, i % 4
                    v.tensor_tensor_reduce(prob[j][:, qb, :], score[i % 2][:], prob[j][:, qb, :], -1.0, MIN_START, ALU.add, ALU.min,
                                           low[:, i % 16:i % 16 + 1]).then_inc(scored, 1)

                def copy_v(b, g, j, pv_count):
                    v.wait_ge(pv_done, pv_count + START)
                    v.tensor_copy(Vg[:, j, :, :], V[:, :, bass.ds(P * g + DH * j, DH)]).then_inc(vg_copied, 1)

                def take_context(b, g, j):
                    v.wait_ge(pv_done, 64 * b + 16 * g + 4 * j + 4 + START)
                    quad = slice(DH * j, DH * (j + 1))
                    v.tensor_scalar(ctxT[quad, bass.ds(g, 1), :].rearrange("p o s -> p (o s)"), context[quad, :], col["bv"][quad, bass.ds(g, 1)], None, ALU.add) \
                        .then_inc(ctx_copied, 1)

                def group(b, g, first, last):
                    n = 4 * b + g
                    for i in range(16):
                        m = 16 * n + i
                        ahead = not (last and i + S_LEAD >= 16)
                        if ahead:
                            await_scores(n, i + S_LEAD)
                        if not (last and i + NORM_LEAD >= 16):
                            invert(m + NORM_LEAD, i + NORM_LEAD)
                        if ahead:
                            scores_at(i + S_LEAD)
                        if not (last and i + NORM_LEAD >= 16):
                            scale_rows(m + NORM_LEAD, i + NORM_LEAD)
                        if i % 4 == 2 and not (first and i == 2):
                            take_context(b, g if i > 2 else g - 1, (i - 6) // 4 % 4)
                        if i == 3:
                            copy_v(b, g, 3, 16 * n)
                        elif i % 4 == 3 and not last:
                            copy_v(b, g + 1, i // 4 - 1, 16 * n + i - 3)
                        if last and 8 <= i < 11:
                            ctx_lo_part(b, i - 8)
                        if not last and i in (2, 3):
                            qk_wide(b, g + 1, i - 2, FILL_QK + g + 1)
                        if not last and i in (4, 5):
                            qk_lo_part(b, g + 1, i - 4)

                def ctx_lo_part(b, g):
                    v.wait_ge(ctx_hi, G * b + g + 1)
                    v.tensor_tensor(xT[1][:, g, :], ctxT[:, g, :], xT[0][:, g, :].bitcast(F32), ALU.subtract).then_inc(ctx_lo, 1)

                def first_qk(b):
                    for c in range(2):
                        qk_wide(b, 0, c, FILL_QK0)
                    for c in range(2):
                        qk_lo_part(b, 0, c)

                link = Link(v, dve_step)
                number_mask(0)
                v.wait_ge(x_in, 16)
                for q in range(TB):
                    variance(link, xin, q)
                for q in range(TB):
                    adapt(link, 0, q, 0)
                for k in range(KB):
                    turn_lo_part(0, k, k, turns[k][:])
                v.wait_ge(consts_in, 16 * 12)
                first_qk(0)
                assert link.n == FIRST_STEPS, link.n
                with v.Fori(0, B) as b:
                    link = Link(v, dve_step, STEPS * b + FIRST_STEPS)
                    v.wait_ge(out_ready, b + START)
                    link(v.tensor_copy(cur[:], scal[:, bass.ds(b, 1), :].rearrange("p o c -> p (o c)")))
                    v.wait_ge(proj_read[0], FILLS * b + FILL_V + 2 + START)
                    v.wait_ge(proj_read[1], FILLS * b + FILL_V + 2 + START)
                    for j in range(3):
                        copy_v(b, 0, j, 64 * b)
                    for i in range(S_LEAD):
                        await_scores(4 * b, i)
                        v.tensor_copy(fence[:, i:i + 1], cur[:, 0:1])
                        scores_at(i)
                    for i in range(NORM_LEAD):
                        invert(64 * b + i, i)
                    for i in range(NORM_LEAD):
                        scale_rows(64 * b + i, i)
                    group(b, 0, True, False)
                    with v.Fori(1, G - 1) as g:
                        group(b, g, False, False)
                    group(b, G - 1, False, True)
                    take_context(b, G - 1, 3)
                    ctx_lo_part(b, G - 1)
                    v.wait_ge(out_done, 16 * b + 16)
                    v.wait_ge(xin_biased, b + 1)
                    for q in range(TB):
                        v.wait_ge(proj_full[q % 2], FILLS * b + FILL_O + q // 2 + 1 + START)
                        v.tensor_tensor(res[:, q, :], proj[q % 2][:], xin[:, q, :], ALU.add).then_inc(proj_read[q % 2], 1)
                        v.wait_ge(proj_read[q % 2], FILLS * b + FILL_O + q // 2 + 1 + START)
                        variance(link, res, q)
                        if q:
                            v.wait_ge(rstd_ready, ROOTS * b + TB + q)
                            link.mark(normalise(tok, res, q - 1))
                    v.wait_ge(rstd_ready, ROOTS * b + 2 * TB)
                    normalise(tok, res, TB - 1).then_inc(z2_ready, 1)
                    for k in range(KB):
                        turn_lo_part(b, KB + k, k, wide[:, k % 2, :])

                    def widen(f):
                        v.wait_ge(proj_full[f % 2], FILLS * b + FILL_F + f // 2 + 1 + START)
                        v.tensor_scalar(wide[:, f % 2, :], proj[f % 2][:], col["b1"][:, f:f + 1], None, ALU.add).then_inc(proj_read[f % 2], 1)

                    def gelu_lo(f):
                        v.wait_ge(g_hi, NF * b + f + 1)
                        v.tensor_tensor(parts[:, 2 * (f % 2) + 1, :], gel[:, f % 2, :], parts[:, 2 * (f % 2), :].bitcast(F32), ALU.subtract).then_inc(g_lo, 1)

                    for f in range(NF):
                        widen(f)
                        gelu_lo(f)
                        if f == 3:
                            number_mask(b + 1)
                        if f == 4:
                            v.wait_ge(x_in, 16 * (b + 2))
                        if 4 <= f < 8:
                            variance(link, xin, f - 4)
                        if f >= 8 and f % 2:
                            adapt(link, b + 1, (f - 8) // 2, ROOTS * b + 2 * TB)
                    v.wait_ge(ff2_done, NF * b + NF + START)
                    v.wait_ge(res_biased, b + 1)
                    for q in range(TB):
                        ins = v.tensor_tensor(tok[:, q, :], ff_sum[q][:], res[:, q, :], ALU.add)
                    ins.then_inc(y_ready, 1)
                    for k in range(KB):
                        turn_lo_part(b, 2 * KB + k, k, turns[k][:])
                    v.wait_ge(proj_full[0], FILLS * b + FILL_L2 + 1 + START)
                    v.tensor_scalar(wide[:, 0, :], proj[0][:], col["down_b"][:, 0:1], None, ALU.add).then_inc(proj_read[0], 1)
                    v.wait_ge(proj_read[0], FILLS * b + FILL_L2 + 1 + START)
                    v.sem_inc(hid_wide, 1)
                    for k in range(2):
                        turn_lo_part(b + 1, k, k, turns[k][:])
                    v.wait_ge(hid_ready, b + 1)
                    v.wait_ge(proj_full[1], FILLS * b + FILL_L2 + 1 + START)
                    v.tensor_scalar(wide[:, 1, :], proj[1][:], cur[:, 0:1], cur[:, 2:3], ALU.mult, ALU.add).then_inc(proj_read[1], 1)
                    v.wait_ge(proj_read[1], FILLS * b + FILL_L2 + 1 + START)
                    v.scalar_tensor_tensor(wide[:, 1, :], gel[:, 0, :], cur[:, 1:2], wide[:, 1, :], ALU.mult, ALU.add).then_inc(mixed, 1)
                    for k in range(2, KB):
                        turn_lo_part(b + 1, k, k, turns[k][:])
                    v.wait_ge(y_biased, b + 1)
                    for q in range(TB):
                        v.wait_ge(proj_full[q % 2], FILLS * b + FILL_UP + q // 2 + 1 + START)
                        v.tensor_tensor(res[:, q, :], proj[q % 2][:], res[:, q, :], ALU.add).then_inc(proj_read[q % 2], 1)
                        v.wait_ge(proj_read[q % 2], FILLS * b + FILL_UP + q // 2 + 1 + START)
                        variance(link, res, q)
                    first_qk(b + 1)
                    v.wait_ge(rstd_ready, ROOTS * (b + 1) + TB)
                    for q in range(TB):
                        link.mark(normalise(res, res, q))
                    link.sync()
                    link(v.tensor_tensor(res[:], res[:], bcast(row["gamma"]), ALU.mult))
                    link(v.tensor_tensor(res[:], res[:], bcast(row["beta"]), ALU.add))
                    quads = res[:].rearrange("p t (q c) -> p (t q) c", c=4)
                    sines = tok[:].rearrange("p t (q c) -> p (t q) c", c=4)
                    for h in range(2):
                        link.mark(v.tensor_scalar(sines[:, :, 2 * h:2 * h + 2], quads[:, :, 2 * h:2 * h + 2], cur[:, 4 + 2 * h:5 + 2 * h], None, ALU.mult))
                    link.sync()
                    for h in range(2):
                        for c in range(2):
                            a, o = 2 * h + c, 2 * h + 1 - c
                            ins = v.scalar_tensor_tensor(quads[:, :, a], quads[:, :, a], cur[:, 3 + 2 * h:4 + 2 * h], sines[:, :, o],
                                                         ALU.mult, ALU.add if c == 0 else ALU.subtract)
                            if a < 3:
                                link.mark(ins)
                    ins.then_inc(out_ready, 1)
                    link.sync()
                    assert link.n == STEPS, link.n


def program(nc, x, dt, step_id, bias, domain, theta, phi, mask, A_grid, B_grid, W_ada, b_ada, Wq, bq, Wk, bk, Wv, bv,
            Wo, bo, W1, b1, W2, b2, g2, beta2, down_W, down_b, up_W, up_b, expert_W, expert_b, emb, gamma, beta,
            freqs, lane, identity, row_slope, row_curve, out):
    x1 = nc.dram_tensor("x1", [B, S, D], F32).ap()
    ada_rows = nc.dram_tensor("ada_rows", [B, 2 * D], F32).ap()
    sel_rows = nc.dram_tensor("sel_rows", [B, A * A], F32).ap()
    sel_turned = nc.dram_tensor("sel_turned", [B, A, A], F32).ap()
    field_step(nc, x, A_grid, B_grid, dt, row_slope, row_curve, x1)
    with ExitStack() as ctx:
        sb = lambda name, shape, t=F32: ctx.enter_context(nc.sbuf_tensor(name, shape, t))
        keep = {"ident": sb("ident", [P, P]), "scal": sb("scal", [P, B, 8]), "up_T": sb("up_T", [A, D]),
                "down_hi": sb("down_hi", [P, KB, A], F32R), "down_lo": sb("down_lo", [P, KB, A], F32R)}
        for name in ("ident_in", "prep_sin", "prep_emb", "prep_ada", "prep_turn"):
            keep[name] = ctx.enter_context(nc.semaphore(name))
        prepare(nc, keep, step_id, domain, theta, phi, W_ada, b_ada, down_W, up_W, expert_W, expert_b, emb,
                freqs, lane, identity, ada_rows, sel_rows, sel_turned)
        layers(nc, keep, x1, mask, bias, ada_rows, sel_turned, Wq, bq, Wk, bk, Wv, bv, Wo, bo, W1, b1, W2, b2, g2, beta2,
               down_b, up_b, gamma, beta, out)


_INS = ["x", "condB_dt", "itok_B_34_63", "fside_Bx16xSxS_0", "itok_B_0_15", "condB_theta", "condB_phi", "mask_Bx1xSxS_bk0",
        "L0_cond_A_grid", "L0_cond_B_grid", "L1_cond_W_ada", "L1_cond_b_ada", "L1_cond_Wq", "L1_cond_bq", "L1_cond_Wk",
        "L1_cond_bk", "L1_cond_Wv", "L1_cond_bv", "L1_cond_Wo", "L1_cond_bo", "L1_cond_W1", "L1_cond_b1", "L1_cond_W2",
        "L1_cond_b2", "L1_cond_g2", "L1_cond_beta2", "L2_cond_down_W", "L2_cond_down_b", "L2_cond_up_W", "L2_cond_up_b",
        "L2_cond_expert_W", "L2_cond_expert_b", "L2_cond_domain_emb", "L2_cond_ln_gamma", "L2_cond_ln_beta"]


def constants():
    half = D // 2
    step = np.float32(-np.log(10000.0) / (half - 1))
    slope, curve = np.zeros((S, S), np.float32), np.zeros((S, S), np.float32)
    for r in range(1, S - 1):
        slope[r, r - 1:r + 2] = -1, 0, 1
        curve[r, r - 1:r + 2] = 1, -2, 1
    slope[0, :3], slope[S - 1, S - 3:] = (-3, 4, -1), (1, -4, 3)
    curve[0, :4], curve[S - 1, S - 4:] = (2, -5, 4, -1), (-1, 4, -5, 2)
    return {"freqs": np.exp(np.arange(half, dtype=np.float32) * step).astype(np.float32),
            "lane": np.arange(P, dtype=np.float32).reshape(P, 1), "identity": np.eye(P, dtype=np.float32),
            "row_slope": np.ascontiguousarray(slope.T), "row_curve": np.ascontiguousarray(curve.T)}


def kernel(**inputs):
    import concourse.bacc as bacc
    from concourse.bass_utils import run_bass_kernel_spmd

    nc = bacc.Bacc("TRN2", target_bir_lowering=False, num_devices=1)
    arrays, args = {}, []
    for name in _INS:
        a = np.ascontiguousarray(inputs[name])
        arrays[f"in_{name}"] = a
    for name, a in constants().items():
        arrays[f"in_{name}"] = a
    for name, a in arrays.items():
        args.append(nc.dram_tensor(name, a.shape, mybir.dt.from_np(a.dtype), kind="ExternalInput").ap())
    args.append(nc.dram_tensor("out", (B, S, D), F32, kind="ExternalOutput").ap())
    program(nc, *args)
    r = run_bass_kernel_spmd(nc, [arrays], core_ids=[0])
    return r.results[0]["out"]
```
